# Optimizing a Trainium2 kernel written in Bass

```python
import numpy as np
import jax
import jax.numpy as jnp

def _softmax(x, axis=-1):
    return jax.nn.softmax(x, axis=axis)

def _gelu(x):
    return jax.nn.gelu(x, approximate=True)

def _silu(x):
    return jax.nn.silu(x)

def _sigmoid(x):
    return jax.nn.sigmoid(x)

def _layernorm(x, axis=-1, eps=1e-05):
    m = jnp.mean(x, axis=axis, keepdims=True)
    v = jnp.var(x, axis=axis, keepdims=True)
    return (x - m) / jnp.sqrt(v + eps)

def _scatter_add(tgt, idx, src, axis=0):
    return tgt.at[idx].add(src)

def _segment_sum(src, seg, n):
    return jax.ops.segment_sum(src, seg, n)
kernel_name = 'mk_gnn_preln_d4_gnn_r32_31c411'

def setup_inputs(seed: int=0):
    np.random.seed(seed)
    _w = jnp.asarray

    def _rec_inputs():
        import jax
        import jax.numpy as jnp
        _gk = jax.random.key(seed)
        x = -0.0002928 + 1 * jax.random.normal(jax.random.fold_in(_gk, 1), (256, 512), jnp.float32)
        src = jax.random.randint(jax.random.fold_in(_gk, 2), (8192,), 0, 256, jnp.int32)
        dst = jax.random.randint(jax.random.fold_in(_gk, 3), (8192,), 0, 256, jnp.int32)
        _o = jnp.argsort(dst, stable=True)
        src = src[_o]
        dst = dst[_o]
        edge_attr_20 = jax.random.uniform(jax.random.fold_in(_gk, 12), (8192, 20), jnp.float32, 0.0, 0.999999)
        edge_attr_3 = -0.0005747 + 0.998114 * jax.random.normal(jax.random.fold_in(_gk, 13), (8192, 3), jnp.float32)
        edge_attr_64 = 0.000279952 + 1.00013 * jax.random.normal(jax.random.fold_in(_gk, 14), (8192, 64), jnp.float32)
        edge_type_8 = jax.random.randint(jax.random.fold_in(_gk, 16), (8192,), 0, 8, jnp.int32)
        edge_weight = jax.random.uniform(jax.random.fold_in(_gk, 17), (8192,), jnp.float32, 0.0, 0.999999)
        return (x, src, dst, edge_attr_20, edge_attr_3, edge_attr_64, edge_type_8, edge_weight)
    x, src, dst, edge_attr_20, edge_attr_3, edge_attr_64, edge_type_8, edge_weight = _rec_inputs()

    def _L0_gnn_setup():
        import jax, jax.numpy as jnp
        import numpy as np
        NUM_NODES = 256
        NUM_EDGES = 8192
        IN_C = 512
        OUT_C = 512
        key = jax.random.key(seed)
        k1, k2, k3, k4 = jax.random.split(key, 4)
        x = jax.random.normal(k1, (NUM_NODES, IN_C), dtype=jnp.float32)
        edge_index = jax.random.randint(k2, (2, NUM_EDGES), 0, NUM_NODES, dtype=jnp.int64)
        W = jax.random.normal(k3, (OUT_C, IN_C), dtype=jnp.float32) * (1.0 / np.sqrt(IN_C))
        b = jax.random.normal(k4, (OUT_C,), dtype=jnp.float32) * 0.01
        return {'x': x, 'edge_index': edge_index, 'W': W, 'b': b}
    _L0_gnn_all = _L0_gnn_setup()
    _L0_gnn_in = {k: v for k, v in _L0_gnn_all.items() if k in ('W', 'b')}
    del _L0_gnn_all

    def _L1_gnn_setup():
        import jax, jax.numpy as jnp
        import numpy as np
        N, IN_DIM, H, D, E = (50000, 512, 8, 64, 25000)
        NEG_SLOPE = 0.2
        LN_EPS = 1e-05
        key = jax.random.key(seed)
        ks = jax.random.split(key, 8)
        x = jax.random.normal(ks[0], (N, IN_DIM), dtype=jnp.float32)
        edge_index = jax.random.randint(ks[1], (2, E), 0, N, dtype=jnp.int64)
        edge_type = jax.random.randint(ks[2], (E,), 0, 8, dtype=jnp.int64)
        edge_weight = jax.random.uniform(ks[3], (E,), dtype=jnp.float32)
        W = jax.random.normal(ks[4], (H * D, IN_DIM), dtype=jnp.float32) * (1.0 / np.sqrt(IN_DIM))
        a_src = jax.random.normal(ks[5], (H, D), dtype=jnp.float32) * (1.0 / np.sqrt(D))
        a_dst = jax.random.normal(ks[6], (H, D), dtype=jnp.float32) * (1.0 / np.sqrt(D))
        et_emb = jax.random.normal(ks[7], (8, H), dtype=jnp.float32)
        ln_gamma = jnp.ones((H * D,), dtype=jnp.float32)
        ln_beta = jnp.zeros((H * D,), dtype=jnp.float32)
        return {'x': x, 'edge_index': edge_index, 'edge_type': edge_type, 'edge_weight': edge_weight, 'W': W, 'a_src': a_src, 'a_dst': a_dst, 'et_emb': et_emb, 'ln_gamma': ln_gamma, 'ln_beta': ln_beta}
    _L1_gnn_all = _L1_gnn_setup()
    _L1_gnn_in = {k: v for k, v in _L1_gnn_all.items() if k in ('W', 'a_src', 'a_dst', 'et_emb', 'ln_gamma', 'ln_beta')}
    del _L1_gnn_all

    def _L2_gnn_setup():
        import jax, jax.numpy as jnp
        import numpy as np
        N_ATOMS = 5000
        N_EDGES = 50000
        C = 128
        F = 128
        N_RBF = 20
        LOG2 = float(np.log(2.0))
        Y0 = float(1.0 / np.sqrt(4.0 * np.pi))
        Y1_SCALE = float(np.sqrt(3.0 / (4.0 * np.pi)))

        def shifted_softplus(x):
            return jax.nn.softplus(x) - LOG2

        def _forward(x, idx_i, idx_j, f_ij, rcut_ij, r_ij, W_in2f_s, W_in2f_v, Wf1, bf1, Wf2, bf2, W1_s, W1_v, W2_s, W2_v):
            n = x.shape[0]
            e = r_ij.shape[0]
            xs = x[:, :C] @ (W_in2f_s / np.sqrt(C))
            xv = jnp.einsum('nci,cf->nfi', x[:, C:].reshape(n, C, 3), W_in2f_v) / np.sqrt(C)
            sj = xs[idx_j]
            vj = xv[idx_j]
            u = r_ij / jnp.linalg.norm(r_ij, axis=-1, keepdims=True)
            Yv = Y1_SCALE * u
            o0a = sj * Y0
            o0b = jnp.einsum('efi,ei->ef', vj, Yv) / np.sqrt(3.0)
            s2 = jnp.stack([o0a, o0b], axis=-1).reshape(e, 2 * F)
            ova = sj[:, :, None] * Yv[:, None, :]
            ovb = vj * Y0
            v2 = jnp.stack([ova, ovb], axis=2)
            w1 = jnp.cross(vj, Yv[:, None, :]) / np.sqrt(2.0)
            ax, ay, az = (vj[..., 0], vj[..., 1], vj[..., 2])
            bx, by, bz = (Yv[:, None, 0], Yv[:, None, 1], Yv[:, None, 2])
            t = jnp.stack([(ax * by + ay * bx) / np.sqrt(2.0), (ay * bz + az * by) / np.sqrt(2.0), (2.0 * az * bz - ax * bx - ay * by) / np.sqrt(6.0), (az * bx + ax * bz) / np.sqrt(2.0), (ax * bx - ay * by) / np.sqrt(2.0)], axis=-1)
            h = shifted_softplus(f_ij @ Wf1 + bf1)
            W = (h @ Wf2 + bf2) * rcut_ij[:, None]
            m_s = s2 * W[:, :2 * F]
            m_v = (v2.reshape(e, 2 * F, 3) * W[:, 2 * F:4 * F, None]).reshape(e, 6 * F)
            m_w = (w1 * W[:, 4 * F:5 * F, None]).reshape(e, 3 * F)
            m_t = (t * W[:, 5 * F:6 * F, None]).reshape(e, 5 * F)
            x_ij = jnp.concatenate([m_s, m_v, m_w, m_t], axis=1)
            agg = jax.ops.segment_sum(x_ij, idx_i, num_segments=n)
            S = agg[:, :2 * F] @ (W1_s / np.sqrt(2 * F))
            V = jnp.einsum('nmi,mc->nci', agg[:, 2 * F:8 * F].reshape(n, 2 * F, 3), W1_v) / np.sqrt(2 * F)
            S = shifted_softplus(S)
            S = S @ (W2_s / np.sqrt(C))
            V = jnp.einsum('nci,cd->ndi', V, W2_v) / np.sqrt(C)
            return jnp.concatenate([S, V.reshape(n, 3 * C)], axis=1)
        key = jax.random.key(seed)
        ks = jax.random.split(key, 16)
        f32 = jnp.float32
        x = jax.random.normal(ks[0], (N_ATOMS, 4 * C), f32)
        idx_i = jnp.sort(jax.random.randint(ks[1], (N_EDGES,), 0, N_ATOMS))
        idx_j = jax.random.randint(ks[2], (N_EDGES,), 0, N_ATOMS)
        f_ij = jax.random.uniform(ks[3], (N_EDGES, N_RBF), f32)
        rcut_ij = jax.random.uniform(ks[4], (N_EDGES,), f32)
        r_ij = jax.random.normal(ks[5], (N_EDGES, 3), f32)
        W_in2f_s = jax.random.normal(ks[6], (C, F), f32)
        W_in2f_v = jax.random.normal(ks[7], (C, F), f32)
        Wf1 = jax.random.normal(ks[8], (N_RBF, F), f32) / np.sqrt(N_RBF)
        bf1 = 0.1 * jax.random.normal(ks[9], (F,), f32)
        Wf2 = jax.random.normal(ks[10], (F, 6 * F), f32) / np.sqrt(F)
        bf2 = 0.1 * jax.random.normal(ks[11], (6 * F,), f32)
        W1_s = jax.random.normal(ks[12], (2 * F, C), f32)
        W1_v = jax.random.normal(ks[13], (2 * F, C), f32)
        W2_s = jax.random.normal(ks[14], (C, C), f32)
        W2_v = jax.random.normal(ks[15], (C, C), f32)
        return dict(x=x, idx_i=idx_i, idx_j=idx_j, f_ij=f_ij, rcut_ij=rcut_ij, r_ij=r_ij, W_in2f_s=W_in2f_s, W_in2f_v=W_in2f_v, Wf1=Wf1, bf1=bf1, Wf2=Wf2, bf2=bf2, W1_s=W1_s, W1_v=W1_v, W2_s=W2_s, W2_v=W2_v)
    _L2_gnn_all = _L2_gnn_setup()
    _L2_gnn_in = {k: v for k, v in _L2_gnn_all.items() if k in ('W_in2f_s', 'W_in2f_v', 'Wf1', 'bf1', 'Wf2', 'bf2', 'W1_s', 'W1_v', 'W2_s', 'W2_v')}
    del _L2_gnn_all

    def _L3_gnn_setup():
        import jax, jax.numpy as jnp
        import numpy as np
        N_NODES = 625
        N_EDGES = 10000
        HIDDEN = 512
        EDGE_DIM = 64
        LN_EPS = 1e-05

        def mish(x):
            return x * jnp.tanh(jax.nn.softplus(x))
        key = jax.random.key(seed)
        ks = jax.random.split(key, 8)
        s = lambda fan_in: 1.0 / np.sqrt(fan_in)
        return {'x': jax.random.normal(ks[0], (N_NODES, HIDDEN), dtype=jnp.float32), 'edge_index': jax.random.randint(ks[1], (2, N_EDGES), 0, N_NODES, dtype=jnp.int64), 'edge_attr': jax.random.normal(ks[2], (N_EDGES, EDGE_DIM), dtype=jnp.float32), 'W1': jax.random.normal(ks[3], (2 * HIDDEN + EDGE_DIM, HIDDEN), dtype=jnp.float32) * s(2 * HIDDEN + EDGE_DIM), 'b1': jnp.zeros((HIDDEN,), dtype=jnp.float32), 'W2': jax.random.normal(ks[4], (HIDDEN, HIDDEN), dtype=jnp.float32) * s(HIDDEN), 'b2': jnp.zeros((HIDDEN,), dtype=jnp.float32), 'W3': jax.random.normal(ks[5], (2 * HIDDEN, HIDDEN), dtype=jnp.float32) * s(2 * HIDDEN), 'b3': jnp.zeros((HIDDEN,), dtype=jnp.float32), 'W4': jax.random.normal(ks[6], (HIDDEN, HIDDEN), dtype=jnp.float32) * s(HIDDEN), 'b4': jnp.zeros((HIDDEN,), dtype=jnp.float32), 'gamma': jnp.ones((HIDDEN,), dtype=jnp.float32), 'beta': jnp.zeros((HIDDEN,), dtype=jnp.float32)}
    _L3_gnn_all = _L3_gnn_setup()
    _L3_gnn_in = {k: v for k, v in _L3_gnn_all.items() if k in ('W1', 'b1', 'W2', 'b2', 'W3', 'b3', 'W4', 'b4', 'gamma', 'beta')}
    del _L3_gnn_all
    return {'x': x, 'src': src, 'dst': dst, 'edge_attr_20': edge_attr_20, 'edge_attr_3': edge_attr_3, 'edge_attr_64': edge_attr_64, 'edge_type_8': edge_type_8, 'edge_weight': edge_weight, 'L0_gnn_W': _L0_gnn_in['W'], 'L0_gnn_b': _L0_gnn_in['b'], 'L1_gnn_W': _L1_gnn_in['W'], 'L1_gnn_a_src': _L1_gnn_in['a_src'], 'L1_gnn_a_dst': _L1_gnn_in['a_dst'], 'L1_gnn_et_emb': _L1_gnn_in['et_emb'], 'L1_gnn_ln_gamma': _L1_gnn_in['ln_gamma'], 'L1_gnn_ln_beta': _L1_gnn_in['ln_beta'], 'L2_gnn_W_in2f_s': _L2_gnn_in['W_in2f_s'], 'L2_gnn_W_in2f_v': _L2_gnn_in['W_in2f_v'], 'L2_gnn_Wf1': _L2_gnn_in['Wf1'], 'L2_gnn_bf1': _L2_gnn_in['bf1'], 'L2_gnn_Wf2': _L2_gnn_in['Wf2'], 'L2_gnn_bf2': _L2_gnn_in['bf2'], 'L2_gnn_W1_s': _L2_gnn_in['W1_s'], 'L2_gnn_W1_v': _L2_gnn_in['W1_v'], 'L2_gnn_W2_s': _L2_gnn_in['W2_s'], 'L2_gnn_W2_v': _L2_gnn_in['W2_v'], 'L3_gnn_W1': _L3_gnn_in['W1'], 'L3_gnn_b1': _L3_gnn_in['b1'], 'L3_gnn_W2': _L3_gnn_in['W2'], 'L3_gnn_b2': _L3_gnn_in['b2'], 'L3_gnn_W3': _L3_gnn_in['W3'], 'L3_gnn_b3': _L3_gnn_in['b3'], 'L3_gnn_W4': _L3_gnn_in['W4'], 'L3_gnn_b4': _L3_gnn_in['b4'], 'L3_gnn_gamma': _L3_gnn_in['gamma'], 'L3_gnn_beta': _L3_gnn_in['beta']}

def reference(x, src, dst, edge_attr_20, edge_attr_3, edge_attr_64, edge_type_8, edge_weight, L0_gnn_W, L0_gnn_b, L1_gnn_W, L1_gnn_a_src, L1_gnn_a_dst, L1_gnn_et_emb, L1_gnn_ln_gamma, L1_gnn_ln_beta, L2_gnn_W_in2f_s, L2_gnn_W_in2f_v, L2_gnn_Wf1, L2_gnn_bf1, L2_gnn_Wf2, L2_gnn_bf2, L2_gnn_W1_s, L2_gnn_W1_v, L2_gnn_W2_s, L2_gnn_W2_v, L3_gnn_W1, L3_gnn_b1, L3_gnn_W2, L3_gnn_b2, L3_gnn_W3, L3_gnn_b3, L3_gnn_W4, L3_gnn_b4, L3_gnn_gamma, L3_gnn_beta):
    import jax
    import jax.numpy as jnp

    def _L0_gnn_ref(x, edge_index, W, b):
        import jax, jax.numpy as jnp
        import numpy as np
        NUM_NODES = 256
        NUM_EDGES = 8192
        IN_C = 512
        OUT_C = 512
        n = x.shape[0]
        loop = jnp.arange(n, dtype=edge_index.dtype)
        rows = jnp.concatenate([edge_index[0], loop])
        cols = jnp.concatenate([edge_index[1], loop])
        adj = jnp.zeros((n, n), dtype=jnp.float32).at[rows, cols].set(1.0)
        deg = adj.sum(axis=1)
        deg_inv_sqrt = jnp.where(deg > 0, jax.lax.rsqrt(jnp.maximum(deg, 1e-30)), 0.0)
        norm = deg_inv_sqrt[:, None] * adj * deg_inv_sqrt[None, :]
        h = x @ W.T + b
        return norm @ h

    def _L1_gnn_ref(x, edge_index, edge_type, edge_weight, W, a_src, a_dst, et_emb, ln_gamma, ln_beta):
        import jax, jax.numpy as jnp
        import numpy as np
        N, IN_DIM, H, D, E = (50000, 512, 8, 64, 25000)
        NEG_SLOPE = 0.2
        LN_EPS = 1e-05
        n, h_, d_ = (x.shape[0], a_src.shape[0], a_src.shape[1])
        h = (x @ W.T).reshape(n, h_, d_)
        src, dst = (edge_index[0], edge_index[1])
        h_src = h[src]
        e_src = jnp.einsum('ehd,hd->eh', h_src, a_src)
        e_dst = jnp.einsum('ehd,hd->eh', h[dst], a_dst)
        e = jax.nn.leaky_relu(e_src + e_dst, NEG_SLOPE)
        e = e * (1.0 + et_emb[edge_type])
        e = e * edge_weight[:, None]
        e_max = jnp.zeros((n, h_), x.dtype).at[dst].max(e)
        e = jnp.exp(e - e_max[dst])
        e_sum = jnp.zeros((n, h_), x.dtype).at[dst].add(e)
        alpha = e / (e_sum[dst] + 1e-10)
        msg = h_src * alpha[:, :, None]
        out = jnp.zeros((n, h_, d_), x.dtype).at[dst].add(msg).reshape(n, h_ * d_)
        out = out + x
        mu = jnp.mean(out, axis=-1, keepdims=True)
        var = jnp.var(out, axis=-1, keepdims=True)
        return (out - mu) / jnp.sqrt(var + LN_EPS) * ln_gamma + ln_beta

    def _L2_gnn_ref(x, idx_i, idx_j, f_ij, rcut_ij, r_ij, W_in2f_s, W_in2f_v, Wf1, bf1, Wf2, bf2, W1_s, W1_v, W2_s, W2_v):
        import jax, jax.numpy as jnp
        import numpy as np
        N_ATOMS = 5000
        N_EDGES = 50000
        C = 128
        F = 128
        N_RBF = 20
        LOG2 = float(np.log(2.0))
        Y0 = float(1.0 / np.sqrt(4.0 * np.pi))
        Y1_SCALE = float(np.sqrt(3.0 / (4.0 * np.pi)))

        def shifted_softplus(x):
            return jax.nn.softplus(x) - LOG2

        def _forward(x, idx_i, idx_j, f_ij, rcut_ij, r_ij, W_in2f_s, W_in2f_v, Wf1, bf1, Wf2, bf2, W1_s, W1_v, W2_s, W2_v):
            n = x.shape[0]
            e = r_ij.shape[0]
            xs = x[:, :C] @ (W_in2f_s / np.sqrt(C))
            xv = jnp.einsum('nci,cf->nfi', x[:, C:].reshape(n, C, 3), W_in2f_v) / np.sqrt(C)
            sj = xs[idx_j]
            vj = xv[idx_j]
            u = r_ij / jnp.linalg.norm(r_ij, axis=-1, keepdims=True)
            Yv = Y1_SCALE * u
            o0a = sj * Y0
            o0b = jnp.einsum('efi,ei->ef', vj, Yv) / np.sqrt(3.0)
            s2 = jnp.stack([o0a, o0b], axis=-1).reshape(e, 2 * F)
            ova = sj[:, :, None] * Yv[:, None, :]
            ovb = vj * Y0
            v2 = jnp.stack([ova, ovb], axis=2)
            w1 = jnp.cross(vj, Yv[:, None, :]) / np.sqrt(2.0)
            ax, ay, az = (vj[..., 0], vj[..., 1], vj[..., 2])
            bx, by, bz = (Yv[:, None, 0], Yv[:, None, 1], Yv[:, None, 2])
            t = jnp.stack([(ax * by + ay * bx) / np.sqrt(2.0), (ay * bz + az * by) / np.sqrt(2.0), (2.0 * az * bz - ax * bx - ay * by) / np.sqrt(6.0), (az * bx + ax * bz) / np.sqrt(2.0), (ax * bx - ay * by) / np.sqrt(2.0)], axis=-1)
            h = shifted_softplus(f_ij @ Wf1 + bf1)
            W = (h @ Wf2 + bf2) * rcut_ij[:, None]
            m_s = s2 * W[:, :2 * F]
            m_v = (v2.reshape(e, 2 * F, 3) * W[:, 2 * F:4 * F, None]).reshape(e, 6 * F)
            m_w = (w1 * W[:, 4 * F:5 * F, None]).reshape(e, 3 * F)
            m_t = (t * W[:, 5 * F:6 * F, None]).reshape(e, 5 * F)
            x_ij = jnp.concatenate([m_s, m_v, m_w, m_t], axis=1)
            agg = jax.ops.segment_sum(x_ij, idx_i, num_segments=n)
            S = agg[:, :2 * F] @ (W1_s / np.sqrt(2 * F))
            V = jnp.einsum('nmi,mc->nci', agg[:, 2 * F:8 * F].reshape(n, 2 * F, 3), W1_v) / np.sqrt(2 * F)
            S = shifted_softplus(S)
            S = S @ (W2_s / np.sqrt(C))
            V = jnp.einsum('nci,cd->ndi', V, W2_v) / np.sqrt(C)
            return jnp.concatenate([S, V.reshape(n, 3 * C)], axis=1)
        return _forward(x, idx_i, idx_j, f_ij, rcut_ij, r_ij, W_in2f_s, W_in2f_v, Wf1, bf1, Wf2, bf2, W1_s, W1_v, W2_s, W2_v)

    def _L3_gnn_ref(x, edge_index, edge_attr, W1, b1, W2, b2, W3, b3, W4, b4, gamma, beta):
        import jax, jax.numpy as jnp
        import numpy as np
        N_NODES = 625
        N_EDGES = 10000
        HIDDEN = 512
        EDGE_DIM = 64
        LN_EPS = 1e-05

        def mish(x):
            return x * jnp.tanh(jax.nn.softplus(x))
        src, dst = (edge_index[0], edge_index[1])
        edge_feat = jnp.concatenate([x[src], x[dst], edge_attr], axis=-1)
        h = mish(edge_feat @ W1 + b1)
        messages = mish(h @ W2 + b2)
        agg = jax.ops.segment_sum(messages, dst, num_segments=x.shape[0])
        u = mish(jnp.concatenate([x, agg], axis=-1) @ W3 + b3)
        out = u @ W4 + b4
        y = x + out
        mu = jnp.mean(y, axis=-1, keepdims=True)
        var = jnp.mean(jnp.square(y - mu), axis=-1, keepdims=True)
        return (y - mu) * jax.lax.rsqrt(var + LN_EPS) * gamma + beta
    edge_index = jnp.stack([src, dst])
    h = jnp.maximum(_layernorm(x, axis=-1), 0.0)
    x = x + _L0_gnn_ref(h, edge_index, L0_gnn_W, L0_gnn_b)
    h = jnp.maximum(_layernorm(x, axis=-1), 0.0)
    x = x + _L1_gnn_ref(h, edge_index, edge_type_8, edge_weight, L1_gnn_W, L1_gnn_a_src, L1_gnn_a_dst, L1_gnn_et_emb, L1_gnn_ln_gamma, L1_gnn_ln_beta)
    h = jnp.maximum(_layernorm(x, axis=-1), 0.0)
    x = x + _L2_gnn_ref(h, src, dst, edge_attr_20, edge_weight, edge_attr_3, L2_gnn_W_in2f_s, L2_gnn_W_in2f_v, L2_gnn_Wf1, L2_gnn_bf1, L2_gnn_Wf2, L2_gnn_bf2, L2_gnn_W1_s, L2_gnn_W1_v, L2_gnn_W2_s, L2_gnn_W2_v)
    h = jnp.maximum(_layernorm(x, axis=-1), 0.0)
    x = x + _L3_gnn_ref(h, edge_index, edge_attr_64, L3_gnn_W1, L3_gnn_b1, L3_gnn_W2, L3_gnn_b2, L3_gnn_W3, L3_gnn_b3, L3_gnn_W4, L3_gnn_b4, L3_gnn_gamma, L3_gnn_beta)
    return x

_drawn_inputs = setup_inputs


def setup_inputs(seed=0):
    import zlib

    import numpy as np

    out = dict(_drawn_inputs(seed))
    spreads = {'L1_gnn_ln_gamma': (1.0, 0.2),
     'L1_gnn_ln_beta': (0.0, 0.1),
     'L3_gnn_b1': (0.0, 0.1),
     'L3_gnn_b2': (0.0, 0.1),
     'L3_gnn_b3': (0.0, 0.8),
     'L3_gnn_b4': (0.0, 0.8),
     'L3_gnn_gamma': (1.0, 0.2),
     'L3_gnn_beta': (0.0, 0.1)}
    factors = {'L0_gnn_b': 5.983}
    for name, (base, spread) in spreads.items():
        noise = np.random.default_rng([zlib.crc32(name.encode()), seed]).standard_normal(out[name].shape)
        drawn = base * np.exp(spread * noise) if base else spread * noise
        out[name] = jnp.asarray(drawn.astype(out[name].dtype))
    for name, factor in factors.items():
        out[name] = (out[name] * factor).astype(out[name].dtype)
    return out
```

```python
from contextlib import ExitStack

import numpy as np

import concourse.bass as bass
from concourse import mybir

F32 = mybir.dt.float32
F32R = mybir.dt.float32r
BF16 = mybir.dt.bfloat16
I32 = mybir.dt.int32
U8 = mybir.dt.uint8
ALU = mybir.AluOpType
ACT = mybir.ActivationFunctionType
AX = mybir.AxisListType.X

P = 128
N = 256
NH = N // P
E = 8192
C = 512
KC = C // P
T = E // P
G = 4
GE = G * P
NG = T // G
HD = 8
F = 128
RBF = 20
ED = 64
LN_EPS = 1e-5
LOG2 = float(np.log(2.0))
Y0 = float(1.0 / np.sqrt(4.0 * np.pi))
Y1 = float(np.sqrt(3.0 / (4.0 * np.pi)))
BANK = 512
CLAMP = 2.0 ** 30


def gnn_stack(nc, d, out, layers=4):
    with ExitStack() as ctx:
        sems = {}

        def sem(name):
            if name not in sems:
                sems[name] = ctx.enter_context(nc.semaphore(name))
            return sems[name]

        def sb(name, shape, dt=F32):
            return ctx.enter_context(nc.sbuf_tensor(name, shape, dt))

        PS = ctx.enter_context(nc.psum_tensor("PS", [P, 8 * BANK], F32))

        def bank(k, n=1):
            return PS[:, k * BANK:(k + n) * BANK]

        node_row = sb("node_row", [P, N])
        node_col = sb("node_col", [P, NH])
        ident = sb("ident", [P, P])
        src_row = sb("src_row", [P, E], U8)
        dst_row = sb("dst_row", [P, E], U8)
        src_col = sb("src_col", [P, T])
        dst_col = sb("dst_col", [P, T])
        idx_raw = sb("idx_raw", [P, 2, T], I32)
        ew = sb("ew", [P, T])
        X = sb("X", [P, NH, C])
        Hn = sb("Hn", [P, NH, C])
        WN = sb("WN", [P, KC, C])
        LW = sb("LW", [P, 8, C])
        V = sb("V", [P, 4, C])
        U = sb("U", [P, 3584])
        stats = sb("stats", [P, NH, 6])
        mv = sb("mv", [P, NH, 2])
        one_col = sb("one_col", [P, 1])
        nt = sb("nt", [P, 2, NH, HD])
        rs = sb("rs", [P, 4, NH])
        ST = sb("ST", [P, 2, NH, GE], F32R)
        DT = sb("DT", [P, 2, NH, GE], F32R)
        EN = sb("EN", [P, 2, G, N], F32R)
        TAB = sb("TAB", [P, 2, 2, NH, C], F32R)
        MSG = sb("MSG", [P, 2, 2, 1024], F32R)
        HT = sb("HT", [P, 2, 2, KC, GE], F32R)
        WF2 = sb("WF2", [P, 2, C], F32R)
        BF2 = sb("BF2", [64, C], F32R)
        W2S = sb("W2S", [P, 2, KC, C], F32R)
        B2S = sb("B2S", [64, C], F32R)
        WEA = sb("WEA", [P, 2, C], F32R)
        EA = sb("EA", [P, 2, GE], F32R)
        EB = sb("EB", [P, 2, GE], F32R)
        ones = sb("ones", [64, P], F32R)
        L = sb("L", [P, T, HD])
        NT = sb("NT", [P, 2, 2, NH, HD], F32R)
        MX = sb("MX", [P, 2, NH, HD], F32R)
        MXf = sb("MXf", [P, NH, HD])
        EMB = sb("EMB", [HD, 2, HD], F32R)
        emb = sb("emb", [HD, HD])
        T8 = HT[0:HD, 0, 0, 0:2]
        Pz = sb("Pz", [P, 2, G * HD])
        Pe = sb("Pe", [P, 2, G * HD])
        Ps = sb("Ps", [P, 2, 2, G * HD], F32R)
        Yv = sb("Yv", [P, T, 3])
        fT = LW[0:RBF, 2:4]
        Wf1 = sb("Wf1", [RBF, F])
        bf1 = sb("bf1", [P, 1])
        Win = sb("Win", [P, 2, F])
        W1sv = sb("W1sv", [P, 2, 2, F])
        W2sv = sb("W2sv", [P, 2, F])
        ea_raw = L[:].rearrange("p a b -> p (a b)")

        block = ctx.enter_context(nc.Block())

        def u(off, *shape):
            n = int(np.prod(shape))
            a = U[:, off:off + n]
            if len(shape) == 2:
                a = a.rearrange("p (a b) -> p a b", a=shape[0])
            if len(shape) == 3:
                a = a.rearrange("p (a b c) -> p a b c", a=shape[0], b=shape[1])
            return a

        f = lambda ap: ap.bitcast(F32)

        l0_on = U[:, 0:512].bitcast(BF16).rearrange("p (s w n) -> p s w n", s=2, w=2)
        adjT = u(512, NH, N)
        dis = u(1024, NH)
        hW = u(1032, NH, C)
        hT = u(2056, KC, N)
        l1_t = u(2056, NH, C)
        l1_em = u(0, T, HD)
        typ = u(512, 2, GE)[0:HD].bitcast(I32)
        R = u(0, HD, N)
        l1_m = u(0, 2, C)
        l2_m = u(0, 2, 9, F)
        l2_w = u(2304, 2, 4, F)
        l2_s = [WN[:, k, :] for k in range(4)]
        UA = [u(0, 2, C), u(1024, 2, C)]
        UB = u(2048, 2, C)
        l2_tab = [u(0, NH, C)[:, h] for h in range(NH)]
        l2_agg = u(0, NH, 8, F)
        aggT = WN[:].rearrange("p a b -> p (a b)").rearrange("p (a b) -> p a b", a=8)
        SV = u(2048, 4, N)
        s2 = u(3072, 2, N)
        agg3 = u(0, NH, C)
        h3T = u(1024, KC, N)
        r_y, r_v, r_sq = u(3090, T), u(3090 + T, T), u(3090 + 2 * T, T, 3)

        RSQRT = ("n0", "r2", "deg", "n1", "n1o", "n2", "n3", "n3o")
        NORMS = ("n0", "n1", "n2", "n3")
        TURNS = ("n0", "n1", "n2", "n3", "n3b", "n3a", "n3u")

        class Chain:

            def __init__(self, eng, name):
                self.eng, self.sem, self.n = eng, sem(name), 0

            def __call__(self, ins):
                self.n += 1
                ins.then_inc(self.sem, 1)
                self.eng.wait_ge(self.sem, self.n)

        def load(eng, dst, src, name):
            eng.dma_start(dst, src).then_inc(sem("in_" + name), 16)

        def row(ap):
            return ap.partition_broadcast(P)

        @block.sync
        def _(sp):
            load(sp, X[:], d["x"], "x")
            load(sp, idx_raw[:], d["idx_cols"], "idx")
            load(sp, WN[:], d["L0_WT"], "L0_W")
            load(sp, V[:, 0], row(d["L0_b"]), "L0_b")
            load(sp, ew[:], d["ew"], "ew")
            if layers > 2:
                load(sp, Yv[:], d["ea3"], "ea3")
            if layers > 1:
                load(sp, V[:, 1], row(d["a_src"]), "l1_vectors")
            if layers > 1:
                load(sp, V[:, 2], row(d["a_dst"]), "l1_vectors")
            if layers > 1:
                load(sp, emb[:], d["emb"], "l1_vectors")
            if layers > 2:
                load(sp, Win[:], d["Win"], "l2_weights")
            if layers > 2:
                load(sp, Wf1[:], d["Wf1"], "l2_weights")
            if layers > 2:
                load(sp, bf1[:], d["bf1"], "l2_weights")
            if layers > 2:
                load(sp, W1sv[:], d["W1sv"], "l2_weights")
            if layers > 2:
                load(sp, W2sv[:], d["W2sv"], "l2_weights")
            for k in range(4):
                if k:
                    sp.wait_ge(sem("rows_cast"), k)
                load(sp, LW[:].rearrange("p a b -> p (a b)").bitcast(I32),
                     row(d["idx_rows"][k // 2, (k % 2) * (E // 2):(k % 2 + 1) * (E // 2)]), "rows")
            sp.wait_ge(sem("l0_hW_ps"), 1)
            if layers > 1:
                load(sp, WN[:], d["L1_WT"], "L1_W")
            if layers > 1:
                sp.wait_ge(sem("x_done"), 1)
                def types(i, b, wait):
                    g = i * 2 + b
                    if wait:
                        sp.wait_ge(sem("l1a_onehots"), g - 1)
                    sp.dma_start(typ[:, b], d["type_rows"][:, bass.ds(g * GE, GE)]).then_inc(sem(f"in_type{b}"), 16)
                types(0, 0, False)
                types(0, 1, False)
                with sp.Fori(1, NG // 2) as i:
                    types(i, 0, True)
                    types(i, 1, True)
                sp.wait_ge(sem("l1_esd"), 1)
                load(sp, V[:, 1], row(d["L1_gamma"]), "l1_affine")
                load(sp, V[:, 2], row(d["L1_beta"]), "l1_affine")
            if layers > 2:
                sp.wait_ge(sem("rows_cast"), 4)
                load(sp, LW[:, 0], d["Wf2"][:, 0:4 * F], "l2_filter")
                load(sp, LW[0:1, 1], d["bf2"][:, 0:4 * F], "l2_filter")
                load(sp, LW[32:33, 1], d["bf2"][:, 0:4 * F], "l2_filter")

                def rbf(i, b, wait):
                    g = i * 2 + b
                    if wait:
                        sp.wait_ge(sem("l2_h_ps"), g - 1)
                    sp.dma_start(fT[:, b], d["ea20T"][:, bass.ds(g * GE, GE)]).then_inc(sem(f"in_rbf{b}"), 16)
                rbf(0, 0, False)
                rbf(0, 1, False)
                with sp.Fori(1, NG // 2) as i:
                    rbf(i, 0, True)
                    rbf(i, 1, True)
            if layers > 3:
                sp.wait_ge(sem("l2_wsplit"), 1)
                sp.wait_ge(sem("l2_h_ps"), NG)
                load(sp, LW[:], d["L3_W1ab"], "L3_W1ab")
                sp.wait_ge(sem("l1_out"), 1)
                load(sp, V[:, 0], row(d["L3_b3"]), "l3_vectors")
                load(sp, V[:, 1], row(d["L3_b4"]), "l3_vectors")
                load(sp, V[:, 2], row(d["L3_gamma"]), "l3_vectors")
                load(sp, V[:, 3], row(d["L3_beta"]), "l3_vectors")
                sp.wait_ge(sem("l2_out"), 1)
                load(sp, WN[:], d["L3_W2"], "L3_W2")
                for r in range(2):
                    load(sp, u(0, 3, C)[64 * r:64 * r + 64, 0], d["W1c"], "l3_edge_weights")
                for r in (64, 96):
                    load(sp, u(0, 3, C)[r:r + 1, 1], d["L3_b1"], "l3_edge_weights")
                for r in (0, 32):
                    load(sp, u(0, 3, C)[r:r + 1, 2], d["L3_b2"], "l3_edge_weights")

                def feats(g, wait):
                    if wait:
                        sp.wait_ge(sem("l3_ea"), g)
                    for r in range(2):
                        sp.dma_start(ea_raw[64 * r:64 * r + 64, :],
                                     d["ea64T"][:, bass.ds(g * GE, GE)]).then_inc(sem("in_ea"), 16)
                feats(0, False)
                with sp.Fori(1, NG) as g:
                    feats(g, True)
                sp.wait_ge(sem("l3_w2split"), 1)
                load(sp, WN[:], d["L3_W4"], "L3_W4")
                sp.wait_ge(sem("l3_tab_ps"), 2)
                load(sp, LW[:], d["L3_W3"], "L3_W3")
            sp.wait_ge(sem("x_done"), layers)
            sp.dma_start(out, X[:]).then_inc(sem("out"), 16)
            sp.wait_ge(sem("out"), 16)

        @block.gpsimd
        def _(pool):
            pool.iota(node_row[:], [[1, N]], base=0, channel_multiplier=0,
                      allow_small_or_imprecise_dtypes=True).then_inc(sem("iotas"), 1)
            pool.iota(node_col[:], [[P, NH]], base=0, channel_multiplier=1,
                      allow_small_or_imprecise_dtypes=True).then_inc(sem("iotas"), 1)

        @block.scalar
        def _(act):
            chain = Chain(act, "act_chain")
            act.preload_act_table_set("natural_log_exp_and_others")

            def rsqrt_guess(tag, v, y):
                act.wait_ge(sem("rsqrt_v"), RSQRT.index(tag) + 1)
                chain(act.activation(y, v, ACT.Ln))
                act.activation(y, y, ACT.Exp, scale=-0.5).then_inc(sem("rsqrt_y"), 1)

            def norm(tag):
                rsqrt_guess(tag, rs[:, 0], rs[:, 1])

            def transposed(tag, k0, dst):
                for q in range(2):
                    act.wait_ge(sem("turned_ps"), 2 * TURNS.index(tag) + q + 1)
                    act.activation(dst[:, 2 * q:2 * q + 2, :].rearrange("p a b -> p (a b)"), bank(k0 + q),
                                   ACT.Copy).then_inc(sem("turned"), 1)

            norm("n0")
            transposed("n0", 3, hT)
            if layers > 2:
                rsqrt_guess("r2", r_v, r_y)
            for k in range(4):
                act.wait_ge(sem("in_rows"), 16 * (k + 1))
                rows = (src_row, dst_row)[k // 2]
                act.activation(rows[:, (k % 2) * (E // 2):(k % 2 + 1) * (E // 2)],
                               LW[:].rearrange("p a b -> p (a b)").bitcast(I32), ACT.Copy).then_inc(sem("rows_cast"), 1)
            rsqrt_guess("deg", rs[:, 0], rs[:, 1])
            if layers > 1:
                norm("n1")
                transposed("n1", 3, hT)

                def logits(i, b):
                    g = i * 2 + b
                    act.wait_ge(sem("l1a_ps"), g + 1)
                    act.activation(L[:, bass.ds(g * G, G), :].rearrange("p a b -> p (a b)"),
                                   bank(b)[:, 0:G * HD], ACT.Copy)
                    act.activation(l1_em[:, bass.ds(g * G, G), :].rearrange("p a b -> p (a b)"),
                                   bank(b)[:, 64:64 + G * HD], ACT.Copy).then_inc(sem("l1a_saved"), 1)
                with act.Fori(0, NG // 2) as i:
                    logits(i, 0)
                    logits(i, 1)

                def soft(g, b):
                    act.wait_ge(sem("l1_shift"), g + 1)
                    act.activation(Pe[:, b], Pz[:, b], ACT.Exp).then_inc(sem("l1_p"), 1)

                def tile(t, q, free):
                    act.wait_ge(sem("l1_msg"), t + 1)
                    if free:
                        act.wait_ge(sem("l1_scat"), t - 1)
                    act.activation(MSG[:, q, 0, 0:C], l1_m[:, q], ACT.Copy).then_inc(sem("l1_hi"), 1)

                def group(i, b, first, last):
                    g = i * 2 + b
                    for j in range(G):
                        tile(g * G + j, j % 2, not (first and b == 0 and j < 2))
                        if j == 2 and not (last and b == 1):
                            soft(g + 1, 1 - b)
                soft(0, 0)
                group(0, 0, True, False)
                group(0, 1, False, False)
                with act.Fori(1, NG // 2 - 1) as i:
                    group(i, 0, False, False)
                    group(i, 1, False, False)
                group(NG // 2 - 1, 0, False, False)
                group(NG // 2 - 1, 1, False, True)
                norm("n1o")
            if layers > 2:
                norm("n2")
                for k in range(NH):
                    act.wait_ge(sem("turned_ps"), 2 * TURNS.index("n2") + k + 1)
                    act.activation(hT[:, :, k * P:(k + 1) * P], bank(3 + k).rearrange("p (a b) -> p a b", a=4),
                                   ACT.Copy).then_inc(sem("turned"), 1)
                for k in range(NH):
                    act.wait_ge(sem("l2_tab_ps"), k + 1)
                    act.activation(l2_tab[k], bank(5 + k), ACT.Copy,
                                   scale=float(1.0 / np.sqrt(F))).then_inc(sem("l2_tab"), 1)

                def filt(g):
                    act.wait_ge(sem("l2_h_ps"), g + 1)
                    if not (isinstance(g, int) and g == 0):
                        act.wait_ge(sem("l2_ssp"), g)
                    act.activation(l2_s[0], bank(7), ACT.Abs, bias=bf1[:, 0:1]).then_inc(sem("l2_abs"), 1)
                    act.activation(l2_s[1], bank(7), ACT.Relu, bias=bf1[:, 0:1])
                    act.wait_ge(sem("l2_abs"), g + 1)
                    act.activation(l2_s[0], l2_s[0], ACT.Exp, scale=-1.0).then_inc(sem("l2_exp"), 1)
                    act.wait_ge(sem("l2_exp"), g + 1)
                    act.activation(l2_s[0], l2_s[0], ACT.Ln, bias=1.0).then_inc(sem("l2_ln"), 1)

                def weights(t, q, free):
                    act.wait_ge(sem("l2_w_ps"), t + 1)
                    if free:
                        act.wait_ge(sem("l2_msg"), t - 1)
                    act.activation(l2_w[:, q].rearrange("p a b -> p (a b)"), bank(6), ACT.Copy,
                                   scale=ew[:, bass.ds(t, 1)]).then_inc(sem("l2_w"), 1)

                def high(t, q, free):
                    act.wait_ge(sem("l2_msg"), t + 1)
                    act.wait_ge(sem("l2_outer"), t + 1)
                    if free:
                        act.wait_ge(sem("l2_scat"), t - 1)
                    act.activation(MSG[:, q, 0], l2_m[:, q, 0:8].rearrange("p a b -> p (a b)"),
                                   ACT.Copy).then_inc(sem("l2_hi"), 1)

                def outer(t, q, free):
                    act.wait_ge(sem("l2_sW"), t + 1)
                    if free:
                        act.wait_ge(sem("l2_lo"), t - 1)
                    for k in range(3):
                        last = act.activation(l2_m[:, q, 2 + k], l2_m[:, q, 8], ACT.Copy,
                                              scale=Yv[:, bass.ds(t, 1), k])
                    last.then_inc(sem("l2_outer"), 1)

                def group(i, b, first, last):
                    g = i * 2 + b
                    for j in range(G):
                        t = g * G + j
                        start = first and b == 0
                        end = last and b == 1
                        if not (end and j == G - 1):
                            weights(t + 1, (j + 1) % 2, not (start and j == 0))
                        outer(t, j % 2, not (start and j < 2))
                        high(t, j % 2, not (start and j < 2))
                        if j == 1 and not end:
                            filt(g + 1)
                act.wait_ge(sem("in_l2_weights"), 80)
                filt(0)
                weights(0, 0, False)
                group(0, 0, True, False)
                group(0, 1, False, False)
                with act.Fori(1, NG // 2 - 1) as i:
                    group(i, 0, False, False)
                    group(i, 1, False, False)
                group(NG // 2 - 1, 0, False, False)
                group(NG // 2 - 1, 1, False, True)
                act.wait_ge(sem("l2_S_ps"), 1)
                chain(act.activation(s2[:, 0], bank(4)[:, 0:N], ACT.Abs))
                act.activation(s2[:, 1], bank(4)[:, 0:N], ACT.Relu)
                chain(act.activation(s2[:, 0], s2[:, 0], ACT.Exp, scale=-1.0))
                act.activation(s2[:, 0], s2[:, 0], ACT.Ln, bias=1.0).then_inc(sem("l2_S_ln"), 1)
            if layers > 3:
                norm("n3")
                transposed("n3", 3, hT)

                def first_exp(kind, n, src, buf, free):
                    act.wait_ge(sem(f"l3{kind}_ps"), n + 1)
                    if free:
                        act.wait_ge(sem(f"l3{kind}_lo"), n - (1 if kind == "a" else 0))
                    act.activation(buf, src, ACT.Exp).then_inc(sem(f"l3{kind}_exp"), 1)

                def rest(kind, n, buf):
                    act.wait_ge(sem(f"l3{kind}_min"), n + 1)
                    act.activation(buf, buf, ACT.Square, bias=1.0).then_inc(sem(f"l3{kind}_sq"), 1)
                    act.wait_ge(sem(f"l3{kind}_sq"), n + 1)
                    act.activation(buf, buf, ACT.Ln, bias=0.5, scale=0.5).then_inc(sem(f"l3{kind}_ln"), 1)
                    act.wait_ge(sem(f"l3{kind}_ln"), n + 1)
                    act.activation(buf, buf, ACT.Exp, scale=-1.0).then_inc(sem(f"l3{kind}_q"), 1)

                fl = lambda a: a.rearrange("p a b -> p (a b)")

                def unit(kind, n, src, buf, free):
                    first_exp(kind, n, src, buf, free)
                    rest(kind, n, buf)

                def body(g, a, b, early):
                    if a:
                        unit("a", 2 * g, bank(0, 2), fl(UA[0]), early != 0)
                    if b:
                        unit("b", 2 * g - 2, bank(4, 2), fl(UB), early != 1)
                    if a:
                        unit("a", 2 * g + 1, bank(2, 2), fl(UA[1]), early != 0)
                    if b:
                        unit("b", 2 * g - 1, bank(4, 2), fl(UB), True)
                body(0, True, False, 0)
                body(1, True, True, 1)
                with act.Fori(2, NG) as g:
                    body(g, True, True, 2)
                body(NG, False, True, 2)
                transposed("n3b", 2, h3T)
                transposed("n3a", 4, hT)
                act.wait_ge(sem("l3_u_in"), 1)
                act.activation(fl(UA[1]), fl(UA[0]), ACT.Exp).then_inc(sem("l3_u_exp"), 1)
                act.wait_ge(sem("l3_u_min"), 1)
                chain(act.activation(fl(UA[1]), fl(UA[1]), ACT.Square, bias=1.0))
                chain(act.activation(fl(UA[1]), fl(UA[1]), ACT.Ln, bias=0.5, scale=0.5))
                act.activation(fl(UA[1]), fl(UA[1]), ACT.Exp, scale=-1.0).then_inc(sem("l3_u_q"), 1)
                transposed("n3u", 3, hT)
                norm("n3o")

        @block.tensor
        def _(pe):
            def transpose_nodes(tag, src, k0):
                pe.wait_ge(sem("h_ready"), NORMS.index(tag) + 1)
                for k in range(KC):
                    for h in range(NH):
                        o = bank(k0 + k // 2)[:, (k % 2) * N + h * P:(k % 2) * N + h * P + P]
                        m = pe.transpose(o, src[:, h, k * P:(k + 1) * P], ident[:])
                    if k % 2:
                        m.then_inc(sem("turned_ps"), 1)

            def node_mm(k0, xT, w, nk=KC, w0=0, start=True, stop=True):
                for h in range(NH):
                    for k in range(nk):
                        m = pe.matmul(bank(k0 + h), xT[:, k, h * P:(h + 1) * P], w[:, w0 + k, :],
                                      start=start and k == 0, stop=stop and k == nk - 1)
                return m

            def both(o, lhsT, hi, lo, start, stop, skip=False):
                pe.matmul(o, lhsT, hi, start=start, stop=False, skip_group_check=skip)
                return pe.matmul(o, lhsT, lo, start=False, stop=stop, skip_group_check=skip)

            def count(t, q, start, stop):
                pe.wait_ge(sem("l0_onehots"), t + 1)
                for h in range(NH):
                    m = pe.matmul(bank(h)[:, 0:N], l0_on[:, q, 0, h * P:(h + 1) * P], l0_on[:, q, 1, :],
                                  start=start, stop=stop)
                m.then_inc(sem("l0_count"), 1)
            transpose_nodes("n0", Hn, 3)
            pe.wait_ge(sem("turned"), 2 * TURNS.index("n0") + 2)
            pe.wait_ge(sem("in_L0_W"), 16)
            node_mm(5, hT, WN).then_inc(sem("l0_hW_ps"), 1)
            count(0, 0, True, False)
            count(1, 1, False, False)
            with pe.Fori(1, T // 2 - 1) as i:
                count(i * 2, 0, False, False)
                count(i * 2 + 1, 1, False, False)
            count(T - 2, 0, False, False)
            count(T - 1, 1, False, True)
            pe.wait_ge(sem("l0_adj"), 1)
            for h in range(NH):
                for k in range(NH):
                    m = pe.matmul(bank(2)[:, h:h + 1], adjT[:, k, h * P:(h + 1) * P], one_col[:, 0:1],
                                  start=k == 0, stop=k == NH - 1)
            m.then_inc(sem("l0_deg"), 1)
            pe.wait_ge(sem("l0_hW"), 1)
            for h in range(NH):
                for k in range(NH):
                    m = pe.matmul(bank(h), adjT[:, k, h * P:(h + 1) * P], hW[:, k, :], start=k == 0, stop=k == NH - 1)
            m.then_inc(sem("l0_ps"), 1)
            if layers > 1:
                transpose_nodes("n1", Hn, 3)
                pe.wait_ge(sem("turned"), 2 * TURNS.index("n1") + 2)
                pe.wait_ge(sem("in_L1_W"), 16)
                node_mm(5, hT, WN).then_inc(sem("l1_h_ps"), 1)
                pe.wait_ge(sem("l1_esd"), 1)

                def logits(i, b, free):
                    g = i * 2 + b
                    pe.wait_ge(sem("l1a_onehots"), g + 1)
                    if free:
                        pe.wait_ge(sem("l1a_saved"), g - 1)
                    for j in range(G):
                        o = bank(b)[:, j * HD:(j + 1) * HD]
                        for w, oh in enumerate((ST, DT)):
                            for h in range(NH):
                                both(o, oh[:, b, h, j * P:(j + 1) * P], NT[:, w, 0, h], NT[:, w, 1, h],
                                     w == 0 and h == 0, w == 1 and h == 1)
                        o = bank(b)[:, 64 + j * HD:64 + (j + 1) * HD]
                        m = both(o, T8[:, b, j * P:(j + 1) * P], EMB[:, 0], EMB[:, 1], True, True)
                    m.then_inc(sem("l1a_ps"), 1)
                logits(0, 0, False)
                logits(0, 1, False)
                with pe.Fori(1, NG // 2) as i:
                    logits(i, 0, True)
                    logits(i, 1, True)

                pe.wait_ge(sem("l1b_max"), T)
                for h in range(NH):
                    for hd in range(HD):
                        k = h * 2 + hd // 4
                        m = pe.transpose(bank(k)[:, (hd % 4) * P:(hd % 4 + 1) * P], R[:, hd, h * P:(h + 1) * P],
                                         ident[:])
                        if hd % 4 == 3:
                            m.then_inc(sem("l1_mx_ps"), 1)

                def shift(g, b, free):
                    pe.wait_ge(sem("l1c_onehots"), g + 1)
                    if free:
                        pe.wait_ge(sem("l1_shift"), g - 1)
                    for j in range(G):
                        for h in range(NH):
                            m = both(bank(6 + b)[:, j * HD:(j + 1) * HD], DT[:, b, h, j * P:(j + 1) * P],
                                     MX[:, 0, h], MX[:, 1, h], h == 0, h == 1)
                    m.then_inc(sem("l1_mg_ps"), 1)

                def gather(t, b, j, free):
                    if free:
                        pe.wait_ge(sem("l1_msg"), t - 1)
                    for h in range(NH):
                        m = both(bank(4 + j % 2), ST[:, b, h, j * P:(j + 1) * P], TAB[:, 0, 0, h], TAB[:, 0, 1, h],
                                 h == 0, h == 1)
                    m.then_inc(sem("l1_hs_ps"), 1)

                def scatter(t, b, j, start, stop):
                    pe.wait_ge(sem("l1_lo"), t + 1)
                    for h in range(NH):
                        oh = EN[:, b, j, h * P:(h + 1) * P]
                        both(bank(h), oh, MSG[:, j % 2, 0, 0:C], MSG[:, j % 2, 1, 0:C], start, stop)
                        m = both(bank(2 + h)[:, 0:HD], oh, Ps[:, b, 0, j * HD:(j + 1) * HD],
                                 Ps[:, b, 1, j * HD:(j + 1) * HD], start, stop)
                    m.then_inc(sem("l1_scat"), 1)

                def group(i, b, first, last):
                    g = i * 2 + b
                    for j in range(G):
                        t = g * G + j
                        begin = first and b == 0
                        if j < G - 1:
                            gather(t + 1, b, j + 1, not (begin and j == 0))
                        elif not (last and b == 1):
                            gather(t + 1, 1 - b, 0, True)
                        if not (begin and j == 0):
                            scatter(t - 1, b if j else 1 - b, (j - 1) % G, begin and j == 1, False)
                        if j == 1 and not (last and b == 1):
                            shift(g + 1, 1 - b, not begin)
                pe.wait_ge(sem("l1_mx"), 1)
                shift(0, 0, False)
                gather(0, 0, 0, False)
                group(0, 0, True, False)
                group(0, 1, False, False)
                with pe.Fori(1, NG // 2 - 1) as i:
                    group(i, 0, False, False)
                    group(i, 1, False, False)
                group(NG // 2 - 1, 0, False, False)
                group(NG // 2 - 1, 1, False, True)
                scatter(T - 1, 1, G - 1, False, True)
            if layers > 2:
                pe.wait_ge(sem("h_ready"), NORMS.index("n2") + 1)
                for h in range(NH):
                    for k in range(4):
                        src = Hn[:, h, 0:F] if k == 0 else Hn[:, h, F + k - 1:C:3]
                        m = pe.transpose(bank(3 + h)[:, k * P:(k + 1) * P], src, ident[:])
                    m.then_inc(sem("turned_ps"), 1)
                pe.wait_ge(sem("in_l2_weights"), 80)
                for h in range(NH):
                    pe.wait_ge(sem("turned"), 2 * TURNS.index("n2") + h + 1)
                    for k in range(4):
                        m = pe.matmul(bank(5 + h)[:, k * F:(k + 1) * F], hT[:, k, h * P:(h + 1) * P],
                                      Win[:, min(k, 1)], start=True, stop=True)
                    m.then_inc(sem("l2_tab_ps"), 1)

                def hidden(g, b, free):
                    pe.wait_ge(sem(f"in_rbf{b}"), (g - b) * 8 + 16)
                    if free:
                        pe.wait_ge(sem("l2_ssp"), g)
                    pe.matmul(bank(7), Wf1[:], fT[:, b], start=True, stop=True).then_inc(sem("l2_h_ps"), 1)

                def gather(t, b, j, free):
                    if free:
                        pe.wait_ge(sem("l2_msg"), t - 1)
                    for h in range(NH):
                        m = both(bank(4 + j % 2), DT[:, b, h, j * P:(j + 1) * P], TAB[:, 0, 0, h], TAB[:, 0, 1, h],
                                 h == 0, h == 1)
                    m.then_inc(sem("l2_g_ps"), 1)

                def weights(t, b, j, free):
                    if free:
                        pe.wait_ge(sem("l2_w"), t)
                    s = slice(j * P, (j + 1) * P)
                    pe.matmul(bank(6), HT[:, b, 0, 0, s], WF2[:, 0], start=True, stop=False)
                    pe.matmul(bank(6), HT[:, b, 0, 0, s], WF2[:, 1], start=False, stop=False)
                    pe.matmul(bank(6), HT[:, b, 1, 0, s], WF2[:, 0], start=False, stop=False)
                    pe.matmul(bank(6), ones[:], BF2[:], start=False, stop=True).then_inc(sem("l2_w_ps"), 1)

                def scatter(t, b, j, start, stop):
                    pe.wait_ge(sem("l2_lo"), t + 1)
                    for h in range(NH):
                        for c in range(2):
                            m = both(bank(2 * h + c), EN[:, b, j, h * P:(h + 1) * P],
                                     MSG[:, j % 2, 0, c * C:(c + 1) * C], MSG[:, j % 2, 1, c * C:(c + 1) * C],
                                     start, stop)
                    m.then_inc(sem("l2_scat"), 1)

                def group(i, b, first, last):
                    g = i * 2 + b
                    begin = first and b == 0
                    for j in range(G):
                        t = g * G + j
                        if j < G - 1:
                            weights(t + 1, b, j + 1, True)
                            gather(t + 1, b, j + 1, not (begin and j == 0))
                        elif not (last and b == 1):
                            pe.wait_ge(sem("l2_onehots"), g + 2)
                            pe.wait_ge(sem("l2_hid"), g + 2)
                            weights(t + 1, 1 - b, 0, True)
                            gather(t + 1, 1 - b, 0, True)
                        if not (begin and j == 0):
                            scatter(t - 1, b if j else 1 - b, (j - 1) % G, begin and j == 1, False)
                        if j == 0 and not (last and b == 1):
                            hidden(g + 1, 1 - b, True)
                pe.wait_ge(sem("in_l2_weights"), 80)
                pe.wait_ge(sem("l2_ready"), 1)
                hidden(0, 0, False)
                pe.wait_ge(sem("l2_onehots"), 1)
                pe.wait_ge(sem("l2_hid"), 1)
                weights(0, 0, 0, False)
                gather(0, 0, 0, False)
                group(0, 0, True, False)
                group(0, 1, False, False)
                with pe.Fori(1, NG // 2 - 1) as i:
                    group(i, 0, False, False)
                    group(i, 1, False, False)
                group(NG // 2 - 1, 0, False, False)
                group(NG // 2 - 1, 1, False, True)
                scatter(T - 1, 1, G - 1, False, True)
                for h in range(NH):
                    pe.wait_ge(sem("l2_agg"), h + 1)
                    for k in range(8):
                        m = pe.transpose(bank(4 + k // 2)[:, (k % 2) * N + h * P:(k % 2) * N + h * P + P],
                                         l2_agg[:, h, k], ident[:])
                m.then_inc(sem("l2_aggT_ps"), 1)
                pe.wait_ge(sem("l2_aggT"), 1)
                pe.wait_ge(sem("in_l2_weights"), 80)
                for k in range(2):
                    m = pe.matmul(bank(4)[:, 0:N], W1sv[:, 0, k], aggT[:, k], start=k == 0, stop=k == 1)
                m.then_inc(sem("l2_S_ps"), 1)
                for c in range(3):
                    for k in range(2):
                        m = pe.matmul(bank(5 + c)[:, 0:N], W1sv[:, 1, k], aggT[:, 2 + 3 * k + c],
                                      start=k == 0, stop=k == 1)
                m.then_inc(sem("l2_V_ps"), 1)
                pe.wait_ge(sem("l2_SV"), 1)
                pe.wait_ge(sem("in_l2_weights"), 80)
                for h in range(NH):
                    for k in range(4):
                        m = pe.matmul(bank(h)[:, k * F:(k + 1) * F], SV[:, k, h * P:(h + 1) * P],
                                      W2sv[:, min(k, 1)], start=True, stop=True)
                m.then_inc(sem("l2_ps"), 1)
            if layers > 3:
                transpose_nodes("n3", Hn, 3)
                pe.wait_ge(sem("turned"), 2 * TURNS.index("n3") + 2)
                pe.wait_ge(sem("in_L3_W1ab"), 16)
                node_mm(5, hT, LW).then_inc(sem("l3_tab_ps"), 1)
                pe.wait_ge(sem("l3_tab"), 1)
                node_mm(5, hT, LW, w0=KC).then_inc(sem("l3_tab_ps"), 1)

                def edge_in(n, g, b, m2, free):
                    if free:
                        pe.wait_ge(sem("l3a_y"), n - 1)
                    for k in range(2):
                        m = 2 * m2 + k
                        o, s = bank(2 * m2 + k), slice(m * P, (m + 1) * P)
                        for w, oh in enumerate((ST, DT)):
                            for h in range(NH):
                                for part in range(2):
                                    pe.matmul(o, TAB[:, w, part, h, s], oh[:, b, h], start=w + h + part == 0,
                                              stop=False)
                        pe.matmul(o, WEA[:, 0, s], EA[:, b], start=False, stop=False)
                        last = pe.matmul(o, WEA[:, 1, s], EB[:, b], start=False, stop=True)
                    last.then_inc(sem("l3a_ps"), 1)

                def edge_hid(n, b, half_, free):
                    if free:
                        pe.wait_ge(sem("l3b_y"), n)
                    for k in range(2):
                        o, s = bank(4 + k), slice((2 * half_ + k) * P, (2 * half_ + k + 1) * P)
                        for c in range(KC):
                            pe.matmul(o, HT[:, b, 0, c, s], W2S[:, 0, c], start=c == 0, stop=False)
                            pe.matmul(o, HT[:, b, 0, c, s], W2S[:, 1, c], start=False, stop=False)
                            pe.matmul(o, HT[:, b, 1, c, s], W2S[:, 0, c], start=False, stop=False)
                        last = pe.matmul(o, ones[:], B2S[:], start=False, stop=True)
                    last.then_inc(sem("l3b_ps"), 1)

                def scatter(n, b, half_, start, stop):
                    pe.wait_ge(sem("l3b_lo"), n + 1)
                    for k in range(2):
                        for h in range(NH):
                            m = both(bank(6 + h), EN[:, b, 2 * half_ + k, h * P:(h + 1) * P],
                                     MSG[:, half_, 0, k * C:(k + 1) * C], MSG[:, half_, 1, k * C:(k + 1) * C],
                                     start and k == 0, stop and k == 1)
                    m.then_inc(sem("l3_scat"), 1)

                def body(g, b, a, bb, early):
                    if a:
                        pe.wait_ge(sem("l3_onehots"), g + 1)
                        edge_in(2 * g, g, b, 0, early != 0)
                    if bb:
                        pe.wait_ge(sem("l3a_lo"), 2 * g)
                        edge_hid(2 * g - 2, 1 - b, 0, early != 1)
                        if early != 1:
                            scatter(2 * g - 3, b, 1, False, False)
                    if a:
                        edge_in(2 * g + 1, g, b, 1, early != 0)
                    if bb:
                        edge_hid(2 * g - 1, 1 - b, 1, True)
                        pe.wait_ge(sem("l3_en"), g)
                        scatter(2 * g - 2, 1 - b, 0, early == 1, False)
                pe.wait_ge(sem("l3_ready"), 1)
                body(0, 0, True, False, 0)
                body(1, 1, True, True, 1)
                with pe.Fori(1, NG // 2) as i:
                    body(i * 2, 0, True, True, 2)
                    body(i * 2 + 1, 1, True, True, 2)
                body(NG, 0, False, True, 2)
                scatter(2 * NG - 1, 1, 1, False, True)
                def transpose_any(tag, src, k0):
                    for k in range(KC):
                        for h in range(NH):
                            o = bank(k0 + k // 2)[:, (k % 2) * N + h * P:(k % 2) * N + h * P + P]
                            m = pe.transpose(o, src[:, h, k * P:(k + 1) * P], ident[:])
                        if k % 2:
                            m.then_inc(sem("turned_ps"), 1)
                pe.wait_ge(sem("l3b_lo"), 2 * NG)
                transpose_any("n3b", Hn, 2)
                pe.wait_ge(sem("l3_agg"), 1)
                transpose_any("n3a", agg3, 4)
                pe.wait_ge(sem("turned"), 2 * TURNS.index("n3b") + 2)
                pe.wait_ge(sem("in_L3_W3"), 16)
                pe.wait_ge(sem("turned"), 2 * TURNS.index("n3a") + 2)
                for h in range(NH):
                    for k in range(2 * KC):
                        xT = h3T if k < KC else hT
                        m = pe.matmul(bank(h), xT[:, k % KC, h * P:(h + 1) * P], LW[:, k, :],
                                      start=k == 0, stop=k == 2 * KC - 1)
                m.then_inc(sem("l3_u_ps"), 1)
                pe.wait_ge(sem("l3_u"), 1)
                transpose_any("n3u", UA[0], 3)
                pe.wait_ge(sem("turned"), 2 * TURNS.index("n3u") + 2)
                pe.wait_ge(sem("in_L3_W4"), 16)
                node_mm(5, hT, WN).then_inc(sem("l3_out_ps"), 1)

        @block.vector
        def _(dve):
            chain = Chain(dve, "dve_chain")
            tt, ts, stt, cp = dve.tensor_tensor, dve.tensor_scalar, dve.scalar_tensor_tensor, dve.tensor_copy

            def split(hi, lo, src):
                chain(cp(hi, src))
                return tt(lo, src, f(hi), ALU.subtract)

            def newton(y, v, t):
                chain(tt(t, y, y, ALU.mult))
                chain(tt(t, t, v, ALU.mult))
                chain(ts(t, t, -0.5, 1.5, ALU.mult, ALU.add))
                chain(tt(y, y, t, ALU.mult))

            def moments(tag, src):
                for h in range(NH):
                    chain(dve.bn_stats(stats[:, h], src[:, h]))
                for h in range(NH):
                    chain(dve.bn_aggr(mv[:, h], stats[:, h]))
                ts(rs[:, 0], mv[:, :, 1], LN_EPS, None, ALU.add).then_inc(sem("rsqrt_v"), 1)
                dve.wait_ge(sem("rsqrt_y"), RSQRT.index(tag) + 1)
                newton(rs[:, 1], rs[:, 0], rs[:, 2])

            def relu_norm(tag):
                moments(tag, X)
                for h in range(NH):
                    chain(ts(Hn[:, h], X[:, h], mv[:, h, 0:1], rs[:, 1, h:h + 1], ALU.subtract, ALU.mult))
                ts(Hn[:], Hn[:], 0.0, None, ALU.max).then_inc(sem("h_ready"), 1)

            def affine_norm(tag, src, gamma, beta):
                moments(tag, src)
                for h in range(NH):
                    chain(ts(src[:, h], src[:, h], mv[:, h, 0:1], rs[:, 1, h:h + 1], ALU.subtract, ALU.mult))
                    chain(tt(src[:, h], src[:, h], gamma, ALU.mult))
                    chain(tt(src[:, h], src[:, h], beta, ALU.add))
                return tt(X[:], X[:], src, ALU.add)

            def onehot_T(dst, row_, b, g):
                for h in range(NH):
                    last = ts(dst[:, b, h], row_[:, bass.ds(g * GE, GE)], node_col[:, h:h + 1], None, ALU.is_equal)
                return last

            def onehot_E(col, b, g):
                for j in range(G):
                    last = ts(EN[:, b, j], node_row[:], col[:, bass.ds(g * G + j, 1)], None, ALU.is_equal)
                return last

            dve.wait_ge(sem("iotas"), 2)
            chain(ts(ident[:], node_row[:, 0:P], node_col[:, 0:1], None, ALU.is_equal))
            chain(dve.memset(one_col[:], 1.0))
            for a, v in ((ones, 1.0), (BF2, 0.0), (B2S, 0.0), (WEA, 0.0), (EB, 1.0)):
                chain(dve.memset(f(a[:]), v))
            dve.wait_ge(sem("in_idx"), 16)
            chain(cp(src_col[:], idx_raw[:, 0]))
            chain(cp(dst_col[:], idx_raw[:, 1]))

            dve.wait_ge(sem("in_x"), 16)
            relu_norm("n0")
            if layers > 2:
                dve.wait_ge(sem("in_ea3"), 16)
                chain(tt(r_sq, Yv[:], Yv[:], ALU.mult))
                dve.tensor_reduce(r_v, r_sq, AX, ALU.add).then_inc(sem("rsqrt_v"), 1)

            def onehots0(t, q, wait):
                if wait:
                    dve.wait_ge(sem("l0_count"), t - 1)
                ts(l0_on[:, q, 0], node_row[:], dst_col[:, bass.ds(t, 1)], None, ALU.is_equal)
                ts(l0_on[:, q, 1], node_row[:], src_col[:, bass.ds(t, 1)], None,
                   ALU.is_equal).then_inc(sem("l0_onehots"), 1)
            onehots0(0, 0, False)
            onehots0(1, 1, False)
            with dve.Fori(1, T // 2) as i:
                onehots0(i * 2, 0, True)
                onehots0(i * 2 + 1, 1, True)
            dve.wait_ge(sem("l0_count"), T)
            for h in range(NH):
                chain(ts(adjT[:, h], bank(h)[:, 0:N], 1.0, None, ALU.min))
            for h in range(NH):
                s = slice(h * P, (h + 1) * P)
                last = tt(adjT[:, h, s], adjT[:, h, s], ident[:], ALU.max)
            last.then_inc(sem("l0_adj"), 1)
            dve.wait_ge(sem("l0_deg"), 1)
            cp(rs[:, 0], bank(2)[:, 0:NH]).then_inc(sem("rsqrt_v"), 1)
            dve.wait_ge(sem("rsqrt_y"), RSQRT.index("deg") + 1)
            newton(rs[:, 1], rs[:, 0], rs[:, 2])
            chain(cp(dis, rs[:, 1]))
            dve.wait_ge(sem("l0_hW_ps"), 1)
            dve.wait_ge(sem("in_L0_b"), 16)
            for h in range(NH):
                chain(tt(hW[:, h], bank(5 + h), V[:, 0], ALU.add))
                last = ts(hW[:, h], hW[:, h], dis[:, h:h + 1], None, ALU.mult)
            last.then_inc(sem("l0_hW"), 1)
            dve.wait_ge(sem("l0_ps"), 1)
            for h in range(NH):
                last = stt(X[:, h], bank(h), dis[:, h:h + 1], X[:, h], ALU.mult, ALU.add)
            chain(last)
            dve.wait_ge(sem("dve_chain"), chain.n)
            done = ts(rs[:, 3], rs[:, 0], 0.0, None, ALU.mult)
            done.then_inc(sem("x_done"), 1)
            dve.wait_ge(sem("x_done"), 1)
            if layers > 2:
                dve.wait_ge(sem("rsqrt_y"), RSQRT.index("r2") + 1)
                newton(r_y, r_v, r_sq.rearrange("p a b -> p (a b)")[:, 0:T])
                chain(ts(r_y, r_y, Y1, None, ALU.mult))
                chain(tt(Yv[:], Yv[:], r_y.unsqueeze(2).to_broadcast([P, T, 3]), ALU.mult))

            if layers > 1:
                relu_norm("n1")
                dve.wait_ge(sem("l1_h_ps"), 1)
                dve.wait_ge(sem("in_l1_vectors"), 48)
                for h in range(NH):
                    split(TAB[:, 0, 0, h], TAB[:, 0, 1, h], bank(5 + h))
                    for w in range(2):
                        chain(tt(l1_t[:, h], bank(5 + h), V[:, 1 + w], ALU.mult))
                        chain(dve.tensor_reduce(nt[:, w, h], l1_t[:, h].rearrange("p (a b) -> p a b", a=HD), AX, ALU.add))
                for w in range(2):
                    last = split(NT[:, w, 0], NT[:, w, 1], nt[:, w])
                dve.wait_ge(sem("in_l1_vectors"), 48)
                split(EMB[:, 0], EMB[:, 1], emb[:]).then_inc(sem("l1_esd"), 1)

                def onehots1(i, b, wait):
                    g = i * 2 + b
                    if wait:
                        dve.wait_ge(sem("l1a_ps"), g - 1)
                    else:
                        dve.wait_ge(sem("rows_cast"), 4)
                    dve.wait_ge(sem(f"in_type{b}"), i * 16 + 16)
                    onehot_T(ST, src_row, b, g)
                    onehot_T(DT, dst_row, b, g)
                    ts(T8[:, b], typ[:, b], node_col[0:HD, 0:1], None, ALU.is_equal).then_inc(sem("l1a_onehots"), 1)
                onehots1(0, 0, False)
                onehots1(0, 1, False)
                with dve.Fori(1, NG // 2) as i:
                    onehots1(i, 0, True)
                    onehots1(i, 1, True)

                dve.wait_ge(sem("l1a_saved"), NG)
                dve.wait_ge(sem("in_ew"), 16)
                chain(stt(L[:], L[:], 0.2, L[:], ALU.mult, ALU.max))
                chain(stt(L[:], l1_em, 1.0, L[:], ALU.add, ALU.mult))
                chain(tt(L[:], L[:], ew[:].unsqueeze(2).to_broadcast([P, T, HD]), ALU.mult))

                chain(dve.memset(R, 0.0))

                def onehots1b(g, b, wait):
                    if wait:
                        dve.wait_ge(sem("l1b_max"), g * G - G)
                    onehot_E(dst_col, b, g).then_inc(sem("l1b_onehots"), 1)

                def maxima(i, b, first, last):
                    g = i * 2 + b
                    if not (last and b == 1):
                        onehots1b(g + 1, 1 - b, not (first and b == 0))
                    dve.wait_ge(sem("l1b_onehots"), g + 1)
                    for j in range(G):
                        if not (first and b == 0 and j == 0):
                            dve.wait_ge(sem("l1b_max"), g * G + j)
                        for hd in range(HD):
                            m = stt(R[:, hd], f(EN[:, b, j]), L[:, bass.ds(g * G + j, 1), hd], R[:, hd],
                                    ALU.mult, ALU.max)
                        m.then_inc(sem("l1b_max"), 1)
                onehots1b(0, 0, False)
                maxima(0, 0, True, False)
                maxima(0, 1, False, False)
                with dve.Fori(1, NG // 2 - 1) as i:
                    maxima(i, 0, False, False)
                    maxima(i, 1, False, False)
                maxima(NG // 2 - 1, 0, False, False)
                maxima(NG // 2 - 1, 1, False, True)
                dve.wait_ge(sem("l1b_max"), T)
                for k in range(2 * NH):
                    dve.wait_ge(sem("l1_mx_ps"), k + 1)
                    chain(dve.tensor_reduce(MXf[:, k // 2, 4 * (k % 2):4 * (k % 2) + 4],
                                            bank(k).rearrange("p (a b) -> p a b", a=4), AX, ALU.max))
                split(MX[:, 0], MX[:, 1], MXf[:]).then_inc(sem("l1_mx"), 1)

                def onehots(g, b, wait):
                    if wait:
                        dve.wait_ge(sem("l1_scat"), g * G - G)
                    onehot_T(DT, dst_row, b, g)
                    onehot_T(ST, src_row, b, g)
                    onehot_E(dst_col, b, g).then_inc(sem("l1c_onehots"), 1)

                def soft(g, b):
                    dve.wait_ge(sem("l1_mg_ps"), g + 1)
                    tt(Pz[:, b], L[:, bass.ds(g * G, G), :].rearrange("p a b -> p (a b)"), bank(6 + b)[:, 0:G * HD],
                       ALU.subtract).then_inc(sem("l1_shift"), 1)
                    dve.wait_ge(sem("l1_p"), g + 1)
                    cp(Ps[:, b, 0], Pe[:, b]).then_inc(sem("l1_phi"), 1)
                    dve.wait_ge(sem("l1_phi"), g + 1)
                    tt(Ps[:, b, 1], Pe[:, b], f(Ps[:, b, 0]), ALU.subtract)

                def message(t, b, j, wait):
                    q = j % 2
                    dve.wait_ge(sem("l1_hs_ps"), t + 1)
                    if wait:
                        dve.wait_ge(sem("l1_lo"), t - 1)
                    p = Pe[:, b, j * HD:(j + 1) * HD].unsqueeze(2).to_broadcast([P, HD, C // HD])
                    tt(l1_m[:, q].rearrange("p (a b) -> p a b", a=HD), bank(4 + q).rearrange("p (a b) -> p a b", a=HD),
                       p, ALU.mult).then_inc(sem("l1_msg"), 1)

                def low(t, q):
                    dve.wait_ge(sem("l1_hi"), t + 1)
                    tt(MSG[:, q, 1, 0:C], l1_m[:, q], f(MSG[:, q, 0, 0:C]), ALU.subtract).then_inc(sem("l1_lo"), 1)

                def group(i, b, first, last):
                    g = i * 2 + b
                    begin = first and b == 0
                    for j in range(G):
                        t = g * G + j
                        message(t, b, j, not (begin and j < 2))
                        if not (begin and j == 0):
                            low(t - 1, (j - 1) % 2)
                        if j == 0 and not (last and b == 1):
                            onehots(g + 1, 1 - b, not begin)
                        if j == 2 and not (last and b == 1):
                            soft(g + 1, 1 - b)
                onehots(0, 0, False)
                soft(0, 0)
                group(0, 0, True, False)
                group(0, 1, False, False)
                with dve.Fori(1, NG // 2 - 1) as i:
                    group(i, 0, False, False)
                    group(i, 1, False, False)
                group(NG // 2 - 1, 0, False, False)
                group(NG // 2 - 1, 1, False, True)
                low(T - 1, 1)
                dve.wait_ge(sem("l1_scat"), T)
                for h in range(NH):
                    chain(ts(nt[:, 0, h], bank(2 + h)[:, 0:HD], 1e-10, None, ALU.add))
                    chain(dve.reciprocal(nt[:, 0, h], nt[:, 0, h]))
                    chain(tt(l1_t[:, h].rearrange("p (a b) -> p a b", a=HD), bank(h).rearrange("p (a b) -> p a b", a=HD),
                             nt[:, 0, h].unsqueeze(2).to_broadcast([P, HD, C // HD]), ALU.mult))
                chain(tt(l1_t, l1_t, Hn[:], ALU.add))
                dve.wait_ge(sem("in_l1_affine"), 32)
                affine_norm("n1o", l1_t, V[:, 1], V[:, 2]).then_inc(sem("x_done"), 1)
                dve.wait_ge(sem("x_done"), 2)
                ts(rs[:, 3], rs[:, 0], 0.0, None, ALU.mult).then_inc(sem("l1_out"), 1)

            if layers > 2:
                dve.wait_ge(sem("in_l2_filter"), 48)
                split(WF2[:, 0], WF2[:, 1], LW[:, 0])
                chain(cp(BF2[0:1], LW[0:1, 1]))
                chain(cp(BF2[32:33], LW[32:33, 1]))
                tt(BF2[32:33], LW[32:33, 1], f(BF2[32:33]), ALU.subtract).then_inc(sem("l2_wsplit"), 1)
                relu_norm("n2")
                for h in range(NH):
                    dve.wait_ge(sem("l2_tab"), h + 1)
                    last = split(TAB[:, 0, 0, h], TAB[:, 0, 1, h], l2_tab[h])
                last.then_inc(sem("l2_ready"), 1)

                def onehots(g, b, wait):
                    if wait:
                        dve.wait_ge(sem("l2_scat"), g * G - G)
                    onehot_T(DT, dst_row, b, g)
                    onehot_E(src_col, b, g).then_inc(sem("l2_onehots"), 1)

                def filt(g, b):
                    dve.wait_ge(sem("l2_ln"), g + 1)
                    stt(l2_s[2], l2_s[1], -LOG2, l2_s[0], ALU.add, ALU.add).then_inc(sem("l2_ssp"), 1)
                    dve.wait_ge(sem("l2_ssp"), g + 1)
                    cp(HT[:, b, 0, 0], l2_s[2]).then_inc(sem("l2_hid_hi"), 1)
                    dve.wait_ge(sem("l2_hid_hi"), g + 1)
                    tt(HT[:, b, 1, 0], l2_s[2], f(HT[:, b, 0, 0]), ALU.subtract).then_inc(sem("l2_hid"), 1)

                def message(t, q, wait):
                    m, w = l2_m[:, q], l2_w[:, q]
                    x = bank(4 + q).rearrange("p (a b) -> p a b", a=4)
                    y = Yv[:, bass.ds(t, 1), :].rearrange("p a b -> p (a b)")
                    dve.wait_ge(sem("l2_g_ps"), t + 1)
                    if wait:
                        dve.wait_ge(sem("l2_lo"), t - 1)
                    ts(m[:, 1], x[:, 1], y[:, 0:1], None, ALU.mult).then_inc(sem("l2_dot"), 1)
                    dve.wait_ge(sem("l2_w"), t + 1)
                    tt(m[:, 0:9:8], x[:, 0:1].to_broadcast([P, 2, F]), w[:, 0:3:2], ALU.mult).then_inc(sem("l2_sW"), 1)
                    dve.wait_ge(sem("l2_dot"), t * 3 + 1)
                    stt(m[:, 1], x[:, 2], y[:, 1:2], m[:, 1], ALU.mult, ALU.add).then_inc(sem("l2_dot"), 1)
                    tt(m[:, 5:8], x[:, 1:4], w[:, 3:4].to_broadcast([P, 3, F]), ALU.mult)
                    dve.wait_ge(sem("l2_dot"), t * 3 + 2)
                    stt(m[:, 1], x[:, 3], y[:, 2:3], m[:, 1], ALU.mult, ALU.add).then_inc(sem("l2_dot"), 1)
                    dve.wait_ge(sem("l2_dot"), t * 3 + 3)
                    tt(m[:, 1], m[:, 1], w[:, 1], ALU.mult).then_inc(sem("l2_msg"), 1)

                def low(t, q):
                    dve.wait_ge(sem("l2_hi"), t + 1)
                    tt(MSG[:, q, 1], l2_m[:, q, 0:8].rearrange("p a b -> p (a b)"), f(MSG[:, q, 0]),
                       ALU.subtract).then_inc(sem("l2_lo"), 1)

                def group(i, b, first, last):
                    g = i * 2 + b
                    begin = first and b == 0
                    for j in range(G):
                        t = g * G + j
                        message(t, j % 2, not (begin and j < 2))
                        if not (begin and j == 0):
                            low(t - 1, (j - 1) % 2)
                        if j == 0 and not (last and b == 1):
                            onehots(g + 1, 1 - b, not begin)
                        if j == 2 and not (last and b == 1):
                            filt(g + 1, 1 - b)
                onehots(0, 0, False)
                filt(0, 0)
                group(0, 0, True, False)
                group(0, 1, False, False)
                with dve.Fori(1, NG // 2 - 1) as i:
                    group(i, 0, False, False)
                    group(i, 1, False, False)
                group(NG // 2 - 1, 0, False, False)
                group(NG // 2 - 1, 1, False, True)
                low(T - 1, 1)
                dve.wait_ge(sem("l2_scat"), T)
                c = 1.0 / float(np.sqrt(2 * F))
                for h in range(NH):
                    a = bank(2 * h, 2).rearrange("p (a b) -> p a b", a=8)
                    for k0, k1, scale in ((0, 1, c * Y0), (1, 2, c / float(np.sqrt(3.0))), (2, 5, c), (5, 8, c * Y0)):
                        last = ts(l2_agg[:, h, k0:k1], a[:, k0:k1], scale, None, ALU.mult)
                    last.then_inc(sem("l2_agg"), 1)
                dve.wait_ge(sem("l2_aggT_ps"), 1)
                cp(aggT.rearrange("p a b -> p (a b)"), bank(4, 4)).then_inc(sem("l2_aggT"), 1)
                dve.wait_ge(sem("l2_V_ps"), 1)
                for k in range(3):
                    cp(SV[:, 1 + k], bank(5 + k)[:, 0:N])
                dve.wait_ge(sem("l2_S_ln"), 1)
                stt(SV[:, 0], s2[:, 1], -LOG2, s2[:, 0], ALU.add, ALU.add).then_inc(sem("l2_SV"), 1)
                dve.wait_ge(sem("l2_ps"), 1)
                c = 1.0 / float(np.sqrt(F))
                for h in range(NH):
                    a = bank(h).rearrange("p (a b) -> p a b", a=4)
                    stt(X[:, h, 0:F], a[:, 0], c, X[:, h, 0:F], ALU.mult, ALU.add)
                    xv = X[:, h, F:C].rearrange("p (f i) -> p i f", i=3)
                    last = stt(xv, a[:, 1:4], c, xv, ALU.mult, ALU.add)
                last.then_inc(sem("x_done"), 1)
                dve.wait_ge(sem("x_done"), 3)
                ts(rs[:, 3], rs[:, 0], 0.0, None, ALU.mult).then_inc(sem("l2_out"), 1)

            if layers > 3:
                relu_norm("n3")
                dve.wait_ge(sem("in_L3_W2"), 16)
                split(W2S[:, 0], W2S[:, 1], WN[:]).then_inc(sem("l3_w2split"), 1)
                dve.wait_ge(sem("in_l3_edge_weights"), 96)
                raw = u(0, 3, C)
                chain(cp(WEA[:, 0], raw[:, 0]))
                chain(tt(WEA[0:64, 1], raw[0:64, 0], f(WEA[0:64, 0]), ALU.subtract))
                chain(cp(WEA[64:65, 1], raw[64:65, 1]))
                chain(cp(WEA[96:97, 1], raw[96:97, 1]))
                chain(tt(WEA[96:97, 1], raw[96:97, 1], f(WEA[96:97, 1]), ALU.subtract))
                chain(cp(B2S[0:1], raw[0:1, 2]))
                chain(cp(B2S[32:33], raw[32:33, 2]))
                chain(tt(B2S[32:33], raw[32:33, 2], f(B2S[32:33]), ALU.subtract))

                def features(g, b):
                    dve.wait_ge(sem("in_ea"), g * 32 + 32)
                    cp(EA[:, b], ea_raw).then_inc(sem("l3_ea_hi"), 1)
                    dve.wait_ge(sem("l3_ea_hi"), g + 1)
                    tt(EA[64:P, b], ea_raw[64:P], f(EA[64:P, b]), ALU.subtract)
                    cp(EB[0:64, b], ea_raw[0:64]).then_inc(sem("l3_ea"), 1)

                def onehots(g, b, wait):
                    if wait:
                        dve.wait_ge(sem("l3a_ps"), g * 2 - 2)
                    features(g, b)
                    onehot_T(ST, src_row, b, g)
                    onehot_T(DT, dst_row, b, g).then_inc(sem("l3_onehots"), 1)

                def onehots_E(g, b, wait):
                    if wait:
                        dve.wait_ge(sem("l3_scat"), g * 2 - 2)
                    onehot_E(dst_col, b, g).then_inc(sem("l3_en"), 1)
                onehots(0, 0, False)
                for w in range(2):
                    dve.wait_ge(sem("l3_tab_ps"), w + 1)
                    for h in range(NH):
                        last = split(TAB[:, w, 0, h], TAB[:, w, 1, h], bank(5 + h))
                    last.then_inc(sem("l3_tab" if w == 0 else "l3_ready"), 1)

                def clamp(kind, n, buf):
                    dve.wait_ge(sem(f"l3{kind}_exp"), n + 1)
                    ts(buf, buf, CLAMP, None, ALU.min).then_inc(sem(f"l3{kind}_min"), 1)

                def finish(kind, n, buf, x, hi, lo, used, count):
                    dve.wait_ge(sem(f"l3{kind}_q"), n + 1)
                    stt(buf, buf, 1.0, x, ALU.subtract, ALU.mult, reverse0=True).then_inc(sem(f"l3{kind}_y"), 1)
                    if count is not None:
                        dve.wait_ge(sem(used), count)
                    dve.wait_ge(sem(f"l3{kind}_y"), n + 1)
                    cp(hi, buf).then_inc(sem(f"l3{kind}_hi"), 1)
                    dve.wait_ge(sem(f"l3{kind}_hi"), n + 1)
                    tt(lo, buf, f(hi), ALU.subtract).then_inc(sem(f"l3{kind}_lo"), 1)

                fl = lambda a: a.rearrange("p a b -> p (a b)")

                def hidden(g, b, m2, wait):
                    finish("a", g * 2 + m2, fl(UA[m2]), bank(2 * m2, 2), fl(HT[:, b, 0, 2 * m2:2 * m2 + 2]),
                           fl(HT[:, b, 1, 2 * m2:2 * m2 + 2]), "l3b_ps", g * 2 - 2 if wait else None)

                def message(g, half_, wait):
                    n = g * 2 + half_
                    finish("b", n, fl(UB), bank(4, 2), MSG[:, half_, 0], MSG[:, half_, 1],
                           "l3_scat", n - 1 if wait else None)

                def body(g, p, a, b, nxt):
                    early = isinstance(g, int) and g < 2
                    if a:
                        clamp("a", g * 2, fl(UA[0]))
                        if nxt:
                            onehots(g + 1, 1 - p, not (isinstance(g, int) and g == 0))
                        hidden(g, p, 0, not early)
                    if b:
                        clamp("b", g * 2 - 2, fl(UB))
                        message(g - 1, 0, not early)
                    if a:
                        clamp("a", g * 2 + 1, fl(UA[1]))
                        onehots_E(g, p, not early)
                        hidden(g, p, 1, not early)
                    if b:
                        clamp("b", g * 2 - 1, fl(UB))
                        message(g - 1, 1, not early)
                body(0, 0, True, False, True)
                body(1, 1, True, True, True)
                with dve.Fori(1, NG // 2 - 1) as i:
                    body(i * 2, 0, True, True, True)
                    body(i * 2 + 1, 1, True, True, True)
                body(NG - 2, 0, True, True, True)
                body(NG - 1, 1, True, True, False)
                body(NG, 0, False, True, False)
                dve.wait_ge(sem("l3_scat"), 2 * NG)
                for h in range(NH):
                    last = cp(agg3[:, h], bank(6 + h))
                last.then_inc(sem("l3_agg"), 1)
                dve.wait_ge(sem("l3_u_ps"), 1)
                dve.wait_ge(sem("in_l3_vectors"), 64)
                for h in range(NH):
                    last = tt(UA[0][:, h], bank(h), V[:, 0], ALU.add)
                last.then_inc(sem("l3_u_in"), 1)
                dve.wait_ge(sem("l3_u_exp"), 1)
                ts(fl(UA[1]), fl(UA[1]), CLAMP, None, ALU.min).then_inc(sem("l3_u_min"), 1)
                dve.wait_ge(sem("l3_u_q"), 1)
                stt(fl(UA[0]), fl(UA[1]), 1.0, fl(UA[0]), ALU.subtract, ALU.mult,
                    reverse0=True).then_inc(sem("l3_u"), 1)
                dve.wait_ge(sem("l3_out_ps"), 1)
                for h in range(NH):
                    chain(tt(UA[1][:, h], bank(5 + h), V[:, 1], ALU.add))
                chain(tt(UA[1], UA[1], Hn[:], ALU.add))
                affine_norm("n3o", UA[1], V[:, 2], V[:, 3]).then_inc(sem("x_done"), 1)


_INS = {
    "x": lambda a: a["x"].reshape(NH, P, C).transpose(1, 0, 2),
    "idx_cols": lambda a: np.stack([a["src"].reshape(T, P).T, a["dst"].reshape(T, P).T], 1),
    "idx_rows": lambda a: np.stack([a["src"], a["dst"]]),
    "type_rows": lambda a: np.broadcast_to(a["edge_type_8"], (HD, E)),
    "ew": lambda a: a["edge_weight"].reshape(T, P).T,
    "ea3": lambda a: a["edge_attr_3"].reshape(T, P, 3).transpose(1, 0, 2),
    "ea20T": lambda a: a["edge_attr_20"].T,
    "ea64T": lambda a: a["edge_attr_64"].T,
    "L0_WT": lambda a: a["L0_gnn_W"].T.reshape(KC, P, C).transpose(1, 0, 2),
    "L0_b": lambda a: a["L0_gnn_b"],
    "L1_WT": lambda a: a["L1_gnn_W"].T.reshape(KC, P, C).transpose(1, 0, 2),
    "a_src": lambda a: a["L1_gnn_a_src"].reshape(C),
    "a_dst": lambda a: a["L1_gnn_a_dst"].reshape(C),
    "emb": lambda a: a["L1_gnn_et_emb"],
    "L1_gamma": lambda a: a["L1_gnn_ln_gamma"],
    "L1_beta": lambda a: a["L1_gnn_ln_beta"],
    "Win": lambda a: np.stack([a["L2_gnn_W_in2f_s"], a["L2_gnn_W_in2f_v"]], 1),
    "Wf1": lambda a: a["L2_gnn_Wf1"],
    "bf1": lambda a: a["L2_gnn_bf1"].reshape(F, 1),
    "Wf2": lambda a: a["L2_gnn_Wf2"].reshape(F, 3, F, 2).transpose(0, 1, 3, 2).reshape(F, 6 * F),
    "bf2": lambda a: a["L2_gnn_bf2"].reshape(3, F, 2).transpose(0, 2, 1).reshape(1, 6 * F),
    "W1sv": lambda a: np.stack([a["L2_gnn_W1_s"], a["L2_gnn_W1_v"]]).reshape(2, F, 2, F).transpose(1, 0, 2, 3),
    "W2sv": lambda a: np.stack([a["L2_gnn_W2_s"], a["L2_gnn_W2_v"]], 1),
    "L3_W1ab": lambda a: a["L3_gnn_W1"][0:2 * C].reshape(2 * KC, P, C).transpose(1, 0, 2),
    "W1c": lambda a: a["L3_gnn_W1"][2 * C:],
    "L3_b1": lambda a: a["L3_gnn_b1"].reshape(1, C),
    "L3_W2": lambda a: a["L3_gnn_W2"].reshape(KC, P, C).transpose(1, 0, 2),
    "L3_b2": lambda a: a["L3_gnn_b2"].reshape(1, C),
    "L3_W3": lambda a: a["L3_gnn_W3"].reshape(2 * KC, P, C).transpose(1, 0, 2),
    "L3_b3": lambda a: a["L3_gnn_b3"],
    "L3_W4": lambda a: a["L3_gnn_W4"].reshape(KC, P, C).transpose(1, 0, 2),
    "L3_b4": lambda a: a["L3_gnn_b4"],
    "L3_gamma": lambda a: a["L3_gnn_gamma"],
    "L3_beta": lambda a: a["L3_gnn_beta"],
}


def kernel(**inputs):
    import concourse.bacc as _bacc
    from concourse.bass_utils import run_bass_kernel_spmd as _run

    nc = _bacc.Bacc("TRN2", target_bir_lowering=False, num_devices=1)
    given = {k: np.asarray(v) for k, v in inputs.items()}
    arrays, aps = {}, {}
    for name, layout in _INS.items():
        a = np.ascontiguousarray(layout(given))
        arrays["in_" + name] = a
        aps[name] = nc.dram_tensor("in_" + name, a.shape, mybir.dt.from_np(a.dtype), kind="ExternalInput").ap()
    out = nc.dram_tensor("out_x", (P, NH, C), F32, kind="ExternalOutput").ap()
    gnn_stack(nc, aps, out)
    r = _run(nc, [arrays], core_ids=[0])
    return np.ascontiguousarray(r.results[0]["out_x"].transpose(1, 0, 2).reshape(N, C))
```

```python
from contextlib import ExitStack

import numpy as np

import concourse.bass as bass
from concourse import mybir

F32 = mybir.dt.float32
F32R = mybir.dt.float32r
BF16 = mybir.dt.bfloat16
I32 = mybir.dt.int32
U8 = mybir.dt.uint8
ALU = mybir.AluOpType
ACT = mybir.ActivationFunctionType
AX = mybir.AxisListType.X

P = 128
N = 256
NH = N // P
E = 8192
C = 512
KC = C // P
T = E // P
G = 4
GE = G * P
NG = T // G
HD = 8
F = 128
RBF = 20
ED = 64
LN_EPS = 1e-5
LOG2 = float(np.log(2.0))
Y0 = float(1.0 / np.sqrt(4.0 * np.pi))
Y1 = float(np.sqrt(3.0 / (4.0 * np.pi)))
BANK = 512
CLAMP = 2.0 ** 30
CE = 1024
NCH = E // CE
DIGIT = 8
NDIG = 32 // DIGIT
NQ = 16
QT = 16
NB = T // QT
PART = 32


def gnn_stack(nc, d, out, layers=4):
    with ExitStack() as ctx:
        sems = {}

        def sem(name):
            if name not in sems:
                sems[name] = ctx.enter_context(nc.semaphore(name))
            return sems[name]

        def sb(name, shape, dt=F32):
            return ctx.enter_context(nc.sbuf_tensor(name, shape, dt))

        def under(name, words):
            with nc.sbuf_tensor(name, [P, 2 * words], BF16) as t:
                return t

        PS = ctx.enter_context(nc.psum_tensor("PS", [P, 8 * BANK], F32))

        def bank(k, n=1):
            return PS[:, k * BANK:(k + n) * BANK]

        node_row = sb("node_row", [P, N])
        node_col = sb("node_col", [P, NH])
        ident = sb("ident", [P, P])
        src_row = sb("src_row", [P, E], U8)
        dst_row = sb("dst_row", [P, E], U8)
        src_col = sb("src_col", [P, T])
        dst_col = sb("dst_col", [P, T])
        idx_raw = sb("idx_raw", [P, 2, T], I32)
        ew = sb("ew", [P, T])
        X = sb("X", [P, NH, C])
        Hn = sb("Hn", [P, NH, C])
        WN = sb("WN", [P, KC, C])
        LW = sb("LW", [P, 8, C])
        V = sb("V", [P, 4, C])
        U = sb("U", [P, 3584])
        stats = sb("stats", [P, NH, 6])
        mv = sb("mv", [P, NH, 2])
        one_col = sb("one_col", [P, 1])
        nt = sb("nt", [P, 2, NH, HD])
        rs = sb("rs", [P, 4, NH])
        ST_16 = under("ST_16", 2 * NH * GE)
        ST = sb("ST", [P, 2, NH, GE], F32R)
        DT_16 = under("DT_16", 2 * NH * GE)
        DT = sb("DT", [P, 2, NH, GE], F32R)
        EN_16 = under("EN_16", 2 * G * N)
        EN = sb("EN", [P, 2, G, N], F32R)
        TAB_16 = under("TAB_16", 4 * NH * C)
        TAB = sb("TAB", [P, 2, 2, NH, C], F32R)
        MSG_16 = under("MSG_16", 4 * 1024)
        MSG = sb("MSG", [P, 2, 2, 1024], F32R)
        HT_16 = under("HT_16", 4 * KC * GE)
        HT = sb("HT", [P, 2, 2, KC, GE], F32R)
        WF2 = sb("WF2", [P, 2, C], F32R)
        BF2 = sb("BF2", [64, C], F32R)
        W2S = sb("W2S", [P, 2, KC, C], F32R)
        B2S = sb("B2S", [64, C], F32R)
        WEA = sb("WEA", [P, 2, C], F32R)
        EA = sb("EA", [P, 2, GE], F32R)
        EB_16 = under("EB_16", 2 * GE)
        EB = sb("EB", [P, 2, GE], F32R)
        ones = sb("ones", [64, P], F32R)
        L = sb("L", [P, T, HD])
        NT = sb("NT", [P, 2, NH, 3, HD], BF16)
        MX = sb("MX", [P, NH, 3, HD], BF16)
        part = sb("part", [P, NH * HD])
        dig = sb("dig", [P, NDIG, NH, HD])
        digI = sb("digI", [P, NDIG, NH, HD], I32)
        dig16 = sb("dig16", [P, NH, HD], BF16)
        EMB = sb("EMB", [HD, 3, HD], BF16)
        emb = sb("emb", [HD, HD])
        node_row16 = sb("node_row16", [P, N], BF16)
        upper = sb("upper", [P, NQ, HD])
        upper16 = sb("upper16", [P, NQ, HD], BF16)
        Yv = sb("Yv", [P, T, 3])
        fT = LW[0:RBF, 2:4]
        Wf1 = sb("Wf1", [RBF, F])
        bf1 = sb("bf1", [P, 1])
        Win = sb("Win", [P, 2, F])
        W1sv = sb("W1sv", [P, 2, 2, F])
        W2sv = sb("W2sv", [P, 2, F])
        ea_raw = L[:].rearrange("p a b -> p (a b)")

        block = ctx.enter_context(nc.Block())

        def u(off, *shape):
            n = int(np.prod(shape))
            a = U[:, off:off + n]
            if len(shape) == 2:
                a = a.rearrange("p (a b) -> p a b", a=shape[0])
            if len(shape) == 3:
                a = a.rearrange("p (a b c) -> p a b c", a=shape[0], b=shape[1])
            return a

        f = lambda ap: ap.bitcast(F32)

        def flat(t):
            names = "abcd"[:len(t.shape) - 1]
            return t[:].rearrange(f"p {' '.join(names)} -> p ({' '.join(names)})")


        EN16 = HT_16[:].rearrange("p (t n) -> p t n", t=T)
        DT16 = [MSG_16, flat(LW).bitcast(BF16)]
        ST16 = ST_16[:].rearrange("p (s h e) -> p s h e", s=2, h=NH)
        T8 = EB_16[0:HD].rearrange("p (s e) -> p s e", s=2)
        P24 = TAB_16[:, 4 * NH * C:4 * NH * C + 3 * T * HD].rearrange(
            "p (t w h) -> p t w h", t=T, w=3)
        l0_on = U[:, 0:512].bitcast(BF16).rearrange("p (s n) -> p s n", s=4)[:, 0:2]
        adjT = u(512, NH, N)
        dis = u(1024, NH)
        hW = u(1032, NH, C)
        hT = u(2056, KC, N)
        l1_t = u(2056, NH, C)
        typ = u(0, 2, CE)[0:HD].bitcast(I32)
        l1_em = u(0, T, HD)
        v_bits = u(512, T * HD)
        active = u(1024, T, HD)
        d_bits = u(1536, T * HD)
        d_bits2 = V[:, 3]
        w_bits = u(2048, T * HD)
        g_bits = u(2560, T * HD)
        g16 = u(3072, 256).bitcast(BF16).rearrange("p (t h) -> p t h", t=T)
        w16 = u(3328, 256).bitcast(BF16).rearrange("p (t h) -> p t h", t=T)
        batch = lambda a: a.rearrange("p (k t q h) -> p k t q h", k=2, t=QT, q=NQ)
        masks = [batch(t[:])[:, k] for t in (ST_16, DT_16) for k in range(2)]
        digits = [batch(t)[:, k] for t in (EN_16[:], flat(WN).bitcast(BF16)) for k in range(2)]
        S_a, S_b = u(0, NH, NQ * HD), u(256, NH, NQ * HD)
        l1_m = u(0, 2, C)
        l2_m = u(0, 2, 9, F)
        l2_w = u(2304, 2, 4, F)
        l2_s = [WN[:, k, :] for k in range(4)]
        UA = [u(0, 2, C), u(1024, 2, C)]
        l3_buf = {"a": [u(m * GE, GE) for m in range(G)], "b": [u(2048 + k * C, C) for k in range(2)]}
        l2_tab = [u(0, NH, C)[:, h] for h in range(NH)]
        l2_agg = u(0, NH, 8, F)
        aggT = WN[:].rearrange("p a b -> p (a b)").rearrange("p (a b) -> p a b", a=8)
        SV = u(2048, 4, N)
        s2 = u(3072, 2, N)
        agg3 = u(0, NH, C)
        h3T = u(1024, KC, N)
        r_y, r_v, r_sq = u(3090, T), u(3090 + T, T), u(3090 + 2 * T, T, 3)

        RSQRT = ("n0", "r2", "deg", "n1", "n1o", "n2", "n3", "n3o")
        NORMS = ("n0", "n1", "n2", "n3")
        TURNS = ("n0", "n1", "n2", "n3", "n3b", "n3a", "n3u")

        LAG = 5

        def l3_tile(g, m):
            n = g * G + m - LAG
            if isinstance(g, int) and not 0 <= n < T:
                return None
            return n, (m - LAG) % G

        def l3_units(g, steps, a):
            for m in range(steps):
                if a:
                    yield "a", g * G + m, m
                if l3_tile(g, m) is not None:
                    yield ("b",) + l3_tile(g, m)

        class Chain:

            def __init__(self, eng, name):
                self.eng, self.sem, self.n = eng, sem(name), 0

            def __call__(self, ins):
                self.n += 1
                ins.then_inc(self.sem, 1)
                self.eng.wait_ge(self.sem, self.n)

        def load(eng, dst, src, name):
            eng.dma_start(dst, src).then_inc(sem("in_" + name), 16)

        def row(ap):
            return ap.partition_broadcast(P)

        @block.sync
        def _(sp):
            load(sp, X[:], d["x"], "x")
            load(sp, idx_raw[:], d["idx_cols"], "idx")
            load(sp, WN[:], d["L0_WT"], "L0_W")
            load(sp, V[:, 0], row(d["L0_b"]), "L0_b")
            load(sp, ew[:], d["ew"], "ew")
            if layers > 2:
                load(sp, Yv[:], d["ea3"], "ea3")
            if layers > 1:
                load(sp, V[:, 1], row(d["a_src"]), "l1_vectors")
            if layers > 1:
                load(sp, V[:, 2], row(d["a_dst"]), "l1_vectors")
            if layers > 1:
                load(sp, emb[:], d["emb"], "l1_vectors")
            if layers > 2:
                load(sp, Win[:], d["Win"], "l2_weights")
            if layers > 2:
                load(sp, Wf1[:], d["Wf1"], "l2_weights")
            if layers > 2:
                load(sp, bf1[:], d["bf1"], "l2_weights")
            if layers > 2:
                load(sp, W1sv[:], d["W1sv"], "l2_weights")
            if layers > 2:
                load(sp, W2sv[:], d["W2sv"], "l2_weights")
            for k in range(4):
                if k:
                    sp.wait_ge(sem("rows_cast"), k)
                load(sp, LW[:].rearrange("p a b -> p (a b)").bitcast(I32),
                     row(d["idx_rows"][k // 2, (k % 2) * (E // 2):(k % 2 + 1) * (E // 2)]), "rows")
            sp.wait_ge(sem("l0_hW_ps"), 1)
            if layers > 1:
                load(sp, WN[:], d["L1_WT"], "L1_W")
            if layers > 1:
                sp.wait_ge(sem("x_done"), 1)
                def types(i, b, wait):
                    c = i * 2 + b
                    if wait:
                        sp.wait_ge(sem("l1a_onehots"), c - 1)
                    sp.dma_start(typ[:, b], d["type_rows"][:, bass.ds(c * CE, CE)]).then_inc(sem(f"in_type{b}"), 16)
                types(0, 0, False)
                types(0, 1, False)
                with sp.Fori(1, NCH // 2) as i:
                    types(i, 0, True)
                    types(i, 1, True)
                sp.wait_ge(sem("l1_esd"), 1)
                load(sp, V[:, 1], row(d["L1_gamma"]), "l1_affine")
                load(sp, V[:, 2], row(d["L1_beta"]), "l1_affine")
            if layers > 2:
                sp.wait_ge(sem("rows_cast"), 4)
                sp.wait_ge(sem("l1_mg_ps"), 1)
                load(sp, LW[:, 0], d["Wf2"][:, 0:4 * F], "l2_filter")
                load(sp, LW[0:1, 1], d["bf2"][:, 0:4 * F], "l2_filter")
                load(sp, LW[32:33, 1], d["bf2"][:, 0:4 * F], "l2_filter")

                def rbf(i, b, wait):
                    g = i * 2 + b
                    if wait:
                        sp.wait_ge(sem("l2_h_ps"), g - 1)
                    sp.dma_start(fT[:, b], d["ea20T"][:, bass.ds(g * GE, GE)]).then_inc(sem(f"in_rbf{b}"), 16)
                rbf(0, 0, False)
                rbf(0, 1, False)
                with sp.Fori(1, NG // 2) as i:
                    rbf(i, 0, True)
                    rbf(i, 1, True)
            if layers > 3:
                sp.wait_ge(sem("l2_wsplit"), 1)
                sp.wait_ge(sem("l2_h_ps"), NG)
                load(sp, LW[:], d["L3_W1ab"], "L3_W1ab")
                sp.wait_ge(sem("l1_out"), 1)
                load(sp, V[:, 0], row(d["L3_b3"]), "l3_vectors")
                load(sp, V[:, 1], row(d["L3_b4"]), "l3_vectors")
                load(sp, V[:, 2], row(d["L3_gamma"]), "l3_vectors")
                load(sp, V[:, 3], row(d["L3_beta"]), "l3_vectors")
                sp.wait_ge(sem("l2_out"), 1)
                load(sp, WN[:], d["L3_W2"], "L3_W2")
                for r in range(2):
                    load(sp, u(0, 3, C)[64 * r:64 * r + 64, 0], d["W1c"], "l3_edge_weights")
                for r in (64, 96):
                    load(sp, u(0, 3, C)[r:r + 1, 1], d["L3_b1"], "l3_edge_weights")
                for r in (0, 32):
                    load(sp, u(0, 3, C)[r:r + 1, 2], d["L3_b2"], "l3_edge_weights")

                def feats(g, wait):
                    if wait:
                        sp.wait_ge(sem("l3_ea"), g)
                    for r in range(2):
                        sp.dma_start(ea_raw[64 * r:64 * r + 64, :],
                                     d["ea64T"][:, bass.ds(g * GE, GE)]).then_inc(sem("in_ea"), 16)
                feats(0, False)
                with sp.Fori(1, NG) as g:
                    feats(g, True)
                sp.wait_ge(sem("l3_w2split"), 1)
                load(sp, WN[:], d["L3_W4"], "L3_W4")
                sp.wait_ge(sem("l3_tab_ps"), 2)
                load(sp, LW[:], d["L3_W3"], "L3_W3")
            sp.wait_ge(sem("x_done"), layers)
            sp.dma_start(out, X[:]).then_inc(sem("out"), 16)
            sp.wait_ge(sem("out"), 16)

        @block.gpsimd
        def _(pool):
            pool.iota(node_row[:], [[1, N]], base=0, channel_multiplier=0,
                      allow_small_or_imprecise_dtypes=True).then_inc(sem("iotas"), 1)
            pool.iota(node_col[:], [[P, NH]], base=0, channel_multiplier=1,
                      allow_small_or_imprecise_dtypes=True).then_inc(sem("iotas"), 1)
            pool.iota(upper[:], [[1, NQ], [0, HD]], base=0, channel_multiplier=0,
                      allow_small_or_imprecise_dtypes=True).then_inc(sem("iotas"), 1)

        @block.scalar
        def _(act):
            chain = Chain(act, "act_chain")
            act.preload_act_table_set("natural_log_exp_and_others")

            def rsqrt_guess(tag, v, y):
                act.wait_ge(sem("rsqrt_v"), RSQRT.index(tag) + 1)
                chain(act.activation(y, v, ACT.Ln))
                act.activation(y, y, ACT.Exp, scale=-0.5).then_inc(sem("rsqrt_y"), 1)

            def norm(tag):
                rsqrt_guess(tag, rs[:, 0], rs[:, 1])

            def transposed(tag, k0, dst):
                for q in range(2):
                    act.wait_ge(sem("turned_ps"), 2 * TURNS.index(tag) + q + 1)
                    act.activation(dst[:, 2 * q:2 * q + 2, :].rearrange("p a b -> p (a b)"), bank(k0 + q),
                                   ACT.Copy).then_inc(sem("turned"), 1)

            norm("n0")
            transposed("n0", 3, hT)
            if layers > 2:
                rsqrt_guess("r2", r_v, r_y)
            for k in range(4):
                act.wait_ge(sem("in_rows"), 16 * (k + 1))
                rows = (src_row, dst_row)[k // 2]
                act.activation(rows[:, (k % 2) * (E // 2):(k % 2 + 1) * (E // 2)],
                               LW[:].rearrange("p a b -> p (a b)").bitcast(I32), ACT.Copy).then_inc(sem("rows_cast"), 1)
            rsqrt_guess("deg", rs[:, 0], rs[:, 1])
            if layers > 1:
                norm("n1")
                transposed("n1", 3, hT)

                act.wait_ge(sem("l1_shift"), 1)
                act.activation(L[:], L[:], ACT.Exp).then_inc(sem("l1_p"), 1)

                def onehots_E(g, b, free):
                    if free:
                        act.wait_ge(sem("l1_scat"), g * G - G)
                    act.activation(EN[:, b].rearrange("p a b -> p (a b)"),
                                   EN16[:, bass.ds(g * G, G)].rearrange("p a b -> p (a b)"),
                                   ACT.Copy).then_inc(sem("l1_en"), 1)

                def tile(t, q, free):
                    act.wait_ge(sem("l1_msg"), t + 1)
                    if free:
                        act.wait_ge(sem("l1_scat"), t - 1)
                    act.activation(MSG[:, q, 0, 0:C], l1_m[:, q], ACT.Copy).then_inc(sem("l1_hi"), 1)

                def group(i, b, first, last):
                    g = i * 2 + b
                    for j in range(G):
                        tile(g * G + j, j % 2, not (first and b == 0 and j < 2))
                        if j == 1 and not (last and b == 1):
                            onehots_E(g + 1, 1 - b, not (first and b == 0))
                act.wait_ge(sem("l1_mg_ps"), 1)
                onehots_E(0, 0, False)
                group(0, 0, True, False)
                group(0, 1, False, False)
                with act.Fori(1, NG // 2 - 1) as i:
                    group(i, 0, False, False)
                    group(i, 1, False, False)
                group(NG // 2 - 1, 0, False, False)
                group(NG // 2 - 1, 1, False, True)
                norm("n1o")
            if layers > 2:
                norm("n2")
                for k in range(NH):
                    act.wait_ge(sem("turned_ps"), 2 * TURNS.index("n2") + k + 1)
                    act.activation(hT[:, :, k * P:(k + 1) * P], bank(3 + k).rearrange("p (a b) -> p a b", a=4),
                                   ACT.Copy).then_inc(sem("turned"), 1)
                for k in range(NH):
                    act.wait_ge(sem("l2_tab_ps"), k + 1)
                    act.activation(l2_tab[k], bank(5 + k), ACT.Copy,
                                   scale=float(1.0 / np.sqrt(F))).then_inc(sem("l2_tab"), 1)

                def filt(g):
                    act.wait_ge(sem("l2_h_ps"), g + 1)
                    if not (isinstance(g, int) and g == 0):
                        act.wait_ge(sem("l2_ssp"), g)
                    act.activation(l2_s[0], bank(7), ACT.Abs, bias=bf1[:, 0:1]).then_inc(sem("l2_abs"), 1)
                    act.activation(l2_s[1], bank(7), ACT.Relu, bias=bf1[:, 0:1])
                    act.wait_ge(sem("l2_abs"), g + 1)
                    act.activation(l2_s[0], l2_s[0], ACT.Exp, scale=-1.0).then_inc(sem("l2_exp"), 1)
                    act.wait_ge(sem("l2_exp"), g + 1)
                    act.activation(l2_s[0], l2_s[0], ACT.Ln, bias=1.0).then_inc(sem("l2_ln"), 1)

                def weights(t, q, free):
                    act.wait_ge(sem("l2_w_ps"), t + 1)
                    if free:
                        act.wait_ge(sem("l2_msg"), t - 1)
                    act.activation(l2_w[:, q].rearrange("p a b -> p (a b)"), bank(6), ACT.Copy,
                                   scale=ew[:, bass.ds(t, 1)]).then_inc(sem("l2_w"), 1)

                def high(t, q, free):
                    act.wait_ge(sem("l2_msg"), t + 1)
                    act.wait_ge(sem("l2_outer"), t + 1)
                    if free:
                        act.wait_ge(sem("l2_scat"), t - 1)
                    act.activation(MSG[:, q, 0], l2_m[:, q, 0:8].rearrange("p a b -> p (a b)"),
                                   ACT.Copy).then_inc(sem("l2_hi"), 1)

                def outer(t, q, free):
                    act.wait_ge(sem("l2_sW"), t + 1)
                    if free:
                        act.wait_ge(sem("l2_lo"), t - 1)
                    for k in range(3):
                        last = act.activation(l2_m[:, q, 2 + k], l2_m[:, q, 8], ACT.Copy,
                                              scale=Yv[:, bass.ds(t, 1), k])
                    last.then_inc(sem("l2_outer"), 1)

                def group(i, b, first, last):
                    g = i * 2 + b
                    for j in range(G):
                        t = g * G + j
                        start = first and b == 0
                        end = last and b == 1
                        if not (end and j == G - 1):
                            weights(t + 1, (j + 1) % 2, not (start and j == 0))
                        outer(t, j % 2, not (start and j < 2))
                        high(t, j % 2, not (start and j < 2))
                        if j == 0 and not end:
                            filt(g + 1)
                act.wait_ge(sem("in_l2_weights"), 80)
                filt(0)
                weights(0, 0, False)
                group(0, 0, True, False)
                group(0, 1, False, False)
                with act.Fori(1, NG // 2 - 1) as i:
                    group(i, 0, False, False)
                    group(i, 1, False, False)
                group(NG // 2 - 1, 0, False, False)
                group(NG // 2 - 1, 1, False, True)
                act.wait_ge(sem("l2_S_ps"), 1)
                chain(act.activation(s2[:, 0], bank(4)[:, 0:N], ACT.Abs))
                act.activation(s2[:, 1], bank(4)[:, 0:N], ACT.Relu)
                chain(act.activation(s2[:, 0], s2[:, 0], ACT.Exp, scale=-1.0))
                act.activation(s2[:, 0], s2[:, 0], ACT.Ln, bias=1.0).then_inc(sem("l2_S_ln"), 1)
            if layers > 3:
                norm("n3")
                transposed("n3", 3, hT)

                def buffer(kind, j):
                    return l3_buf["a"][j] if kind == "a" else l3_buf["b"][j % 2]

                def start(kind, n, j):
                    act.wait_ge(sem(f"l3{kind}_ps"), n + 1)
                    ring = G if kind == "a" else 2
                    if not (isinstance(n, int) and n < ring):
                        act.wait_ge(sem(f"l3{kind}_lo"), n + 1 - ring)
                    src = bank(j) if kind == "a" else bank(4 + j % 2)
                    act.activation(buffer(kind, j), src, ACT.Exp).then_inc(sem(f"l3{kind}_exp"), 1)

                def square(kind, n, j):
                    act.wait_ge(sem(f"l3{kind}_min"), n + 1)
                    act.activation(buffer(kind, j), buffer(kind, j), ACT.Square,
                                   bias=1.0).then_inc(sem(f"l3{kind}_sq"), 1)

                def log(kind, n, j):
                    act.wait_ge(sem(f"l3{kind}_sq"), n + 1)
                    act.activation(buffer(kind, j), buffer(kind, j), ACT.Ln, bias=0.5,
                                   scale=0.5).then_inc(sem(f"l3{kind}_ln"), 1)

                def quotient(kind, n, j):
                    act.wait_ge(sem(f"l3{kind}_ln"), n + 1)
                    act.activation(buffer(kind, j), buffer(kind, j), ACT.Exp,
                                   scale=-1.0).then_inc(sem(f"l3{kind}_q"), 1)

                fl = lambda a: a.rearrange("p a b -> p (a b)")

                def body(g, prev, steps=G, a=True):
                    for unit in l3_units(g, steps, a):
                        start(*unit)
                        if prev:
                            log(*prev)
                        square(*unit)
                        if prev:
                            quotient(*prev)
                        prev = unit
                    return prev
                prev = body(0, None)
                prev = body(1, prev)
                with act.Fori(2, NG) as g:
                    body(g, ("b", g * G - 1 - LAG, (-1 - LAG) % G))
                prev = body(NG, ("b", NG * G - 1 - LAG, (-1 - LAG) % G), steps=LAG, a=False)
                log(*prev)
                quotient(*prev)
                transposed("n3b", 2, h3T)
                transposed("n3a", 4, hT)
                act.wait_ge(sem("l3_u_in"), 1)
                act.activation(fl(UA[1]), fl(UA[0]), ACT.Exp).then_inc(sem("l3_u_exp"), 1)
                act.wait_ge(sem("l3_u_min"), 1)
                chain(act.activation(fl(UA[1]), fl(UA[1]), ACT.Square, bias=1.0))
                chain(act.activation(fl(UA[1]), fl(UA[1]), ACT.Ln, bias=0.5, scale=0.5))
                act.activation(fl(UA[1]), fl(UA[1]), ACT.Exp, scale=-1.0).then_inc(sem("l3_u_q"), 1)
                transposed("n3u", 3, hT)
                norm("n3o")

        @block.tensor
        def _(pe):
            def transpose_nodes(tag, src, k0):
                pe.wait_ge(sem("h_ready"), NORMS.index(tag) + 1)
                for k in range(KC):
                    for h in range(NH):
                        o = bank(k0 + k // 2)[:, (k % 2) * N + h * P:(k % 2) * N + h * P + P]
                        m = pe.transpose(o, src[:, h, k * P:(k + 1) * P], ident[:])
                    if k % 2:
                        m.then_inc(sem("turned_ps"), 1)

            def node_mm(k0, xT, w, nk=KC, w0=0, start=True, stop=True):
                for h in range(NH):
                    for k in range(nk):
                        m = pe.matmul(bank(k0 + h), xT[:, k, h * P:(h + 1) * P], w[:, w0 + k, :],
                                      start=start and k == 0, stop=stop and k == nk - 1)
                return m

            def both(o, lhsT, hi, lo, start, stop, skip=False):
                pe.matmul(o, lhsT, hi, start=start, stop=False, skip_group_check=skip)
                return pe.matmul(o, lhsT, lo, start=False, stop=stop, skip_group_check=skip)

            def count(t, q, start, stop):
                pe.wait_ge(sem("l0_onehots"), t + 1)
                for h in range(NH):
                    m = pe.matmul(bank(h)[:, 0:N], EN16[:, bass.ds(t, 1), h * P:(h + 1) * P].rearrange("p a b -> p (a b)"),
                                  l0_on[:, q],
                                  start=start, stop=stop)
                m.then_inc(sem("l0_count"), 1)
            transpose_nodes("n0", Hn, 3)
            pe.wait_ge(sem("turned"), 2 * TURNS.index("n0") + 2)
            pe.wait_ge(sem("in_L0_W"), 16)
            node_mm(5, hT, WN).then_inc(sem("l0_hW_ps"), 1)
            count(0, 0, True, False)
            count(1, 1, False, False)
            with pe.Fori(1, T // 2 - 1) as i:
                count(i * 2, 0, False, False)
                count(i * 2 + 1, 1, False, False)
            count(T - 2, 0, False, False)
            count(T - 1, 1, False, True)
            pe.wait_ge(sem("l0_adj"), 1)
            for h in range(NH):
                for k in range(NH):
                    m = pe.matmul(bank(2)[:, h:h + 1], adjT[:, k, h * P:(h + 1) * P], one_col[:, 0:1],
                                  start=k == 0, stop=k == NH - 1)
            m.then_inc(sem("l0_deg"), 1)
            pe.wait_ge(sem("l0_hW"), 1)
            for h in range(NH):
                for k in range(NH):
                    m = pe.matmul(bank(h), adjT[:, k, h * P:(h + 1) * P], hW[:, k, :], start=k == 0, stop=k == NH - 1)
            m.then_inc(sem("l0_ps"), 1)
            if layers > 1:
                transpose_nodes("n1", Hn, 3)
                pe.wait_ge(sem("turned"), 2 * TURNS.index("n1") + 2)
                pe.wait_ge(sem("in_L1_W"), 16)
                node_mm(5, hT, WN).then_inc(sem("l1_h_ps"), 1)
                pe.wait_ge(sem("l1_esd"), 1)

                def spot(k, t):
                    return PS[:, bass.ds(k * BANK + t * PART, 3 * HD)]

                fl = lambda a: a.rearrange("p a b -> p (a b)")

                def logits(i, b):
                    c = i * 2 + b
                    pe.wait_ge(sem("l1a_onehots"), c + 1)
                    for j in range(CE // P):
                        t = c * (CE // P) + j
                        for h in range(NH):
                            pe.matmul(spot(0, t), ST16[:, b, h, j * P:(j + 1) * P], fl(NT[:, 0, h]),
                                      start=h == 0, stop=False)
                        for h in range(NH):
                            pe.matmul(spot(0, t), DT16[h][:, bass.ds(t * P, P)], fl(NT[:, 1, h]),
                                      start=False, stop=h == 1)
                        m = pe.matmul(spot(4, t), T8[:, b, j * P:(j + 1) * P], fl(EMB[:]), start=True, stop=True)
                    m.then_inc(sem("l1a_ps"), 1)
                with pe.Fori(0, NCH // 2) as i:
                    logits(i, 0)
                    logits(i, 1)

                def sums(k):
                    for q in range(NB):
                        pe.wait_ge(sem("l1b_digits"), k * NB + q + 1)
                        for j in range(QT):
                            t = q * QT + j
                            for h in range(NH):
                                m = pe.matmul(bank(h)[:, 0:NQ * HD], EN16[:, t, h * P:(h + 1) * P],
                                              fl(digits[q][:, j]), start=t == 0, stop=t == T - 1)
                        m.then_inc(sem("l1b_sum"), 1)
                def to_edges(out, table):
                    for t in range(T):
                        for h in range(NH):
                            m = pe.matmul(out(t), DT16[h][:, t * P:(t + 1) * P], table[:, h], start=h == 0, stop=h == 1)
                    return m
                with pe.Fori(0, NDIG - 1) as k:
                    sums(k)
                    pe.wait_ge(sem("l1b_dig"), k + 1)
                    to_edges(lambda t: bank(2)[:, t * HD:(t + 1) * HD], dig16).then_inc(sem("l1b_match"), 1)
                sums(NDIG - 1)

                pe.wait_ge(sem("l1_mx"), 1)
                to_edges(lambda t: spot(3, t), MX[:].rearrange("p n a b -> p n (a b)")).then_inc(sem("l1_mg_ps"), 1)

                pe.wait_ge(sem("l1_p24"), 1)
                for t in range(T):
                    for h in range(NH):
                        m = pe.matmul(bank(2 + h)[:, 0:3 * HD], EN16[:, t, h * P:(h + 1) * P], fl(P24[:, t]),
                                      start=t == 0, stop=t == T - 1)
                m.then_inc(sem("l1_den"), 1)

                def gather(t, b, j, free):
                    if free:
                        pe.wait_ge(sem("l1_msg"), t - 1)
                    for h in range(NH):
                        m = both(bank(4 + j % 2), ST[:, b, h, j * P:(j + 1) * P], TAB[:, 0, 0, h], TAB[:, 0, 1, h],
                                 h == 0, h == 1)
                    m.then_inc(sem("l1_hs_ps"), 1)

                def scatter(t, g, b, j, start, stop):
                    pe.wait_ge(sem("l1_lo"), t + 1)
                    if j == 0:
                        pe.wait_ge(sem("l1_en"), g + 1)
                    for h in range(NH):
                        m = both(bank(h), EN[:, b, j, h * P:(h + 1) * P], MSG[:, j % 2, 0, 0:C],
                                 MSG[:, j % 2, 1, 0:C], start, stop)
                    m.then_inc(sem("l1_scat"), 1)

                def group(i, b, first, last):
                    g = i * 2 + b
                    for j in range(G):
                        t = g * G + j
                        begin = first and b == 0
                        if j < G - 1:
                            gather(t + 1, b, j + 1, not (begin and j == 0))
                        elif not (last and b == 1):
                            pe.wait_ge(sem("l1_st"), g + 2)
                            gather(t + 1, 1 - b, 0, True)
                        if not (begin and j == 0):
                            scatter(t - 1, g if j else g - 1, b if j else 1 - b, (j - 1) % G, begin and j == 1, False)
                pe.wait_ge(sem("l1_st"), 1)
                gather(0, 0, 0, False)
                group(0, 0, True, False)
                group(0, 1, False, False)
                with pe.Fori(1, NG // 2 - 1) as i:
                    group(i, 0, False, False)
                    group(i, 1, False, False)
                group(NG // 2 - 1, 0, False, False)
                group(NG // 2 - 1, 1, False, True)
                scatter(T - 1, NG - 1, 1, G - 1, False, True)
            if layers > 2:
                pe.wait_ge(sem("h_ready"), NORMS.index("n2") + 1)
                for h in range(NH):
                    for k in range(4):
                        src = Hn[:, h, 0:F] if k == 0 else Hn[:, h, F + k - 1:C:3]
                        m = pe.transpose(bank(3 + h)[:, k * P:(k + 1) * P], src, ident[:])
                    m.then_inc(sem("turned_ps"), 1)
                pe.wait_ge(sem("in_l2_weights"), 80)
                for h in range(NH):
                    pe.wait_ge(sem("turned"), 2 * TURNS.index("n2") + h + 1)
                    for k in range(4):
                        m = pe.matmul(bank(5 + h)[:, k * F:(k + 1) * F], hT[:, k, h * P:(h + 1) * P],
                                      Win[:, min(k, 1)], start=True, stop=True)
                    m.then_inc(sem("l2_tab_ps"), 1)

                def hidden(g, b, free):
                    pe.wait_ge(sem(f"in_rbf{b}"), (g - b) * 8 + 16)
                    if free:
                        pe.wait_ge(sem("l2_ssp"), g)
                    pe.matmul(bank(7), Wf1[:], fT[:, b], start=True, stop=True).then_inc(sem("l2_h_ps"), 1)

                def gather(t, b, j, free):
                    if free:
                        pe.wait_ge(sem("l2_msg"), t - 1)
                    for h in range(NH):
                        m = both(bank(4 + j % 2), DT[:, b, h, j * P:(j + 1) * P], TAB[:, 0, 0, h], TAB[:, 0, 1, h],
                                 h == 0, h == 1)
                    m.then_inc(sem("l2_g_ps"), 1)

                def weights(t, b, j, free):
                    if free:
                        pe.wait_ge(sem("l2_w"), t)
                    s = slice(j * P, (j + 1) * P)
                    pe.matmul(bank(6), HT[:, b, 0, 0, s], WF2[:, 0], start=True, stop=False)
                    pe.matmul(bank(6), HT[:, b, 0, 0, s], WF2[:, 1], start=False, stop=False)
                    pe.matmul(bank(6), HT[:, b, 1, 0, s], WF2[:, 0], start=False, stop=False)
                    pe.matmul(bank(6), ones[:], BF2[:], start=False, stop=True).then_inc(sem("l2_w_ps"), 1)

                def scatter(t, g, b, j, start, stop):
                    pe.wait_ge(sem("l2_lo"), t + 1)
                    if j % 2 == 0:
                        pe.wait_ge(sem("l2_en"), g * 2 + j // 2 + 1)
                    for h in range(NH):
                        for c in range(2):
                            m = both(bank(2 * h + c), EN[:, b, j, h * P:(h + 1) * P],
                                     MSG[:, j % 2, 0, c * C:(c + 1) * C], MSG[:, j % 2, 1, c * C:(c + 1) * C],
                                     start, stop)
                    m.then_inc(sem("l2_scat"), 1)

                def group(i, b, first, last):
                    g = i * 2 + b
                    begin = first and b == 0
                    for j in range(G):
                        t = g * G + j
                        if j == 0 and not (last and b == 1):
                            hidden(g + 1, 1 - b, True)
                        if j < G - 1:
                            weights(t + 1, b, j + 1, True)
                            gather(t + 1, b, j + 1, not (begin and j == 0))
                        elif not (last and b == 1):
                            pe.wait_ge(sem("l2_onehots"), g + 2)
                            pe.wait_ge(sem("l2_hid"), g + 2)
                            weights(t + 1, 1 - b, 0, True)
                            gather(t + 1, 1 - b, 0, True)
                        if not (begin and j == 0):
                            scatter(t - 1, g if j else g - 1, b if j else 1 - b, (j - 1) % G, begin and j == 1, False)
                pe.wait_ge(sem("in_l2_weights"), 80)
                pe.wait_ge(sem("l2_ready"), 1)
                hidden(0, 0, False)
                pe.wait_ge(sem("l2_onehots"), 1)
                pe.wait_ge(sem("l2_hid"), 1)
                weights(0, 0, 0, False)
                gather(0, 0, 0, False)
                group(0, 0, True, False)
                group(0, 1, False, False)
                with pe.Fori(1, NG // 2 - 1) as i:
                    group(i, 0, False, False)
                    group(i, 1, False, False)
                group(NG // 2 - 1, 0, False, False)
                group(NG // 2 - 1, 1, False, True)
                scatter(T - 1, NG - 1, 1, G - 1, False, True)
                for h in range(NH):
                    pe.wait_ge(sem("l2_agg"), h + 1)
                    for k in range(8):
                        m = pe.transpose(bank(4 + k // 2)[:, (k % 2) * N + h * P:(k % 2) * N + h * P + P],
                                         l2_agg[:, h, k], ident[:])
                m.then_inc(sem("l2_aggT_ps"), 1)
                pe.wait_ge(sem("l2_aggT"), 1)
                pe.wait_ge(sem("in_l2_weights"), 80)
                for k in range(2):
                    m = pe.matmul(bank(4)[:, 0:N], W1sv[:, 0, k], aggT[:, k], start=k == 0, stop=k == 1)
                m.then_inc(sem("l2_S_ps"), 1)
                for c in range(3):
                    for k in range(2):
                        m = pe.matmul(bank(5 + c)[:, 0:N], W1sv[:, 1, k], aggT[:, 2 + 3 * k + c],
                                      start=k == 0, stop=k == 1)
                m.then_inc(sem("l2_V_ps"), 1)
                pe.wait_ge(sem("l2_SV"), 1)
                pe.wait_ge(sem("in_l2_weights"), 80)
                for h in range(NH):
                    for k in range(4):
                        m = pe.matmul(bank(h)[:, k * F:(k + 1) * F], SV[:, k, h * P:(h + 1) * P],
                                      W2sv[:, min(k, 1)], start=True, stop=True)
                m.then_inc(sem("l2_ps"), 1)
            if layers > 3:
                transpose_nodes("n3", Hn, 3)
                pe.wait_ge(sem("turned"), 2 * TURNS.index("n3") + 2)
                pe.wait_ge(sem("in_L3_W1ab"), 16)
                node_mm(5, hT, LW).then_inc(sem("l3_tab_ps"), 1)
                pe.wait_ge(sem("l3_tab"), 1)
                node_mm(5, hT, LW, w0=KC).then_inc(sem("l3_tab_ps"), 1)

                def edge_in(g, b, m):
                    n = g * G + m
                    if m == 0:
                        pe.wait_ge(sem("l3_onehots"), g + 1)
                    if not (isinstance(n, int) and n < G):
                        pe.wait_ge(sem("l3a_y"), n + 1 - G)
                    s = slice(m * P, (m + 1) * P)
                    for w, oh in enumerate((ST, DT)):
                        for h in range(NH):
                            for part in range(2):
                                pe.matmul(bank(m), TAB[:, w, part, h, s], oh[:, b, h], start=w + h + part == 0,
                                          stop=False)
                    pe.matmul(bank(m), WEA[:, 0, s], EA[:, b], start=False, stop=False)
                    pe.matmul(bank(m), WEA[:, 1, s], EB[:, b], start=False, stop=True).then_inc(sem("l3a_ps"), 1)

                def edge_hid(n, b, j):
                    if j == 0:
                        pe.wait_ge(sem("l3a_lo"), n + G)
                    if not (isinstance(n, int) and n < 2):
                        pe.wait_ge(sem("l3b_y"), n - 1)
                    o, s = bank(4 + j % 2), slice(j * P, (j + 1) * P)
                    for c in range(KC):
                        pe.matmul(o, HT[:, b, 0, c, s], W2S[:, 0, c], start=c == 0, stop=False)
                        pe.matmul(o, HT[:, b, 0, c, s], W2S[:, 1, c], start=False, stop=False)
                        pe.matmul(o, HT[:, b, 1, c, s], W2S[:, 0, c], start=False, stop=False)
                    pe.matmul(o, ones[:], B2S[:], start=False, stop=True).then_inc(sem("l3b_ps"), 1)

                def scatter(n, b, j):
                    pe.wait_ge(sem("l3b_lo"), n + 1)
                    first, last = isinstance(n, int) and n == 0, isinstance(n, int) and n == T - 1
                    for h in range(NH):
                        s = slice(j % 2 * C, (j % 2 + 1) * C)
                        m = both(bank(6 + h), EN[:, b, j, h * P:(h + 1) * P], MSG[:, j // 2, 0, s],
                                 MSG[:, j // 2, 1, s], first, last)
                    m.then_inc(sem("l3_scat"), 1)

                def body(g, b, steps=G, a=True):
                    for m in range(steps):
                        if a:
                            edge_in(g, b, m)
                        tile = l3_tile(g, m)
                        if tile is not None:
                            edge_hid(tile[0], b if m < LAG - G else 1 - b, tile[1])
                        tile = l3_tile(g, m - 2)
                        if tile is not None:
                            if tile[1] == 0:
                                pe.wait_ge(sem("l3_en"), g)
                            scatter(tile[0], b if m - 2 < LAG - G else 1 - b, tile[1])
                pe.wait_ge(sem("l3_ready"), 1)
                body(0, 0)
                body(1, 1)
                with pe.Fori(1, NG // 2) as i:
                    body(i * 2, 0)
                    body(i * 2 + 1, 1)
                body(NG, 0, steps=LAG + 2, a=False)
                def transpose_any(tag, src, k0):
                    for k in range(KC):
                        for h in range(NH):
                            o = bank(k0 + k // 2)[:, (k % 2) * N + h * P:(k % 2) * N + h * P + P]
                            m = pe.transpose(o, src[:, h, k * P:(k + 1) * P], ident[:])
                        if k % 2:
                            m.then_inc(sem("turned_ps"), 1)
                pe.wait_ge(sem("l3b_lo"), T)
                transpose_any("n3b", Hn, 2)
                pe.wait_ge(sem("l3_agg"), 1)
                transpose_any("n3a", agg3, 4)
                pe.wait_ge(sem("turned"), 2 * TURNS.index("n3b") + 2)
                pe.wait_ge(sem("in_L3_W3"), 16)
                pe.wait_ge(sem("turned"), 2 * TURNS.index("n3a") + 2)
                for h in range(NH):
                    for k in range(2 * KC):
                        xT = h3T if k < KC else hT
                        m = pe.matmul(bank(h), xT[:, k % KC, h * P:(h + 1) * P], LW[:, k, :],
                                      start=k == 0, stop=k == 2 * KC - 1)
                m.then_inc(sem("l3_u_ps"), 1)
                pe.wait_ge(sem("l3_u"), 1)
                transpose_any("n3u", UA[0], 3)
                pe.wait_ge(sem("turned"), 2 * TURNS.index("n3u") + 2)
                pe.wait_ge(sem("in_L3_W4"), 16)
                node_mm(5, hT, WN).then_inc(sem("l3_out_ps"), 1)

        @block.vector
        def _(dve):
            chain = Chain(dve, "dve_chain")
            tt, ts, stt, cp = dve.tensor_tensor, dve.tensor_scalar, dve.scalar_tensor_tensor, dve.tensor_copy

            def split(hi, lo, src):
                chain(cp(hi, src))
                return tt(lo, src, f(hi), ALU.subtract)

            def newton(y, v, t):
                chain(tt(t, y, y, ALU.mult))
                chain(tt(t, t, v, ALU.mult))
                chain(ts(t, t, -0.5, 1.5, ALU.mult, ALU.add))
                chain(tt(y, y, t, ALU.mult))

            def moments(tag, src):
                for h in range(NH):
                    chain(dve.bn_stats(stats[:, h], src[:, h]))
                for h in range(NH):
                    chain(dve.bn_aggr(mv[:, h], stats[:, h]))
                ts(rs[:, 0], mv[:, :, 1], LN_EPS, None, ALU.add).then_inc(sem("rsqrt_v"), 1)
                dve.wait_ge(sem("rsqrt_y"), RSQRT.index(tag) + 1)
                newton(rs[:, 1], rs[:, 0], rs[:, 2])

            def relu_norm(tag):
                moments(tag, X)
                for h in range(NH):
                    chain(ts(Hn[:, h], X[:, h], mv[:, h, 0:1], rs[:, 1, h:h + 1], ALU.subtract, ALU.mult))
                ts(Hn[:], Hn[:], 0.0, None, ALU.max).then_inc(sem("h_ready"), 1)

            def affine_norm(tag, src, gamma, beta):
                moments(tag, src)
                for h in range(NH):
                    chain(ts(src[:, h], src[:, h], mv[:, h, 0:1], rs[:, 1, h:h + 1], ALU.subtract, ALU.mult))
                    chain(tt(src[:, h], src[:, h], gamma, ALU.mult))
                    chain(tt(src[:, h], src[:, h], beta, ALU.add))
                return tt(X[:], X[:], src, ALU.add)

            def onehot_T(dst, row_, b, g):
                for h in range(NH):
                    last = ts(dst[:, b, h], row_[:, bass.ds(g * GE, GE)], node_col[:, h:h + 1], None, ALU.is_equal)
                return last

            def onehot_E(col, b, g, tiles=range(G)):
                for j in tiles:
                    last = ts(EN[:, b, j], node_row[:], col[:, bass.ds(g * G + j, 1)], None, ALU.is_equal)
                return last

            dve.wait_ge(sem("iotas"), 3)
            chain(cp(node_row16[:], node_row[:]))
            chain(cp(upper16[:], upper[:]))
            chain(ts(upper[:], upper[:], float(NQ), 1.0, ALU.mult, ALU.add))
            chain(ts(ident[:], node_row[:, 0:P], node_col[:, 0:1], None, ALU.is_equal))
            chain(dve.memset(one_col[:], 1.0))
            for a, v in ((ones, 1.0), (BF2, 0.0), (B2S, 0.0), (WEA, 0.0), (EB, 1.0)):
                chain(dve.memset(f(a[:]), v))
            dve.wait_ge(sem("in_idx"), 16)
            chain(cp(src_col[:], idx_raw[:, 0]))
            chain(cp(dst_col[:], idx_raw[:, 1]))

            dve.wait_ge(sem("in_x"), 16)
            relu_norm("n0")
            if layers > 2:
                dve.wait_ge(sem("in_ea3"), 16)
                chain(tt(r_sq, Yv[:], Yv[:], ALU.mult))
                dve.tensor_reduce(r_v, r_sq, AX, ALU.add).then_inc(sem("rsqrt_v"), 1)

            def onehots0(t, q, wait):
                if wait:
                    dve.wait_ge(sem("l0_count"), t - 1)
                ts(EN16[:, bass.ds(t, 1)].rearrange("p a b -> p (a b)"), node_row16[:], dst_col[:, bass.ds(t, 1)],
                   None, ALU.is_equal)
                ts(l0_on[:, q], node_row16[:], src_col[:, bass.ds(t, 1)], None,
                   ALU.is_equal).then_inc(sem("l0_onehots"), 1)
            onehots0(0, 0, False)
            onehots0(1, 1, False)
            with dve.Fori(1, T // 2) as i:
                onehots0(i * 2, 0, True)
                onehots0(i * 2 + 1, 1, True)
            dve.wait_ge(sem("l0_count"), T)
            for h in range(NH):
                chain(ts(adjT[:, h], bank(h)[:, 0:N], 1.0, None, ALU.min))
            for h in range(NH):
                s = slice(h * P, (h + 1) * P)
                last = tt(adjT[:, h, s], adjT[:, h, s], ident[:], ALU.max)
            last.then_inc(sem("l0_adj"), 1)
            dve.wait_ge(sem("l0_deg"), 1)
            cp(rs[:, 0], bank(2)[:, 0:NH]).then_inc(sem("rsqrt_v"), 1)
            dve.wait_ge(sem("rsqrt_y"), RSQRT.index("deg") + 1)
            newton(rs[:, 1], rs[:, 0], rs[:, 2])
            chain(cp(dis, rs[:, 1]))
            dve.wait_ge(sem("l0_hW_ps"), 1)
            dve.wait_ge(sem("in_L0_b"), 16)
            for h in range(NH):
                chain(tt(hW[:, h], bank(5 + h), V[:, 0], ALU.add))
                last = ts(hW[:, h], hW[:, h], dis[:, h:h + 1], None, ALU.mult)
            last.then_inc(sem("l0_hW"), 1)
            dve.wait_ge(sem("l0_ps"), 1)
            for h in range(NH):
                last = stt(X[:, h], bank(h), dis[:, h:h + 1], X[:, h], ALU.mult, ALU.add)
            chain(last)
            dve.wait_ge(sem("dve_chain"), chain.n)
            done = ts(rs[:, 3], rs[:, 0], 0.0, None, ALU.mult)
            done.then_inc(sem("x_done"), 1)
            dve.wait_ge(sem("x_done"), 1)
            if layers > 2:
                dve.wait_ge(sem("rsqrt_y"), RSQRT.index("r2") + 1)
                newton(r_y, r_v, r_sq.rearrange("p a b -> p (a b)")[:, 0:T])
                chain(ts(r_y, r_y, Y1, None, ALU.mult))
                chain(tt(Yv[:], Yv[:], r_y.unsqueeze(2).to_broadcast([P, T, 3]), ALU.mult))

            if layers > 1:
                relu_norm("n1")
                dve.wait_ge(sem("l1_h_ps"), 1)
                dve.wait_ge(sem("in_l1_vectors"), 48)
                for h in range(NH):
                    split(TAB[:, 0, 0, h], TAB[:, 0, 1, h], bank(5 + h))
                    for w in range(2):
                        chain(tt(l1_t[:, h], bank(5 + h), V[:, 1 + w], ALU.mult))
                        chain(dve.tensor_reduce(nt[:, w, h], l1_t[:, h].rearrange("p (a b) -> p a b", a=HD), AX, ALU.add))
                def split3(dst, src, rest):
                    chain(cp(dst(0), src))
                    chain(tt(rest, src, dst(0), ALU.subtract))
                    chain(cp(dst(1), rest))
                    chain(tt(rest, rest, dst(1), ALU.subtract))
                    return cp(dst(2), rest)
                for w in range(2):
                    chain(split3(lambda k: NT[:, w, :, k], nt[:, w], part[:].rearrange("p (a b) -> p a b", a=NH)))
                split3(lambda k: EMB[:, k], emb[:], part[0:HD, 0:HD]).then_inc(sem("l1_esd"), 1)

                dve.wait_ge(sem("rows_cast"), 4)

                def onehots1(i, b, wait):
                    c = i * 2 + b
                    if wait:
                        dve.wait_ge(sem("l1a_ps"), c - 1)
                    for h in range(NH):
                        ts(ST16[:, b, h], src_row[:, bass.ds(c * CE, CE)], node_col[:, h:h + 1], None, ALU.is_equal)
                        ts(DT16[h][:, bass.ds(c * CE, CE)], dst_row[:, bass.ds(c * CE, CE)], node_col[:, h:h + 1],
                           None, ALU.is_equal)
                    dve.wait_ge(sem(f"in_type{b}"), i * 16 + 16)
                    ts(T8[:, b], typ[:, b], node_col[0:HD, 0:1], None, ALU.is_equal).then_inc(sem("l1a_onehots"), 1)
                onehots1(0, 0, False)
                onehots1(0, 1, False)
                with dve.Fori(1, NCH // 2) as i:
                    onehots1(i, 0, True)
                    onehots1(i, 1, True)

                def gathered(k):
                    return bank(k, 4).rearrange("p (t w) -> p t w", t=T)[:, :, 0:3 * HD].rearrange(
                        "p t (w h) -> p t h w", w=3)
                dve.wait_ge(sem("l1a_ps"), NCH)
                dve.wait_ge(sem("in_ew"), 16)
                chain(dve.tensor_reduce(L[:], gathered(0), AX, ALU.add))
                chain(dve.tensor_reduce(l1_em, gathered(4), AX, ALU.add))
                chain(stt(L[:], L[:], 0.2, L[:], ALU.mult, ALU.max))
                chain(stt(L[:], l1_em, 1.0, L[:], ALU.add, ALU.mult))
                chain(tt(L[:], L[:], ew[:].unsqueeze(2).to_broadcast([P, T, HD]), ALU.mult))

                chain(ts(v_bits, L[:].rearrange("p a b -> p (a b)"), 0.0, None, ALU.max))
                fl = lambda a: a.rearrange("p a b -> p (a b)")
                vi, wi, gi = (a.bitcast(I32) for a in (v_bits, w_bits, g_bits))
                di = [d_bits.bitcast(I32), d_bits2.bitcast(I32)]

                def halves(k):
                    s = 32 - DIGIT * (k + 1)
                    ts(di[k % 2], vi, s, 2 ** DIGIT - 1, ALU.logical_shift_right, ALU.bitwise_and)
                    ts(gi, vi, s + 4, NQ - 1, ALU.logical_shift_right, ALU.bitwise_and)
                    chain(ts(wi, vi, s, NQ - 1, ALU.logical_shift_right, ALU.bitwise_and))
                    cp(fl(g16), gi)
                    chain(ts(wi, wi, 27, 1 << 23, ALU.logical_shift_left, ALU.bitwise_or))

                def columns():
                    for q in range(NB):
                        g = g16[:, q * QT:(q + 1) * QT].unsqueeze(2).to_broadcast([P, QT, NQ, HD])
                        last = tt(masks[q], g, upper16[:].unsqueeze(1).to_broadcast([P, QT, NQ, HD]), ALU.is_equal)
                    chain(last)

                halves(0)
                columns()
                for k in range(NDIG):
                    w = w_bits.rearrange("p (a b) -> p a b", a=T)
                    if k:
                        dve.wait_ge(sem("l1b_match"), k)
                        if k == 1:
                            chain(tt(fl(active), di[0], bank(2), ALU.is_equal))
                        else:
                            chain(tt(g_bits, di[(k - 1) % 2], bank(2), ALU.is_equal))
                            chain(tt(fl(active), fl(active), g_bits, ALU.mult))
                        chain(tt(w16, w, active, ALU.mult))
                    else:
                        chain(cp(w16, w))
                    for q in range(NB):
                        tt(digits[q], masks[q], w16[:, q * QT:(q + 1) * QT].unsqueeze(2).to_broadcast(
                            [P, QT, NQ, HD]), ALU.mult).then_inc(sem("l1b_digits"), 1)
                    dve.wait_ge(sem("l1b_digits"), (k + 1) * NB)
                    if k + 1 < NDIG:
                        halves(k + 1)
                    dve.wait_ge(sem("l1b_sum"), (k + 1) * NB)
                    sums = bank(0, 2).rearrange("p (n w) -> p n w", n=NH)[:, :, 0:NQ * HD]
                    ts(S_a.bitcast(I32), sums.bitcast(I32), 27, None, ALU.logical_shift_right)
                    chain(stt(S_b, sums, 0.0, upper[:].rearrange("p a b -> p (a b)").unsqueeze(1).to_broadcast(
                        [P, NH, NQ * HD]), ALU.is_gt, ALU.mult))
                    chain(tt(S_b, S_b, S_a.bitcast(I32), ALU.add))
                    chain(dve.tensor_reduce(dig[:, k], S_b.rearrange("p n (q h) -> p n h q", q=NQ), AX, ALU.max))
                    chain(ts(dig[:, k], dig[:, k], -1.0, 0.0, ALU.add, ALU.max))
                    if k + 1 < NDIG:
                        cp(dig16[:], dig[:, k]).then_inc(sem("l1b_dig"), 1)
                        columns()
                chain(cp(digI[:], dig[:]))
                for k in range(1, NDIG):
                    chain(stt(digI[:, 0], digI[:, 0], DIGIT, digI[:, k], ALU.logical_shift_left, ALU.bitwise_or))
                split3(lambda k: MX[:, :, k], f(digI[:, 0]),
                       part[:].rearrange("p (a b) -> p a b", a=NH)).then_inc(sem("l1_mx"), 1)

                dve.wait_ge(sem("l1_mg_ps"), 1)
                chain(dve.tensor_reduce(active, gathered(3), AX, ALU.add))
                tt(L[:], L[:], active, ALU.subtract).then_inc(sem("l1_shift"), 1)
                dve.wait_ge(sem("l1_p"), 1)
                split3(lambda k: P24[:, :, k], L[:], active).then_inc(sem("l1_p24"), 1)

                def onehots_S(g, b, wait):
                    if wait:
                        dve.wait_ge(sem("l1_hs_ps"), g * G - G)
                    onehot_T(ST, src_row, b, g).then_inc(sem("l1_st"), 1)

                def message(t, b, j, wait):
                    q = j % 2
                    dve.wait_ge(sem("l1_hs_ps"), t + 1)
                    if wait:
                        dve.wait_ge(sem("l1_lo"), t - 1)
                    p = L[:, bass.ds(t, 1)].rearrange("p a b -> p (a b)").unsqueeze(2).to_broadcast([P, HD, C // HD])
                    tt(l1_m[:, q].rearrange("p (a b) -> p a b", a=HD), bank(4 + q).rearrange("p (a b) -> p a b", a=HD),
                       p, ALU.mult).then_inc(sem("l1_msg"), 1)

                def low(t, q):
                    dve.wait_ge(sem("l1_hi"), t + 1)
                    tt(MSG[:, q, 1, 0:C], l1_m[:, q], f(MSG[:, q, 0, 0:C]), ALU.subtract).then_inc(sem("l1_lo"), 1)

                def group(i, b, first, last):
                    g = i * 2 + b
                    begin = first and b == 0
                    for j in range(G):
                        t = g * G + j
                        message(t, b, j, not (begin and j < 2))
                        if not (begin and j == 0):
                            low(t - 1, (j - 1) % 2)
                        if last and b == 1:
                            continue
                        if j == 1:
                            onehots_S(g + 1, 1 - b, not begin)
                onehots_S(0, 0, False)
                group(0, 0, True, False)
                group(0, 1, False, False)
                with dve.Fori(1, NG // 2 - 1) as i:
                    group(i, 0, False, False)
                    group(i, 1, False, False)
                group(NG // 2 - 1, 0, False, False)
                group(NG // 2 - 1, 1, False, True)
                low(T - 1, 1)
                dve.wait_ge(sem("l1_scat"), T)
                dve.wait_ge(sem("l1_den"), 1)
                for h in range(NH):
                    chain(dve.tensor_reduce(nt[:, 0, h], bank(2 + h)[:, 0:3 * HD].rearrange("p (w h) -> p h w", w=3),
                                            AX, ALU.add))
                    chain(ts(nt[:, 0, h], nt[:, 0, h], 1e-10, None, ALU.add))
                    chain(dve.reciprocal(nt[:, 0, h], nt[:, 0, h]))
                    chain(tt(l1_t[:, h].rearrange("p (a b) -> p a b", a=HD), bank(h).rearrange("p (a b) -> p a b", a=HD),
                             nt[:, 0, h].unsqueeze(2).to_broadcast([P, HD, C // HD]), ALU.mult))
                chain(tt(l1_t, l1_t, Hn[:], ALU.add))
                dve.wait_ge(sem("in_l1_affine"), 32)
                affine_norm("n1o", l1_t, V[:, 1], V[:, 2]).then_inc(sem("x_done"), 1)
                dve.wait_ge(sem("x_done"), 2)
                ts(rs[:, 3], rs[:, 0], 0.0, None, ALU.mult).then_inc(sem("l1_out"), 1)

            if layers > 2:
                dve.wait_ge(sem("in_l2_filter"), 48)
                split(WF2[:, 0], WF2[:, 1], LW[:, 0])
                chain(cp(BF2[0:1], LW[0:1, 1]))
                chain(cp(BF2[32:33], LW[32:33, 1]))
                tt(BF2[32:33], LW[32:33, 1], f(BF2[32:33]), ALU.subtract).then_inc(sem("l2_wsplit"), 1)
                relu_norm("n2")
                for h in range(NH):
                    dve.wait_ge(sem("l2_tab"), h + 1)
                    last = split(TAB[:, 0, 0, h], TAB[:, 0, 1, h], l2_tab[h])
                last.then_inc(sem("l2_ready"), 1)

                def onehots_T(g, b, wait):
                    if wait:
                        dve.wait_ge(sem("l2_g_ps"), g * G - G)
                    onehot_T(DT, dst_row, b, g).then_inc(sem("l2_onehots"), 1)

                def onehots_E(g, b, half_, wait):
                    if wait:
                        dve.wait_ge(sem("l2_scat"), g * G - G)
                    onehot_E(src_col, b, g, range(2 * half_, 2 * half_ + 2)).then_inc(sem("l2_en"), 1)

                def filt(g, b):
                    dve.wait_ge(sem("l2_ln"), g + 1)
                    stt(l2_s[2], l2_s[1], -LOG2, l2_s[0], ALU.add, ALU.add).then_inc(sem("l2_ssp"), 1)
                    dve.wait_ge(sem("l2_ssp"), g + 1)
                    cp(HT[:, b, 0, 0], l2_s[2]).then_inc(sem("l2_hid_hi"), 1)
                    dve.wait_ge(sem("l2_hid_hi"), g + 1)
                    tt(HT[:, b, 1, 0], l2_s[2], f(HT[:, b, 0, 0]), ALU.subtract).then_inc(sem("l2_hid"), 1)

                def message(t, q, wait):
                    m, w = l2_m[:, q], l2_w[:, q]
                    x = bank(4 + q).rearrange("p (a b) -> p a b", a=4)
                    y = Yv[:, bass.ds(t, 1), :].rearrange("p a b -> p (a b)")
                    dve.wait_ge(sem("l2_g_ps"), t + 1)
                    if wait:
                        dve.wait_ge(sem("l2_lo"), t - 1)
                    ts(m[:, 1], x[:, 1], y[:, 0:1], None, ALU.mult).then_inc(sem("l2_dot"), 1)
                    dve.wait_ge(sem("l2_w"), t + 1)
                    tt(m[:, 0:9:8], x[:, 0:1].to_broadcast([P, 2, F]), w[:, 0:3:2], ALU.mult).then_inc(sem("l2_sW"), 1)
                    dve.wait_ge(sem("l2_dot"), t * 3 + 1)
                    stt(m[:, 1], x[:, 2], y[:, 1:2], m[:, 1], ALU.mult, ALU.add).then_inc(sem("l2_dot"), 1)
                    tt(m[:, 5:8], x[:, 1:4], w[:, 3:4].to_broadcast([P, 3, F]), ALU.mult)
                    dve.wait_ge(sem("l2_dot"), t * 3 + 2)
                    stt(m[:, 1], x[:, 3], y[:, 2:3], m[:, 1], ALU.mult, ALU.add).then_inc(sem("l2_dot"), 1)
                    dve.wait_ge(sem("l2_dot"), t * 3 + 3)
                    tt(m[:, 1], m[:, 1], w[:, 1], ALU.mult).then_inc(sem("l2_msg"), 1)

                def low(t, q):
                    dve.wait_ge(sem("l2_hi"), t + 1)
                    tt(MSG[:, q, 1], l2_m[:, q, 0:8].rearrange("p a b -> p (a b)"), f(MSG[:, q, 0]),
                       ALU.subtract).then_inc(sem("l2_lo"), 1)

                def group(i, b, first, last):
                    g = i * 2 + b
                    begin = first and b == 0
                    for j in range(G):
                        t = g * G + j
                        message(t, j % 2, not (begin and j < 2))
                        if not (begin and j == 0):
                            low(t - 1, (j - 1) % 2)
                        if last and b == 1:
                            continue
                        if j == 0:
                            onehots_T(g + 1, 1 - b, not begin)
                        if j == 1:
                            filt(g + 1, 1 - b)
                        if j >= 2:
                            onehots_E(g + 1, 1 - b, j - 2, not begin)
                onehots_T(0, 0, False)
                filt(0, 0)
                onehots_E(0, 0, 0, False)
                onehots_E(0, 0, 1, False)
                group(0, 0, True, False)
                group(0, 1, False, False)
                with dve.Fori(1, NG // 2 - 1) as i:
                    group(i, 0, False, False)
                    group(i, 1, False, False)
                group(NG // 2 - 1, 0, False, False)
                group(NG // 2 - 1, 1, False, True)
                low(T - 1, 1)
                dve.wait_ge(sem("l2_scat"), T)
                c = 1.0 / float(np.sqrt(2 * F))
                for h in range(NH):
                    a = bank(2 * h, 2).rearrange("p (a b) -> p a b", a=8)
                    for k0, k1, scale in ((0, 1, c * Y0), (1, 2, c / float(np.sqrt(3.0))), (2, 5, c), (5, 8, c * Y0)):
                        last = ts(l2_agg[:, h, k0:k1], a[:, k0:k1], scale, None, ALU.mult)
                    last.then_inc(sem("l2_agg"), 1)
                dve.wait_ge(sem("l2_aggT_ps"), 1)
                cp(aggT.rearrange("p a b -> p (a b)"), bank(4, 4)).then_inc(sem("l2_aggT"), 1)
                dve.wait_ge(sem("l2_V_ps"), 1)
                for k in range(3):
                    cp(SV[:, 1 + k], bank(5 + k)[:, 0:N])
                dve.wait_ge(sem("l2_S_ln"), 1)
                stt(SV[:, 0], s2[:, 1], -LOG2, s2[:, 0], ALU.add, ALU.add).then_inc(sem("l2_SV"), 1)
                dve.wait_ge(sem("l2_ps"), 1)
                c = 1.0 / float(np.sqrt(F))
                for h in range(NH):
                    a = bank(h).rearrange("p (a b) -> p a b", a=4)
                    stt(X[:, h, 0:F], a[:, 0], c, X[:, h, 0:F], ALU.mult, ALU.add)
                    xv = X[:, h, F:C].rearrange("p (f i) -> p i f", i=3)
                    last = stt(xv, a[:, 1:4], c, xv, ALU.mult, ALU.add)
                last.then_inc(sem("x_done"), 1)
                dve.wait_ge(sem("x_done"), 3)
                ts(rs[:, 3], rs[:, 0], 0.0, None, ALU.mult).then_inc(sem("l2_out"), 1)

            if layers > 3:
                relu_norm("n3")
                dve.wait_ge(sem("in_L3_W2"), 16)
                split(W2S[:, 0], W2S[:, 1], WN[:]).then_inc(sem("l3_w2split"), 1)
                dve.wait_ge(sem("in_l3_edge_weights"), 96)
                raw = u(0, 3, C)
                chain(cp(WEA[:, 0], raw[:, 0]))
                chain(tt(WEA[0:64, 1], raw[0:64, 0], f(WEA[0:64, 0]), ALU.subtract))
                chain(cp(WEA[64:65, 1], raw[64:65, 1]))
                chain(cp(WEA[96:97, 1], raw[96:97, 1]))
                chain(tt(WEA[96:97, 1], raw[96:97, 1], f(WEA[96:97, 1]), ALU.subtract))
                chain(cp(B2S[0:1], raw[0:1, 2]))
                chain(cp(B2S[32:33], raw[32:33, 2]))
                chain(tt(B2S[32:33], raw[32:33, 2], f(B2S[32:33]), ALU.subtract))

                def features(g, b):
                    dve.wait_ge(sem("in_ea"), g * 32 + 32)
                    cp(EA[:, b], ea_raw).then_inc(sem("l3_ea_hi"), 1)
                    dve.wait_ge(sem("l3_ea_hi"), g + 1)
                    tt(EA[64:P, b], ea_raw[64:P], f(EA[64:P, b]), ALU.subtract)
                    cp(EB[0:64, b], ea_raw[0:64]).then_inc(sem("l3_ea"), 1)

                def onehots(g, b, wait):
                    if wait:
                        dve.wait_ge(sem("l3a_ps"), g * G - G)
                    features(g, b)
                    onehot_T(ST, src_row, b, g)

                def onehots_D(g, b):
                    onehot_T(DT, dst_row, b, g).then_inc(sem("l3_onehots"), 1)

                def onehots_E(g, b, wait):
                    if wait:
                        dve.wait_ge(sem("l3_scat"), g * G - G)
                    onehot_E(dst_col, b, g).then_inc(sem("l3_en"), 1)
                onehots(0, 0, False)
                onehots_D(0, 0)
                for w in range(2):
                    dve.wait_ge(sem("l3_tab_ps"), w + 1)
                    for h in range(NH):
                        last = split(TAB[:, w, 0, h], TAB[:, w, 1, h], bank(5 + h))
                    last.then_inc(sem("l3_tab" if w == 0 else "l3_ready"), 1)

                def clamp(kind, n, j):
                    buf = l3_buf["a"][j] if kind == "a" else l3_buf["b"][j % 2]
                    dve.wait_ge(sem(f"l3{kind}_exp"), n + 1)
                    ts(buf, buf, CLAMP, None, ALU.min).then_inc(sem(f"l3{kind}_min"), 1)

                def mish(kind, n, j):
                    buf = l3_buf["a"][j] if kind == "a" else l3_buf["b"][j % 2]
                    x = bank(j) if kind == "a" else bank(4 + j % 2)
                    dve.wait_ge(sem(f"l3{kind}_q"), n + 1)
                    stt(buf, buf, 1.0, x, ALU.subtract, ALU.mult, reverse0=True).then_inc(sem(f"l3{kind}_y"), 1)

                def parts(kind, n, j, p):
                    early = isinstance(n, int)
                    if kind == "a":
                        buf, used = l3_buf["a"][j], "l3b_ps"
                        hi, lo = HT[:, p, 0, j], HT[:, p, 1, j]
                        count = None if early and n < 2 * G else n - j - G
                    else:
                        buf, used = l3_buf["b"][j % 2], "l3_scat"
                        s = slice(j % 2 * C, (j % 2 + 1) * C)
                        hi, lo = MSG[:, j // 2, 0, s], MSG[:, j // 2, 1, s]
                        count = None if early and n < G else n + 1 - G
                    if count is not None:
                        dve.wait_ge(sem(used), count)
                    dve.wait_ge(sem(f"l3{kind}_y"), n + 1)
                    cp(hi, buf).then_inc(sem(f"l3{kind}_hi"), 1)
                    dve.wait_ge(sem(f"l3{kind}_hi"), n + 1)
                    tt(lo, buf, f(hi), ALU.subtract).then_inc(sem(f"l3{kind}_lo"), 1)

                fl = lambda a: a.rearrange("p a b -> p (a b)")

                def body(g, p, behind, nxt=True):
                    early = isinstance(g, int) and g < 2
                    for unit in l3_units(g, G, True):
                        old = behind[0] if len(behind) == 2 else None
                        if old:
                            mish(*old[0])
                        clamp(*unit)
                        if old:
                            parts(*old[0], old[1])
                        behind = (behind + ((unit, p),))[-2:]
                        if nxt and unit[0] == "a" and unit[2] == 0:
                            onehots(g + 1, 1 - p, not (isinstance(g, int) and g == 0))
                        if nxt and unit[0] == "a" and unit[2] == 1:
                            onehots_D(g + 1, 1 - p)
                        if unit[0] == "a" and unit[2] == G - 1:
                            onehots_E(g, p, not early)
                    return behind
                before = lambda g, p: ((("a", g * G - 1, G - 1), p), (("b", g * G - 1 - LAG, (-1 - LAG) % G), p))
                behind = body(0, 0, ())
                behind = body(1, 1, behind)
                behind = body(2, 0, behind)
                body(3, 1, behind)
                with dve.Fori(2, NG // 2 - 1) as i:
                    body(i * 2, 0, before(i * 2, 1))
                    body(i * 2 + 1, 1, before(i * 2 + 1, 0))
                body(NG - 2, 0, before(NG - 2, 1))
                body(NG - 1, 1, before(NG - 1, 0), nxt=False)
                (old, p), (prev, _) = before(NG, 1)
                mish(*old)
                parts(*old, p)
                for unit in l3_units(NG, LAG, False):
                    clamp(*unit)
                    mish(*prev)
                    parts(*prev, 0)
                    prev = unit
                mish(*prev)
                parts(*prev, 0)
                dve.wait_ge(sem("l3_scat"), T)
                for h in range(NH):
                    last = cp(agg3[:, h], bank(6 + h))
                last.then_inc(sem("l3_agg"), 1)
                dve.wait_ge(sem("l3_u_ps"), 1)
                dve.wait_ge(sem("in_l3_vectors"), 64)
                for h in range(NH):
                    last = tt(UA[0][:, h], bank(h), V[:, 0], ALU.add)
                last.then_inc(sem("l3_u_in"), 1)
                dve.wait_ge(sem("l3_u_exp"), 1)
                ts(fl(UA[1]), fl(UA[1]), CLAMP, None, ALU.min).then_inc(sem("l3_u_min"), 1)
                dve.wait_ge(sem("l3_u_q"), 1)
                stt(fl(UA[0]), fl(UA[1]), 1.0, fl(UA[0]), ALU.subtract, ALU.mult,
                    reverse0=True).then_inc(sem("l3_u"), 1)
                dve.wait_ge(sem("l3_out_ps"), 1)
                for h in range(NH):
                    chain(tt(UA[1][:, h], bank(5 + h), V[:, 1], ALU.add))
                chain(tt(UA[1], UA[1], Hn[:], ALU.add))
                affine_norm("n3o", UA[1], V[:, 2], V[:, 3]).then_inc(sem("x_done"), 1)


_INS = {
    "x": lambda a: a["x"].reshape(NH, P, C).transpose(1, 0, 2),
    "idx_cols": lambda a: np.stack([a["src"].reshape(T, P).T, a["dst"].reshape(T, P).T], 1),
    "idx_rows": lambda a: np.stack([a["src"], a["dst"]]),
    "type_rows": lambda a: np.broadcast_to(a["edge_type_8"], (HD, E)),
    "ew": lambda a: a["edge_weight"].reshape(T, P).T,
    "ea3": lambda a: a["edge_attr_3"].reshape(T, P, 3).transpose(1, 0, 2),
    "ea20T": lambda a: a["edge_attr_20"].T,
    "ea64T": lambda a: a["edge_attr_64"].T,
    "L0_WT": lambda a: a["L0_gnn_W"].T.reshape(KC, P, C).transpose(1, 0, 2),
    "L0_b": lambda a: a["L0_gnn_b"],
    "L1_WT": lambda a: a["L1_gnn_W"].T.reshape(KC, P, C).transpose(1, 0, 2),
    "a_src": lambda a: a["L1_gnn_a_src"].reshape(C),
    "a_dst": lambda a: a["L1_gnn_a_dst"].reshape(C),
    "emb": lambda a: a["L1_gnn_et_emb"],
    "L1_gamma": lambda a: a["L1_gnn_ln_gamma"],
    "L1_beta": lambda a: a["L1_gnn_ln_beta"],
    "Win": lambda a: np.stack([a["L2_gnn_W_in2f_s"], a["L2_gnn_W_in2f_v"]], 1),
    "Wf1": lambda a: a["L2_gnn_Wf1"],
    "bf1": lambda a: a["L2_gnn_bf1"].reshape(F, 1),
    "Wf2": lambda a: a["L2_gnn_Wf2"].reshape(F, 3, F, 2).transpose(0, 1, 3, 2).reshape(F, 6 * F),
    "bf2": lambda a: a["L2_gnn_bf2"].reshape(3, F, 2).transpose(0, 2, 1).reshape(1, 6 * F),
    "W1sv": lambda a: np.stack([a["L2_gnn_W1_s"], a["L2_gnn_W1_v"]]).reshape(2, F, 2, F).transpose(1, 0, 2, 3),
    "W2sv": lambda a: np.stack([a["L2_gnn_W2_s"], a["L2_gnn_W2_v"]], 1),
    "L3_W1ab": lambda a: a["L3_gnn_W1"][0:2 * C].reshape(2 * KC, P, C).transpose(1, 0, 2),
    "W1c": lambda a: a["L3_gnn_W1"][2 * C:],
    "L3_b1": lambda a: a["L3_gnn_b1"].reshape(1, C),
    "L3_W2": lambda a: a["L3_gnn_W2"].reshape(KC, P, C).transpose(1, 0, 2),
    "L3_b2": lambda a: a["L3_gnn_b2"].reshape(1, C),
    "L3_W3": lambda a: a["L3_gnn_W3"].reshape(2 * KC, P, C).transpose(1, 0, 2),
    "L3_b3": lambda a: a["L3_gnn_b3"],
    "L3_W4": lambda a: a["L3_gnn_W4"].reshape(KC, P, C).transpose(1, 0, 2),
    "L3_b4": lambda a: a["L3_gnn_b4"],
    "L3_gamma": lambda a: a["L3_gnn_gamma"],
    "L3_beta": lambda a: a["L3_gnn_beta"],
}


def kernel(**inputs):
    import concourse.bacc as _bacc
    from concourse.bass_utils import run_bass_kernel_spmd as _run

    nc = _bacc.Bacc("TRN2", target_bir_lowering=False, num_devices=1)
    given = {k: np.asarray(v) for k, v in inputs.items()}
    arrays, aps = {}, {}
    for name, layout in _INS.items():
        a = np.ascontiguousarray(layout(given))
        arrays["in_" + name] = a
        aps[name] = nc.dram_tensor("in_" + name, a.shape, mybir.dt.from_np(a.dtype), kind="ExternalInput").ap()
    out = nc.dram_tensor("out_x", (P, NH, C), F32, kind="ExternalOutput").ap()
    gnn_stack(nc, aps, out)
    r = _run(nc, [arrays], core_ids=[0])
    return np.ascontiguousarray(r.results[0]["out_x"].transpose(1, 0, 2).reshape(N, C))
```

```python
from contextlib import ExitStack

import numpy as np

import concourse.bass as bass
from concourse import mybir

F32 = mybir.dt.float32
F32R = mybir.dt.float32r
BF16 = mybir.dt.bfloat16
I32 = mybir.dt.int32
U8 = mybir.dt.uint8
ALU = mybir.AluOpType
ACT = mybir.ActivationFunctionType
AX = mybir.AxisListType.X

P = 128
N = 256
NH = N // P
E = 8192
C = 512
KC = C // P
T = E // P
G = 4
GE = G * P
NG = T // G
HD = 8
F = 128
RBF = 20
ED = 64
LN_EPS = 1e-5
LOG2 = float(np.log(2.0))
Y0 = float(1.0 / np.sqrt(4.0 * np.pi))
Y1 = float(np.sqrt(3.0 / (4.0 * np.pi)))
BANK = 512
CLAMP = 2.0 ** 30
CE = 1024
NCH = E // CE
DIGIT = 8
NDIG = 32 // DIGIT
NQ = 16
QT = 16
NB = T // QT
PART = 32


def gnn_stack(nc, d, out, layers=4):
    with ExitStack() as ctx:
        sems = {}

        def sem(name):
            if name not in sems:
                sems[name] = ctx.enter_context(nc.semaphore(name))
            return sems[name]

        def sb(name, shape, dt=F32):
            return ctx.enter_context(nc.sbuf_tensor(name, shape, dt))

        def under(name, words, dt=BF16):
            with nc.sbuf_tensor(name, [P, words * (2 if dt == BF16 else 1)], dt) as t:
                return t

        PS = ctx.enter_context(nc.psum_tensor("PS", [P, 8 * BANK], F32))

        def bank(k, n=1):
            return PS[:, k * BANK:(k + n) * BANK]

        node_row = sb("node_row", [P, N])
        node_col = sb("node_col", [P, NH])
        ident = sb("ident", [P, P])
        src_row = sb("src_row", [P, E], U8)
        dst_row = sb("dst_row", [P, E], U8)
        src_col = sb("src_col", [P, T])
        dst_col = sb("dst_col", [P, T])
        idx_raw = sb("idx_raw", [P, 2, T], I32)
        ew = sb("ew", [P, T])
        X = sb("X", [P, NH, C])
        Hn = sb("Hn", [P, NH, C])
        WN = sb("WN", [P, KC, C])
        LW = sb("LW", [P, 8, C])
        V = sb("V", [P, 4, C])
        U = sb("U", [P, 3584])
        stats = sb("stats", [P, NH, 6])
        mv = sb("mv", [P, NH, 2])
        one_col = sb("one_col", [P, 1])
        nt = sb("nt", [P, 2, NH, HD])
        rs = sb("rs", [P, 4, NH])
        ST_16 = under("ST_16", 2 * NH * GE)
        ST = sb("ST", [P, 2, NH, GE], F32R)
        DT_16 = under("DT_16", 2 * NH * GE)
        DT = sb("DT", [P, 2, NH, GE], F32R)
        EN_16 = under("EN_16", 2 * G * N)
        EN = sb("EN", [P, 2, G, N], F32R)
        TAB_16 = under("TAB_16", 4 * NH * C)
        TAB = sb("TAB", [P, 2, 2, NH, C], F32R)
        MSG_16 = under("MSG_16", 4 * 1024)
        MSG = sb("MSG", [P, 2, 2, 1024], F32R)
        HT_16 = under("HT_16", 4 * KC * GE)
        HT = sb("HT", [P, 2, 2, KC, GE], F32R)
        WF2_32 = under("WF2_32", 2 * C, F32)
        WF2 = sb("WF2", [P, 2, C], F32R)
        BF2 = sb("BF2", [64, C], F32R)
        W2S_16 = under("W2S_16", 2 * KC * C)
        W2S = sb("W2S", [P, 2, KC, C], F32R)
        B2S = sb("B2S", [64, C], F32R)
        WEA = sb("WEA", [P, 2, C], F32R)
        EA = sb("EA", [P, 2, GE], F32R)
        EB_16 = under("EB_16", 2 * GE)
        EB = sb("EB", [P, 2, GE], F32R)
        ones = sb("ones", [64, P], F32R)
        L = sb("L", [P, T, HD])
        NT = sb("NT", [P, 2, NH, 3, HD], BF16)
        MX = sb("MX", [P, NH, 3, HD], BF16)
        part = sb("part", [P, NH * HD])
        dig = sb("dig", [P, NDIG, NH, HD])
        digI = sb("digI", [P, NDIG, NH, HD], I32)
        dig16 = sb("dig16", [P, NH, HD], BF16)
        EMB = sb("EMB", [HD, 3, HD], BF16)
        emb = sb("emb", [HD, HD])
        node_row16 = sb("node_row16", [P, N], BF16)
        upper = sb("upper", [P, NQ, HD])
        upper16 = sb("upper16", [P, NQ, HD], BF16)
        Yv = sb("Yv", [P, T, 3])
        fT = LW[0:RBF, 2:4]
        Wf1 = sb("Wf1", [RBF, F])
        bf1 = sb("bf1", [P, 1])
        Win = sb("Win", [P, 2, F])
        W1sv = sb("W1sv", [P, 2, 2, F])
        W2sv = sb("W2sv", [P, 2, F])
        ea_raw = L[:].rearrange("p a b -> p (a b)")

        block = ctx.enter_context(nc.Block())

        def u(off, *shape):
            n = int(np.prod(shape))
            a = U[:, off:off + n]
            if len(shape) == 2:
                a = a.rearrange("p (a b) -> p a b", a=shape[0])
            if len(shape) == 3:
                a = a.rearrange("p (a b c) -> p a b c", a=shape[0], b=shape[1])
            return a

        f = lambda ap: ap.bitcast(F32)

        def flat(t):
            names = "abcd"[:len(t.shape) - 1]
            return t[:].rearrange(f"p {' '.join(names)} -> p ({' '.join(names)})")


        EN16 = HT_16[:].rearrange("p (t n) -> p t n", t=T)
        DT16 = [MSG_16, flat(LW).bitcast(BF16)]
        ST16 = ST_16[:].rearrange("p (s h e) -> p s h e", s=2, h=NH)
        T8 = EB_16[0:HD].rearrange("p (s e) -> p s e", s=2)
        SN16 = [t[:, 0:T // 2 * N].rearrange("p (t n) -> p t n", t=T // 2) for t in (TAB_16, W2S_16)]
        P24 = TAB_16[:, 4 * NH * C:4 * NH * C + 3 * T * HD].rearrange(
            "p (t w h) -> p t w h", t=T, w=3)
        adjT = u(512, NH, N)
        dis = u(1024, NH)
        hW = u(1032, NH, C)
        hT = u(2056, KC, N)
        l1_t = u(2056, NH, C)
        typ = u(0, 2, CE)[0:HD].bitcast(I32)
        l1_em = u(0, T, HD)
        v_bits = u(512, T * HD)
        active = u(1024, T, HD)
        d_bits = u(1536, T * HD)
        d_bits2 = V[:, 3]
        w_bits = u(2048, T * HD)
        g_bits = u(2560, T * HD)
        g16 = u(3072, 256).bitcast(BF16).rearrange("p (t h) -> p t h", t=T)
        w16 = u(3328, 256).bitcast(BF16).rearrange("p (t h) -> p t h", t=T)
        batch = lambda a: a.rearrange("p (k t q h) -> p k t q h", k=2, t=QT, q=NQ)
        masks = [batch(t[:])[:, k] for t in (ST_16, DT_16) for k in range(2)]
        digits = [batch(t)[:, k] for t in (EN_16[:], flat(WN).bitcast(BF16)) for k in range(2)]
        S_a, S_b = u(0, NH, NQ * HD), u(256, NH, NQ * HD)
        l1_m = u(0, 2, C)
        l2_m = u(0, 2, 9, F)
        l2_w = u(2304, 2, 4, F)
        l2_s = [WN[:, k, :] for k in range(4)]
        UA = [u(0, 2, C), u(1024, 2, C)]
        l3_buf = {"a": [u(m * GE, GE) for m in range(G)], "b": [u(2048 + k * C, C) for k in range(2)]}
        l2_tab = [u(0, NH, C)[:, h] for h in range(NH)]
        l2_agg = u(0, NH, 8, F)
        aggT = WN[:].rearrange("p a b -> p (a b)").rearrange("p (a b) -> p a b", a=8)
        SV = u(2048, 4, N)
        s2 = u(3072, 2, N)
        agg3 = u(0, NH, C)
        h3T = WF2_32[:].rearrange("p (a b) -> p a b", a=KC)
        r_y, r_v, r_sq = u(3090, T), u(3090 + T, T), u(3090 + 2 * T, T, 3)

        RSQRT = ("n0", "r2", "deg", "n1", "n1o", "n2", "n3", "n3o")
        NORMS = ("n0", "n1", "n2", "n3")
        TURNS = ("n0", "n1", "n2", "n3", "n3a", "n3u")

        LAG = 5

        def l3_tile(g, m):
            n = g * G + m - LAG
            if isinstance(g, int) and not 0 <= n < T:
                return None
            return n, (m - LAG) % G

        def l3_units(g, steps, a):
            for m in range(steps):
                if a:
                    yield "a", g * G + m, m
                if l3_tile(g, m) is not None:
                    yield ("b",) + l3_tile(g, m)

        def l3_bank(kind, n, j):
            if kind == "a":
                return bank(j)
            return bank(j) if isinstance(n, int) and n >= T - G else bank(4 + j % 2)

        def l3_scratch(kind, n, j):
            if kind == "a" or isinstance(n, int) and n >= T - G:
                return l3_buf["a"][j]
            return l3_buf["b"][j % 2]

        class Chain:

            def __init__(self, eng, name):
                self.eng, self.sem, self.n = eng, sem(name), 0

            def __call__(self, ins):
                self.n += 1
                ins.then_inc(self.sem, 1)
                self.eng.wait_ge(self.sem, self.n)

        def load(eng, dst, src, name):
            eng.dma_start(dst, src).then_inc(sem("in_" + name), 16)

        def row(ap):
            return ap.partition_broadcast(P)

        @block.sync
        def _(sp):
            load(sp, X[:], d["x"], "x")
            load(sp, idx_raw[:], d["idx_cols"], "idx")
            load(sp, WN[:], d["L0_WT"], "L0_W")
            load(sp, V[:, 0], row(d["L0_b"]), "L0_b")
            load(sp, ew[:], d["ew"], "ew")
            if layers > 2:
                load(sp, Yv[:], d["ea3"], "ea3")
            if layers > 1:
                load(sp, V[:, 1], row(d["a_src"]), "l1_vectors")
            if layers > 1:
                load(sp, V[:, 2], row(d["a_dst"]), "l1_vectors")
            if layers > 1:
                load(sp, emb[:], d["emb"], "l1_vectors")
            if layers > 2:
                load(sp, Win[:], d["Win"], "l2_weights")
            if layers > 2:
                load(sp, Wf1[:], d["Wf1"], "l2_weights")
            if layers > 2:
                load(sp, bf1[:], d["bf1"], "l2_weights")
            if layers > 2:
                load(sp, W1sv[:], d["W1sv"], "l2_weights")
            if layers > 2:
                load(sp, W2sv[:], d["W2sv"], "l2_weights")
            for k in range(4):
                if k:
                    sp.wait_ge(sem("rows_cast"), k)
                load(sp, LW[:].rearrange("p a b -> p (a b)").bitcast(I32),
                     row(d["idx_rows"][1 - k // 2, (k % 2) * (E // 2):(k % 2 + 1) * (E // 2)]), "rows")
            sp.wait_ge(sem("l0_hW_ps"), 1)
            if layers > 1:
                load(sp, WN[:], d["L1_WT"], "L1_W")
            if layers > 1:
                sp.wait_ge(sem("x_done"), 1)
                def types(i, b, wait):
                    c = i * 2 + b
                    if wait:
                        sp.wait_ge(sem("l1a_onehots"), c - 1)
                    sp.dma_start(typ[:, b], d["type_rows"][:, bass.ds(c * CE, CE)]).then_inc(sem(f"in_type{b}"), 16)
                types(0, 0, False)
                types(0, 1, False)
                with sp.Fori(1, NCH // 2) as i:
                    types(i, 0, True)
                    types(i, 1, True)
                sp.wait_ge(sem("l1_esd"), 1)
                load(sp, V[:, 1], row(d["L1_gamma"]), "l1_affine")
                load(sp, V[:, 2], row(d["L1_beta"]), "l1_affine")
            if layers > 2:
                sp.wait_ge(sem("rows_cast"), 4)
                sp.wait_ge(sem("l1_mg_ps"), 1)
                load(sp, LW[:, 0], d["Wf2"][:, 0:4 * F], "l2_filter")
                load(sp, LW[0:1, 1], d["bf2"][:, 0:4 * F], "l2_filter")
                load(sp, LW[32:33, 1], d["bf2"][:, 0:4 * F], "l2_filter")

                def rbf(i, b, wait):
                    g = i * 2 + b
                    if wait:
                        sp.wait_ge(sem("l2_h_ps"), g - 1)
                    sp.dma_start(fT[:, b], d["ea20T"][:, bass.ds(g * GE, GE)]).then_inc(sem(f"in_rbf{b}"), 16)
                rbf(0, 0, False)
                rbf(0, 1, False)
                with sp.Fori(1, NG // 2) as i:
                    rbf(i, 0, True)
                    rbf(i, 1, True)
            if layers > 3:
                sp.wait_ge(sem("l2_wsplit"), 1)
                sp.wait_ge(sem("l2_h_ps"), NG)
                load(sp, LW[:], d["L3_W1ab"], "L3_W1ab")
                sp.wait_ge(sem("l1_out"), 1)
                load(sp, V[:, 0], row(d["L3_b3"]), "l3_vectors")
                load(sp, V[:, 1], row(d["L3_b4"]), "l3_vectors")
                load(sp, V[:, 2], row(d["L3_gamma"]), "l3_vectors")
                load(sp, V[:, 3], row(d["L3_beta"]), "l3_vectors")
                sp.wait_ge(sem("l2_out"), 1)
                load(sp, WN[:], d["L3_W2"], "L3_W2")
                for r in range(2):
                    load(sp, u(0, 3, C)[64 * r:64 * r + 64, 0], d["W1c"], "l3_edge_weights")
                for r in (64, 96):
                    load(sp, u(0, 3, C)[r:r + 1, 1], d["L3_b1"], "l3_edge_weights")
                for r in (0, 32):
                    load(sp, u(0, 3, C)[r:r + 1, 2], d["L3_b2"], "l3_edge_weights")

                def feats(g, wait):
                    if wait:
                        sp.wait_ge(sem("l3_ea"), g)
                    for r in range(2):
                        sp.dma_start(ea_raw[64 * r:64 * r + 64, :],
                                     d["ea64T"][:, bass.ds(g * GE, GE)]).then_inc(sem("in_ea"), 16)
                feats(0, False)
                with sp.Fori(1, NG) as g:
                    feats(g, True)
                sp.wait_ge(sem("l3_w2split"), 1)
                load(sp, WN[:], d["L3_W4"], "L3_W4")
                sp.wait_ge(sem("l3_tab_ps"), 2)
                load(sp, LW[:], d["L3_W3"], "L3_W3")
            sp.wait_ge(sem("x_done"), layers)
            sp.dma_start(out, X[:]).then_inc(sem("out"), 16)
            sp.wait_ge(sem("out"), 16)

        @block.gpsimd
        def _(pool):
            pool.iota(node_row[:], [[1, N]], base=0, channel_multiplier=0,
                      allow_small_or_imprecise_dtypes=True).then_inc(sem("iotas"), 1)
            pool.iota(node_col[:], [[P, NH]], base=0, channel_multiplier=1,
                      allow_small_or_imprecise_dtypes=True).then_inc(sem("iotas"), 1)
            pool.iota(upper[:], [[1, NQ], [0, HD]], base=0, channel_multiplier=0,
                      allow_small_or_imprecise_dtypes=True).then_inc(sem("iotas"), 1)


            def onehot_T(dst, row_, b, g):
                for h in range(NH):
                    last = pool.tensor_scalar(dst[:, b, h], row_[:, g * GE:(g + 1) * GE], node_col[:, h:h + 1], None,
                                              ALU.is_equal)
                return last

            if layers > 1:
                def sources(g, b, wait):
                    if wait:
                        pool.wait_ge(sem("l1_hs_ps"), g * G - G)
                    onehot_T(ST, src_row, b, g).then_inc(sem("l1_st"), 1)
                pool.wait_ge(sem("rows_cast"), 4)
                pool.wait_ge(sem("l1_mg_ps"), 1)
                for g in range(NG):
                    sources(g, g % 2, g >= 2)
            if layers > 2:
                def both_ends(g, b, wait):
                    if wait:
                        pool.wait_ge(sem("l2_g_ps"), g * G - G)
                    onehot_T(DT, dst_row, b, g).then_inc(sem("l2_onehots"), 1)
                    if wait:
                        pool.wait_ge(sem("l2_scat"), g * G - G)
                    else:
                        pool.wait_ge(sem("l1_scat"), T - G + b * G)
                    for j in range(G):
                        t = g * G + j
                        last = pool.tensor_scalar(EN[:, b, j], node_row[:], src_col[:, t:t + 1], None, ALU.is_equal)
                    last.then_inc(sem("l2_en"), 1)
                for g in range(NG):
                    both_ends(g, g % 2, g >= 2)

        @block.scalar
        def _(act):
            chain = Chain(act, "act_chain")
            act.preload_act_table_set("natural_log_exp_and_others")

            def rsqrt_guess(tag, v, y):
                act.wait_ge(sem("rsqrt_v"), RSQRT.index(tag) + 1)
                chain(act.activation(y, v, ACT.Ln))
                act.activation(y, y, ACT.Exp, scale=-0.5).then_inc(sem("rsqrt_y"), 1)

            def norm(tag):
                rsqrt_guess(tag, rs[:, 0], rs[:, 1])

            def transposed(tag, k0, dst):
                for q in range(2):
                    act.wait_ge(sem("turned_ps"), 2 * TURNS.index(tag) + q + 1)
                    act.activation(dst[:, 2 * q:2 * q + 2, :].rearrange("p a b -> p (a b)"), bank(k0 + q),
                                   ACT.Copy).then_inc(sem("turned"), 1)

            norm("n0")
            transposed("n0", 3, hT)
            if layers > 2:
                rsqrt_guess("r2", r_v, r_y)
            for k in range(4):
                act.wait_ge(sem("in_rows"), 16 * (k + 1))
                rows = (dst_row, src_row)[k // 2]
                act.activation(rows[:, (k % 2) * (E // 2):(k % 2 + 1) * (E // 2)],
                               LW[:].rearrange("p a b -> p (a b)").bitcast(I32), ACT.Copy).then_inc(sem("rows_cast"), 1)
            rsqrt_guess("deg", rs[:, 0], rs[:, 1])
            def filt_abs(g):
                act.wait_ge(sem("l2_h_ps"), g + 1)
                if not (isinstance(g, int) and g == 0):
                    act.wait_ge(sem("l2_ssp"), g)
                act.activation(l2_s[0], bank(7), ACT.Abs, bias=bf1[:, 0:1]).then_inc(sem("l2_abs"), 1)
                act.activation(l2_s[1], bank(7), ACT.Relu, bias=bf1[:, 0:1])

            def filt_ln(g):
                act.wait_ge(sem("l2_abs"), g + 1)
                act.activation(l2_s[0], l2_s[0], ACT.Exp, scale=-1.0).then_inc(sem("l2_exp"), 1)
                act.wait_ge(sem("l2_exp"), g + 1)
                act.activation(l2_s[0], l2_s[0], ACT.Ln, bias=1.0).then_inc(sem("l2_ln"), 1)

            if layers > 1:
                norm("n1")
                transposed("n1", 3, hT)

                act.wait_ge(sem("l1_shift"), 1)
                act.activation(L[:], L[:], ACT.Exp).then_inc(sem("l1_p"), 1)

                def onehots_E(g, b, free):
                    if free:
                        act.wait_ge(sem("l1_scat"), g * G - G)
                    act.activation(EN[:, b].rearrange("p a b -> p (a b)"),
                                   EN16[:, bass.ds(g * G, G)].rearrange("p a b -> p (a b)"),
                                   ACT.Copy).then_inc(sem("l1_en"), 1)

                def tile(t, q, free):
                    act.wait_ge(sem("l1_msg"), t + 1)
                    if free:
                        act.wait_ge(sem("l1_scat"), t - 1)
                    act.activation(MSG[:, q, 0, 0:C], l1_m[:, q], ACT.Copy).then_inc(sem("l1_hi"), 1)

                def group(i, b, first, last):
                    g = i * 2 + b
                    for j in range(G):
                        tile(g * G + j, j % 2, not (first and b == 0 and j < 2))
                        if j == 1 and not (last and b == 1):
                            onehots_E(g + 1, 1 - b, not (first and b == 0))
                act.wait_ge(sem("l1_mg_ps"), 1)
                onehots_E(0, 0, False)
                group(0, 0, True, False)
                group(0, 1, False, False)
                with act.Fori(1, NG // 2 - 1) as i:
                    group(i, 0, False, False)
                    group(i, 1, False, False)
                group(NG // 2 - 1, 0, False, False)
                group(NG // 2 - 1, 1, False, True)
                if layers > 2:
                    act.wait_ge(sem("in_l2_weights"), 80)
                    filt_abs(0)
                    filt_ln(0)
                norm("n1o")
            if layers > 2:
                norm("n2")
                for k in range(NH):
                    act.wait_ge(sem("turned_ps"), 2 * TURNS.index("n2") + k + 1)
                    act.activation(hT[:, :, k * P:(k + 1) * P], bank(3 + k).rearrange("p (a b) -> p a b", a=4),
                                   ACT.Copy).then_inc(sem("turned"), 1)
                for k in range(NH):
                    act.wait_ge(sem("l2_tab_ps"), k + 1)
                    act.activation(l2_tab[k], bank(5 + k), ACT.Copy,
                                   scale=float(1.0 / np.sqrt(F))).then_inc(sem("l2_tab"), 1)

                def weights(t, q, free):
                    act.wait_ge(sem("l2_w_ps"), t + 1)
                    if free:
                        act.wait_ge(sem("l2_msg"), t - 1)
                    act.activation(l2_w[:, q].rearrange("p a b -> p (a b)"), bank(6), ACT.Copy,
                                   scale=ew[:, bass.ds(t, 1)]).then_inc(sem("l2_w"), 1)

                def high(t, q, free):
                    act.wait_ge(sem("l2_msg"), t + 1)
                    act.wait_ge(sem("l2_outer"), t + 1)
                    if free:
                        act.wait_ge(sem("l2_scat"), t - 1)
                    act.activation(MSG[:, q, 0], l2_m[:, q, 0:8].rearrange("p a b -> p (a b)"),
                                   ACT.Copy).then_inc(sem("l2_hi"), 1)

                def outer(t, q, free):
                    act.wait_ge(sem("l2_sW"), t + 1)
                    if free:
                        act.wait_ge(sem("l2_lo"), t - 1)
                    for k in range(3):
                        last = act.activation(l2_m[:, q, 2 + k], l2_m[:, q, 8], ACT.Copy,
                                              scale=Yv[:, bass.ds(t, 1), k])
                    last.then_inc(sem("l2_outer"), 1)

                def group(i, b, first, last):
                    g = i * 2 + b
                    for j in range(G):
                        t = g * G + j
                        start = first and b == 0
                        end = last and b == 1
                        if not (end and j == G - 1):
                            weights(t + 1, (j + 1) % 2, not (start and j == 0))
                        outer(t, j % 2, not (start and j < 2))
                        high(t, j % 2, not (start and j < 2))
                        if j == 0 and not end:
                            filt_abs(g + 1)
                        if j == 1 and not end:
                            filt_ln(g + 1)
                act.wait_ge(sem("in_l2_weights"), 80)
                weights(0, 0, False)
                group(0, 0, True, False)
                group(0, 1, False, False)
                with act.Fori(1, NG // 2 - 1) as i:
                    group(i, 0, False, False)
                    group(i, 1, False, False)
                group(NG // 2 - 1, 0, False, False)
                group(NG // 2 - 1, 1, False, True)
                act.wait_ge(sem("l2_S_ps"), 1)
                chain(act.activation(s2[:, 0], bank(4)[:, 0:N], ACT.Abs))
                act.activation(s2[:, 1], bank(4)[:, 0:N], ACT.Relu)
                chain(act.activation(s2[:, 0], s2[:, 0], ACT.Exp, scale=-1.0))
                act.activation(s2[:, 0], s2[:, 0], ACT.Ln, bias=1.0).then_inc(sem("l2_S_ln"), 1)
            if layers > 3:
                norm("n3")
                transposed("n3", 3, h3T)

                def start(kind, n, j):
                    act.wait_ge(sem(f"l3{kind}_ps"), n + 1)
                    ring = G if kind == "a" else 2
                    if kind == "b" and isinstance(n, int) and n >= T - G:
                        act.wait_ge(sem("l3a_lo"), T)
                    elif not (isinstance(n, int) and n < ring):
                        act.wait_ge(sem(f"l3{kind}_lo"), n + 1 - ring)
                    act.activation(l3_scratch(kind, n, j), l3_bank(kind, n, j), ACT.Exp).then_inc(sem(f"l3{kind}_exp"), 1)

                def square(kind, n, j):
                    act.wait_ge(sem(f"l3{kind}_min"), n + 1)
                    act.activation(l3_scratch(kind, n, j), l3_scratch(kind, n, j), ACT.Square,
                                   bias=1.0).then_inc(sem(f"l3{kind}_sq"), 1)

                def log(kind, n, j):
                    act.wait_ge(sem(f"l3{kind}_sq"), n + 1)
                    act.activation(l3_scratch(kind, n, j), l3_scratch(kind, n, j), ACT.Ln, bias=0.5,
                                   scale=0.5).then_inc(sem(f"l3{kind}_ln"), 1)

                def quotient(kind, n, j):
                    act.wait_ge(sem(f"l3{kind}_ln"), n + 1)
                    act.activation(l3_scratch(kind, n, j), l3_scratch(kind, n, j), ACT.Exp,
                                   scale=-1.0).then_inc(sem(f"l3{kind}_q"), 1)

                fl = lambda a: a.rearrange("p a b -> p (a b)")

                def body(g, prev, steps=G, a=True):
                    for unit in l3_units(g, steps, a):
                        start(*unit)
                        if prev:
                            log(*prev)
                        square(*unit)
                        if prev:
                            quotient(*prev)
                        prev = unit
                    return prev
                prev = body(0, None)
                prev = body(1, prev)
                with act.Fori(2, NG) as g:
                    body(g, ("b", g * G - 1 - LAG, (-1 - LAG) % G))
                prev = body(NG, ("b", NG * G - 1 - LAG, (-1 - LAG) % G), steps=LAG, a=False)
                log(*prev)
                quotient(*prev)
                transposed("n3a", 0, hT)
                for h in range(NH):
                    act.wait_ge(sem("l3_u_in"), h + 1)
                    act.activation(UA[1][:, h], UA[0][:, h], ACT.Exp).then_inc(sem("l3_u_exp"), 1)
                    act.wait_ge(sem("l3_u_min"), h + 1)
                    chain(act.activation(UA[1][:, h], UA[1][:, h], ACT.Square, bias=1.0))
                    chain(act.activation(UA[1][:, h], UA[1][:, h], ACT.Ln, bias=0.5, scale=0.5))
                    act.activation(UA[1][:, h], UA[1][:, h], ACT.Exp, scale=-1.0).then_inc(sem("l3_u_q"), 1)
                norm("n3o")

        @block.tensor
        def _(pe):
            def transpose_nodes(tag, src, k0):
                pe.wait_ge(sem("h_ready"), NORMS.index(tag) + 1)
                for k in range(KC):
                    for h in range(NH):
                        o = bank(k0 + k // 2)[:, (k % 2) * N + h * P:(k % 2) * N + h * P + P]
                        m = pe.transpose(o, src[:, h, k * P:(k + 1) * P], ident[:])
                    if k % 2:
                        m.then_inc(sem("turned_ps"), 1)

            def node_mm(k0, xT, w, nk=KC, w0=0, start=True, stop=True):
                for h in range(NH):
                    for k in range(nk):
                        m = pe.matmul(bank(k0 + h), xT[:, k, h * P:(h + 1) * P], w[:, w0 + k, :],
                                      start=start and k == 0, stop=stop and k == nk - 1)
                return m

            def both(o, lhsT, hi, lo, start, stop, skip=False):
                pe.matmul(o, lhsT, hi, start=start, stop=False, skip_group_check=skip)
                return pe.matmul(o, lhsT, lo, start=False, stop=stop, skip_group_check=skip)

            transpose_nodes("n0", Hn, 3)
            pe.wait_ge(sem("turned"), 2 * TURNS.index("n0") + 2)
            pe.wait_ge(sem("in_L0_W"), 16)
            node_mm(5, hT, WN).then_inc(sem("l0_hW_ps"), 1)
            for t in range(T):
                if t % G == 0:
                    pe.wait_ge(sem("l0_onehots"), t // G + 1)
                for h in range(NH):
                    m = pe.matmul(bank(h)[:, 0:N], EN16[:, t, h * P:(h + 1) * P], SN16[2 * t // T][:, t % (T // 2)],
                                  start=t == 0, stop=t == T - 1)
            m.then_inc(sem("l0_count"), 1)
            pe.wait_ge(sem("l0_adj"), 1)
            for h in range(NH):
                for k in range(NH):
                    m = pe.matmul(bank(2)[:, h:h + 1], adjT[:, k, h * P:(h + 1) * P], one_col[:, 0:1],
                                  start=k == 0, stop=k == NH - 1)
            m.then_inc(sem("l0_deg"), 1)
            pe.wait_ge(sem("l0_hW"), 1)
            for h in range(NH):
                for k in range(NH):
                    m = pe.matmul(bank(h), adjT[:, k, h * P:(h + 1) * P], hW[:, k, :], start=k == 0, stop=k == NH - 1)
            m.then_inc(sem("l0_ps"), 1)
            def hidden(g, b, free):
                pe.wait_ge(sem(f"in_rbf{b}"), (g - b) * 8 + 16)
                if free:
                    pe.wait_ge(sem("l2_ssp"), g)
                pe.matmul(bank(7), Wf1[:], fT[:, b], start=True, stop=True).then_inc(sem("l2_h_ps"), 1)

            if layers > 1:
                transpose_nodes("n1", Hn, 3)
                pe.wait_ge(sem("turned"), 2 * TURNS.index("n1") + 2)
                pe.wait_ge(sem("in_L1_W"), 16)
                node_mm(5, hT, WN).then_inc(sem("l1_h_ps"), 1)
                pe.wait_ge(sem("l1_esd"), 1)

                def spot(k, t):
                    return PS[:, k * BANK + t * PART:k * BANK + t * PART + 3 * HD]

                fl = lambda a: a.rearrange("p a b -> p (a b)")

                for c in range(NCH):
                    pe.wait_ge(sem("l1a_onehots"), c + 1)
                    for j in range(CE // P):
                        t = c * (CE // P) + j
                        for h in range(NH):
                            pe.matmul(spot(0, t), ST16[:, c % 2, h, j * P:(j + 1) * P], fl(NT[:, 0, h]),
                                      start=h == 0, stop=False)
                        for h in range(NH):
                            pe.matmul(spot(0, t), DT16[h][:, t * P:(t + 1) * P], fl(NT[:, 1, h]),
                                      start=False, stop=h == 1)
                        m = pe.matmul(spot(4, t), T8[:, c % 2, j * P:(j + 1) * P], fl(EMB[:]), start=True, stop=True)
                    m.then_inc(sem("l1a_ps"), 1)
                def sums(k):
                    for q in range(NB):
                        pe.wait_ge(sem("l1b_digits"), k * NB + q + 1)
                        for j in range(QT):
                            t = q * QT + j
                            for h in range(NH):
                                m = pe.matmul(bank(h)[:, 0:NQ * HD], EN16[:, t, h * P:(h + 1) * P],
                                              fl(digits[q][:, j]), start=t == 0, stop=t == T - 1)
                        m.then_inc(sem("l1b_sum"), 1)
                def to_edges(out, table):
                    for t in range(T):
                        for h in range(NH):
                            m = pe.matmul(out(t), DT16[h][:, t * P:(t + 1) * P], table[:, h], start=h == 0, stop=h == 1)
                    return m
                with pe.Fori(0, NDIG - 1) as k:
                    sums(k)
                    pe.wait_ge(sem("l1b_dig"), k + 1)
                    to_edges(lambda t: bank(2)[:, t * HD:(t + 1) * HD], dig16).then_inc(sem("l1b_match"), 1)
                sums(NDIG - 1)

                pe.wait_ge(sem("l1_mx"), 1)
                to_edges(lambda t: spot(3, t), MX[:].rearrange("p n a b -> p n (a b)")).then_inc(sem("l1_mg_ps"), 1)

                pe.wait_ge(sem("l1_p24"), 1)
                for t in range(T):
                    for h in range(NH):
                        m = pe.matmul(bank(2 + h)[:, 0:3 * HD], EN16[:, t, h * P:(h + 1) * P], fl(P24[:, t]),
                                      start=t == 0, stop=t == T - 1)
                m.then_inc(sem("l1_den"), 1)

                def gather(t, b, j, free):
                    if free:
                        pe.wait_ge(sem("l1_msg"), t - 1)
                    for h in range(NH):
                        m = both(bank(4 + j % 2), ST[:, b, h, j * P:(j + 1) * P], TAB[:, 0, 0, h], TAB[:, 0, 1, h],
                                 h == 0, h == 1)
                    m.then_inc(sem("l1_hs_ps"), 1)

                def scatter(t, g, b, j, start, stop):
                    pe.wait_ge(sem("l1_lo"), t + 1)
                    if j == 0:
                        pe.wait_ge(sem("l1_en"), g + 1)
                    for h in range(NH):
                        m = both(bank(h), EN[:, b, j, h * P:(h + 1) * P], MSG[:, j % 2, 0, 0:C],
                                 MSG[:, j % 2, 1, 0:C], start, stop)
                    m.then_inc(sem("l1_scat"), 1)

                def group(i, b, first, last):
                    g = i * 2 + b
                    for j in range(G):
                        t = g * G + j
                        begin = first and b == 0
                        if j < G - 1:
                            gather(t + 1, b, j + 1, not (begin and j == 0))
                        elif not (last and b == 1):
                            pe.wait_ge(sem("l1_st"), g + 2)
                            gather(t + 1, 1 - b, 0, True)
                        if not (begin and j == 0):
                            scatter(t - 1, g if j else g - 1, b if j else 1 - b, (j - 1) % G, begin and j == 1, False)
                pe.wait_ge(sem("l1_st"), 1)
                gather(0, 0, 0, False)
                group(0, 0, True, False)
                group(0, 1, False, False)
                with pe.Fori(1, NG // 2 - 1) as i:
                    group(i, 0, False, False)
                    group(i, 1, False, False)
                group(NG // 2 - 1, 0, False, False)
                group(NG // 2 - 1, 1, False, True)
                if layers > 2:
                    pe.wait_ge(sem("in_l2_weights"), 80)
                    hidden(0, 0, False)
                scatter(T - 1, NG - 1, 1, G - 1, False, True)
            if layers > 2:
                pe.wait_ge(sem("h_ready"), NORMS.index("n2") + 1)
                for h in range(NH):
                    for k in range(4):
                        src = Hn[:, h, 0:F] if k == 0 else Hn[:, h, F + k - 1:C:3]
                        m = pe.transpose(bank(3 + h)[:, k * P:(k + 1) * P], src, ident[:])
                    m.then_inc(sem("turned_ps"), 1)
                pe.wait_ge(sem("in_l2_weights"), 80)
                for h in range(NH):
                    pe.wait_ge(sem("turned"), 2 * TURNS.index("n2") + h + 1)
                    for k in range(4):
                        m = pe.matmul(bank(5 + h)[:, k * F:(k + 1) * F], hT[:, k, h * P:(h + 1) * P],
                                      Win[:, min(k, 1)], start=True, stop=True)
                    m.then_inc(sem("l2_tab_ps"), 1)

                def gather(t, b, j, free):
                    if free:
                        pe.wait_ge(sem("l2_msg"), t - 1)
                    for h in range(NH):
                        m = both(bank(4 + j % 2), DT[:, b, h, j * P:(j + 1) * P], TAB[:, 0, 0, h], TAB[:, 0, 1, h],
                                 h == 0, h == 1)
                    m.then_inc(sem("l2_g_ps"), 1)

                def weights(t, b, j, free):
                    if free:
                        pe.wait_ge(sem("l2_w"), t)
                    s = slice(j * P, (j + 1) * P)
                    pe.matmul(bank(6), HT[:, b, 0, 0, s], WF2[:, 0], start=True, stop=False)
                    pe.matmul(bank(6), HT[:, b, 0, 0, s], WF2[:, 1], start=False, stop=False)
                    pe.matmul(bank(6), HT[:, b, 1, 0, s], WF2[:, 0], start=False, stop=False)
                    pe.matmul(bank(6), ones[:], BF2[:], start=False, stop=True).then_inc(sem("l2_w_ps"), 1)

                def scatter(t, g, b, j, start, stop):
                    pe.wait_ge(sem("l2_lo"), t + 1)
                    if j == 0:
                        pe.wait_ge(sem("l2_en"), g + 1)
                    for h in range(NH):
                        for c in range(2):
                            m = both(bank(2 * h + c), EN[:, b, j, h * P:(h + 1) * P],
                                     MSG[:, j % 2, 0, c * C:(c + 1) * C], MSG[:, j % 2, 1, c * C:(c + 1) * C],
                                     start, stop)
                    m.then_inc(sem("l2_scat"), 1)

                def group(i, b, first, last):
                    g = i * 2 + b
                    begin = first and b == 0
                    for j in range(G):
                        t = g * G + j
                        if j == 0 and not (last and b == 1):
                            hidden(g + 1, 1 - b, True)
                        if j < G - 1:
                            weights(t + 1, b, j + 1, True)
                            gather(t + 1, b, j + 1, not (begin and j == 0))
                        elif not (last and b == 1):
                            pe.wait_ge(sem("l2_onehots"), g + 2)
                            pe.wait_ge(sem("l2_hid"), g + 2)
                            weights(t + 1, 1 - b, 0, True)
                            gather(t + 1, 1 - b, 0, True)
                        if not (begin and j == 0):
                            scatter(t - 1, g if j else g - 1, b if j else 1 - b, (j - 1) % G, begin and j == 1, False)
                pe.wait_ge(sem("in_l2_weights"), 80)
                pe.wait_ge(sem("l2_ready"), 1)
                pe.wait_ge(sem("l2_onehots"), 1)
                pe.wait_ge(sem("l2_hid"), 1)
                weights(0, 0, 0, False)
                gather(0, 0, 0, False)
                group(0, 0, True, False)
                group(0, 1, False, False)
                with pe.Fori(1, NG // 2 - 1) as i:
                    group(i, 0, False, False)
                    group(i, 1, False, False)
                group(NG // 2 - 1, 0, False, False)
                group(NG // 2 - 1, 1, False, True)
                scatter(T - 1, NG - 1, 1, G - 1, False, True)
                for h in range(NH):
                    pe.wait_ge(sem("l2_agg"), h + 1)
                    for k in range(8):
                        m = pe.transpose(bank(4 + k // 2)[:, (k % 2) * N + h * P:(k % 2) * N + h * P + P],
                                         l2_agg[:, h, k], ident[:])
                m.then_inc(sem("l2_aggT_ps"), 1)
                pe.wait_ge(sem("l2_aggT"), 1)
                pe.wait_ge(sem("in_l2_weights"), 80)
                for k in range(2):
                    m = pe.matmul(bank(4)[:, 0:N], W1sv[:, 0, k], aggT[:, k], start=k == 0, stop=k == 1)
                m.then_inc(sem("l2_S_ps"), 1)
                for c in range(3):
                    for k in range(2):
                        m = pe.matmul(bank(5 + c)[:, 0:N], W1sv[:, 1, k], aggT[:, 2 + 3 * k + c],
                                      start=k == 0, stop=k == 1)
                m.then_inc(sem("l2_V_ps"), 1)
                pe.wait_ge(sem("l2_SV"), 1)
                pe.wait_ge(sem("in_l2_weights"), 80)
                for h in range(NH):
                    for k in range(4):
                        m = pe.matmul(bank(h)[:, k * F:(k + 1) * F], SV[:, k, h * P:(h + 1) * P],
                                      W2sv[:, min(k, 1)], start=True, stop=True)
                m.then_inc(sem("l2_ps"), 1)
            if layers > 3:
                transpose_nodes("n3", Hn, 3)
                pe.wait_ge(sem("turned"), 2 * TURNS.index("n3") + 2)
                pe.wait_ge(sem("in_L3_W1ab"), 16)
                node_mm(5, h3T, LW).then_inc(sem("l3_tab_ps"), 1)
                node_mm(1, h3T, LW, w0=KC).then_inc(sem("l3_tab_ps"), 1)

                def edge_in(g, b, m):
                    n = g * G + m
                    if m == 0:
                        pe.wait_ge(sem("l3_onehots"), g + 1)
                    if not (isinstance(n, int) and n < G):
                        pe.wait_ge(sem("l3a_y"), n + 1 - G)
                    s = slice(m * P, (m + 1) * P)
                    for w, oh in enumerate((ST, DT)):
                        for h in range(NH):
                            for part in range(2):
                                pe.matmul(bank(m), TAB[:, w, part, h, s], oh[:, b, h], start=w + h + part == 0,
                                          stop=False)
                    pe.matmul(bank(m), WEA[:, 0, s], EA[:, b], start=False, stop=False)
                    pe.matmul(bank(m), WEA[:, 1, s], EB[:, b], start=False, stop=True).then_inc(sem("l3a_ps"), 1)

                def edge_hid(n, b, j):
                    if j == 0:
                        pe.wait_ge(sem("l3a_lo"), n + G)
                    if isinstance(n, int) and n >= T - G:
                        pe.wait_ge(sem("l3a_y"), T)
                    elif not (isinstance(n, int) and n < 2):
                        pe.wait_ge(sem("l3b_y"), n - 1)
                    o, s = l3_bank("b", n, j), slice(j * P, (j + 1) * P)
                    for c in range(KC):
                        pe.matmul(o, HT[:, b, 0, c, s], W2S[:, 0, c], start=c == 0, stop=False)
                        pe.matmul(o, HT[:, b, 0, c, s], W2S[:, 1, c], start=False, stop=False)
                        pe.matmul(o, HT[:, b, 1, c, s], W2S[:, 0, c], start=False, stop=False)
                    pe.matmul(o, ones[:], B2S[:], start=False, stop=True).then_inc(sem("l3b_ps"), 1)

                def scatter(n, b, j):
                    pe.wait_ge(sem("l3b_lo"), n + 1)
                    first, last = isinstance(n, int) and n == 0, isinstance(n, int) and n == T - 1
                    for h in range(NH):
                        s = slice(j % 2 * C, (j % 2 + 1) * C)
                        m = both(bank(6 + h), EN[:, b, j, h * P:(h + 1) * P], MSG[:, j // 2, 0, s],
                                 MSG[:, j // 2, 1, s], first, last)
                    m.then_inc(sem("l3_scat"), 1)

                def body(g, b, steps=G, a=True):
                    for m in range(steps):
                        if m == LAG:
                            pe.wait_ge(sem("in_L3_W3"), 16)
                            pe.wait_ge(sem("l3b_y"), T - G)
                            for h in range(NH):
                                for k in range(KC):
                                    pe.matmul(bank(4 + h), h3T[:, k, h * P:(h + 1) * P], LW[:, k, :],
                                              start=k == 0, stop=False)
                        if a:
                            edge_in(g, b, m)
                        tile = l3_tile(g, m)
                        if tile is not None:
                            edge_hid(tile[0], b if m < LAG - G else 1 - b, tile[1])
                        tile = l3_tile(g, m - 2)
                        if tile is not None:
                            if tile[1] == 0:
                                pe.wait_ge(sem("l3_en"), g)
                            scatter(tile[0], b if m - 2 < LAG - G else 1 - b, tile[1])
                pe.wait_ge(sem("l3_ready"), 1)
                body(0, 0)
                body(1, 1)
                with pe.Fori(1, NG // 2) as i:
                    body(i * 2, 0)
                    body(i * 2 + 1, 1)
                body(NG, 0, steps=LAG + 2, a=False)
                def transpose_any(tag, src, k0):
                    for k in range(KC):
                        for h in range(NH):
                            o = bank(k0 + k // 2)[:, (k % 2) * N + h * P:(k % 2) * N + h * P + P]
                            m = pe.transpose(o, src[:, h, k * P:(k + 1) * P], ident[:])
                        if k % 2:
                            m.then_inc(sem("turned_ps"), 1)
                pe.wait_ge(sem("l3_agg"), 1)
                transpose_any("n3a", agg3, 0)
                pe.wait_ge(sem("turned"), 2 * TURNS.index("n3a") + 2)
                for h in range(NH):
                    for k in range(KC):
                        m = pe.matmul(bank(4 + h), hT[:, k, h * P:(h + 1) * P], LW[:, KC + k, :],
                                      start=False, stop=k == KC - 1)
                    m.then_inc(sem("l3_u_ps"), 1)
                pe.wait_ge(sem("in_L3_W4"), 16)
                for h in range(NH):
                    pe.wait_ge(sem("l3_u"), h + 1)
                    for k in range(KC):
                        m = pe.transpose(bank(h)[:, k * P:(k + 1) * P], UA[0][:, h, k * P:(k + 1) * P], ident[:])
                    m.then_inc(sem("turned_ps"), 1)
                    pe.wait_ge(sem("turned"), 2 * TURNS.index("n3u") + h + 1)
                    for k in range(KC):
                        m = pe.matmul(bank(2 + h), hT[:, k, h * P:(h + 1) * P], WN[:, k, :],
                                      start=k == 0, stop=k == KC - 1)
                    m.then_inc(sem("l3_out_ps"), 1)

        @block.vector
        def _(dve):
            chain = Chain(dve, "dve_chain")
            tt, ts, stt, cp = dve.tensor_tensor, dve.tensor_scalar, dve.scalar_tensor_tensor, dve.tensor_copy

            def split(hi, lo, src):
                chain(cp(hi, src))
                return tt(lo, src, f(hi), ALU.subtract)

            def newton(y, v, t):
                chain(tt(t, y, y, ALU.mult))
                chain(tt(t, t, v, ALU.mult))
                chain(ts(t, t, -0.5, 1.5, ALU.mult, ALU.add))
                chain(tt(y, y, t, ALU.mult))

            def moments(tag, src, counted=False):
                if not counted:
                    for h in range(NH):
                        last = dve.bn_stats(stats[:, h], src[:, h])
                    chain(last)
                for h in range(NH):
                    last = dve.bn_aggr(mv[:, h], stats[:, h])
                chain(last)
                ts(rs[:, 0], mv[:, :, 1], LN_EPS, None, ALU.add).then_inc(sem("rsqrt_v"), 1)
                dve.wait_ge(sem("rsqrt_y"), RSQRT.index(tag) + 1)
                newton(rs[:, 1], rs[:, 0], rs[:, 2])

            def relu_norm(tag):
                moments(tag, X)
                for h in range(NH):
                    last = ts(Hn[:, h], X[:, h], mv[:, h, 0:1], rs[:, 1, h:h + 1], ALU.subtract, ALU.mult)
                chain(last)
                ts(Hn[:], Hn[:], 0.0, None, ALU.max).then_inc(sem("h_ready"), 1)

            def affine_norm(tag, src, gamma, beta, counted=False):
                moments(tag, src, counted)
                for h in range(NH):
                    last = stt(src[:, h], src[:, h], mv[:, h, 0:1], gamma, ALU.subtract, ALU.mult)
                chain(last)
                for h in range(NH):
                    last = stt(src[:, h], src[:, h], rs[:, 1, h:h + 1], beta, ALU.mult, ALU.add)
                chain(last)
                return tt(X[:], X[:], src, ALU.add)

            def onehot_T(dst, row_, b, g):
                for h in range(NH):
                    last = ts(dst[:, b, h], row_[:, bass.ds(g * GE, GE)], node_col[:, h:h + 1], None, ALU.is_equal)
                return last

            def onehot_E(col, b, g, tiles=range(G)):
                for j in tiles:
                    last = ts(EN[:, b, j], node_row[:], col[:, bass.ds(g * G + j, 1)], None, ALU.is_equal)
                return last

            dve.wait_ge(sem("iotas"), 3)
            chain(cp(node_row16[:], node_row[:]))
            chain(cp(upper16[:], upper[:]))
            chain(ts(upper[:], upper[:], float(NQ), 1.0, ALU.mult, ALU.add))
            chain(ts(ident[:], node_row[:, 0:P], node_col[:, 0:1], None, ALU.is_equal))
            chain(dve.memset(one_col[:], 1.0))
            for a, v in ((ones, 1.0), (BF2, 0.0), (B2S, 0.0), (WEA, 0.0), (EB, 1.0)):
                chain(dve.memset(f(a[:]), v))
            dve.wait_ge(sem("in_idx"), 16)
            chain(cp(src_col[:], idx_raw[:, 0]))
            chain(cp(dst_col[:], idx_raw[:, 1]))

            dve.wait_ge(sem("in_x"), 16)
            relu_norm("n0")
            if layers > 2:
                dve.wait_ge(sem("in_ea3"), 16)
                chain(tt(r_sq, Yv[:], Yv[:], ALU.mult))
                dve.tensor_reduce(r_v, r_sq, AX, ALU.add).then_inc(sem("rsqrt_v"), 1)

            def onehots0(i, k):
                for j in range(G):
                    t = i * G + j
                    tile = bass.ds(t + k * (T // 2), 1)
                    ts(EN16[:, tile].rearrange("p a b -> p (a b)"), node_row16[:], dst_col[:, tile], None, ALU.is_equal)
                    last = ts(SN16[k][:, bass.ds(t, 1)].rearrange("p a b -> p (a b)"), node_row16[:], src_col[:, tile],
                              None, ALU.is_equal)
                last.then_inc(sem("l0_onehots"), 1)
            for k in range(2):
                with dve.Fori(0, NG // 2) as i:
                    onehots0(i, k)
            dve.wait_ge(sem("l0_hW_ps"), 1)
            dve.wait_ge(sem("in_L0_b"), 16)
            for h in range(NH):
                last = tt(hW[:, h], bank(5 + h), V[:, 0], ALU.add)
            chain(last)
            if layers > 2:
                dve.wait_ge(sem("rsqrt_y"), RSQRT.index("r2") + 1)
                newton(r_y, r_v, r_sq.rearrange("p a b -> p (a b)")[:, 0:T])
                chain(ts(r_y, r_y, Y1, None, ALU.mult))
                chain(tt(Yv[:], Yv[:], r_y.unsqueeze(2).to_broadcast([P, T, 3]), ALU.mult))
            dve.wait_ge(sem("l0_count"), 1)
            for h in range(NH):
                chain(ts(adjT[:, h], bank(h)[:, 0:N], 1.0, None, ALU.min))
            for h in range(NH):
                s = slice(h * P, (h + 1) * P)
                last = tt(adjT[:, h, s], adjT[:, h, s], ident[:], ALU.max)
            last.then_inc(sem("l0_adj"), 1)
            dve.wait_ge(sem("l0_deg"), 1)
            cp(rs[:, 0], bank(2)[:, 0:NH]).then_inc(sem("rsqrt_v"), 1)
            dve.wait_ge(sem("rsqrt_y"), RSQRT.index("deg") + 1)
            newton(rs[:, 1], rs[:, 0], rs[:, 2])
            chain(cp(dis, rs[:, 1]))
            for h in range(NH):
                last = ts(hW[:, h], hW[:, h], dis[:, h:h + 1], None, ALU.mult)
            last.then_inc(sem("l0_hW"), 1)
            dve.wait_ge(sem("l0_ps"), 1)
            for h in range(NH):
                last = stt(X[:, h], bank(h), dis[:, h:h + 1], X[:, h], ALU.mult, ALU.add)
            chain(last)
            dve.wait_ge(sem("dve_chain"), chain.n)
            done = ts(rs[:, 3], rs[:, 0], 0.0, None, ALU.mult)
            done.then_inc(sem("x_done"), 1)
            dve.wait_ge(sem("x_done"), 1)
            def filt(g, b):
                dve.wait_ge(sem("l2_ln"), g + 1)
                stt(l2_s[2], l2_s[1], -LOG2, l2_s[0], ALU.add, ALU.add).then_inc(sem("l2_ssp"), 1)
                dve.wait_ge(sem("l2_ssp"), g + 1)
                cp(HT[:, b, 0, 0], l2_s[2]).then_inc(sem("l2_hid_hi"), 1)
                dve.wait_ge(sem("l2_hid_hi"), g + 1)
                tt(HT[:, b, 1, 0], l2_s[2], f(HT[:, b, 0, 0]), ALU.subtract).then_inc(sem("l2_hid"), 1)

            if layers > 1:
                relu_norm("n1")
                dve.wait_ge(sem("rows_cast"), 4)
                for h in range(NH):
                    for c in range(E // 2048):
                        e = slice(c * 2048, (c + 1) * 2048)
                        ts(DT16[h][:, e], dst_row[:, e], node_col[:, h:h + 1], None, ALU.is_equal)
                dve.wait_ge(sem("l1_h_ps"), 1)
                dve.wait_ge(sem("in_l1_vectors"), 48)
                for h in range(NH):
                    split(TAB[:, 0, 0, h], TAB[:, 0, 1, h], bank(5 + h))
                    for w in range(2):
                        chain(tt(l1_t[:, h], bank(5 + h), V[:, 1 + w], ALU.mult))
                        chain(dve.tensor_reduce(nt[:, w, h], l1_t[:, h].rearrange("p (a b) -> p a b", a=HD), AX, ALU.add))
                def split3(dst, src, rest):
                    chain(cp(dst(0), src))
                    chain(tt(rest, src, dst(0), ALU.subtract))
                    chain(cp(dst(1), rest))
                    chain(tt(rest, rest, dst(1), ALU.subtract))
                    return cp(dst(2), rest)
                for w in range(2):
                    chain(split3(lambda k: NT[:, w, :, k], nt[:, w], part[:].rearrange("p (a b) -> p a b", a=NH)))
                split3(lambda k: EMB[:, k], emb[:], part[0:HD, 0:HD]).then_inc(sem("l1_esd"), 1)

                def onehots1(i, b, wait):
                    c = i * 2 + b
                    if wait:
                        dve.wait_ge(sem("l1a_ps"), c - 1)
                    for h in range(NH):
                        ts(ST16[:, b, h], src_row[:, bass.ds(c * CE, CE)], node_col[:, h:h + 1], None, ALU.is_equal)
                    dve.wait_ge(sem(f"in_type{b}"), i * 16 + 16)
                    ts(T8[:, b], typ[:, b], node_col[0:HD, 0:1], None, ALU.is_equal).then_inc(sem("l1a_onehots"), 1)
                onehots1(0, 0, False)
                onehots1(0, 1, False)
                with dve.Fori(1, NCH // 2) as i:
                    onehots1(i, 0, True)
                    onehots1(i, 1, True)

                def gathered(k):
                    return bank(k, 4).rearrange("p (t w) -> p t w", t=T)[:, :, 0:3 * HD].rearrange(
                        "p t (w h) -> p t h w", w=3)
                dve.wait_ge(sem("l1a_ps"), NCH)
                dve.wait_ge(sem("in_ew"), 16)
                chain(dve.tensor_reduce(L[:], gathered(0), AX, ALU.add))
                chain(dve.tensor_reduce(l1_em, gathered(4), AX, ALU.add))
                chain(stt(L[:], L[:], 0.2, L[:], ALU.mult, ALU.max))
                chain(stt(L[:], l1_em, 1.0, L[:], ALU.add, ALU.mult))
                chain(tt(L[:], L[:], ew[:].unsqueeze(2).to_broadcast([P, T, HD]), ALU.mult))

                chain(ts(v_bits, L[:].rearrange("p a b -> p (a b)"), 0.0, None, ALU.max))
                fl = lambda a: a.rearrange("p a b -> p (a b)")
                vi, wi, gi = (a.bitcast(I32) for a in (v_bits, w_bits, g_bits))
                di = [d_bits.bitcast(I32), d_bits2.bitcast(I32)]

                def halves(k):
                    s = 32 - DIGIT * (k + 1)
                    ts(di[k % 2], vi, s, 2 ** DIGIT - 1, ALU.logical_shift_right, ALU.bitwise_and)
                    ts(gi, vi, s + 4, NQ - 1, ALU.logical_shift_right, ALU.bitwise_and)
                    chain(ts(wi, vi, s, NQ - 1, ALU.logical_shift_right, ALU.bitwise_and))
                    cp(fl(g16), gi)
                    chain(ts(wi, wi, 27, 1 << 23, ALU.logical_shift_left, ALU.bitwise_or))

                def columns():
                    for q in range(NB):
                        g = g16[:, q * QT:(q + 1) * QT].unsqueeze(2).to_broadcast([P, QT, NQ, HD])
                        last = tt(masks[q], g, upper16[:].unsqueeze(1).to_broadcast([P, QT, NQ, HD]), ALU.is_equal)
                    chain(last)

                halves(0)
                columns()
                for k in range(NDIG):
                    w = w_bits.rearrange("p (a b) -> p a b", a=T)
                    if k:
                        dve.wait_ge(sem("l1b_match"), k)
                        if k == 1:
                            chain(tt(fl(active), di[0], bank(2), ALU.is_equal))
                        else:
                            chain(tt(g_bits, di[(k - 1) % 2], bank(2), ALU.is_equal))
                            chain(tt(fl(active), fl(active), g_bits, ALU.mult))
                        chain(tt(w16, w, active, ALU.mult))
                    else:
                        chain(cp(w16, w))
                    for q in range(NB):
                        tt(digits[q], masks[q], w16[:, q * QT:(q + 1) * QT].unsqueeze(2).to_broadcast(
                            [P, QT, NQ, HD]), ALU.mult).then_inc(sem("l1b_digits"), 1)
                    dve.wait_ge(sem("l1b_digits"), (k + 1) * NB)
                    if k + 1 < NDIG:
                        halves(k + 1)
                    dve.wait_ge(sem("l1b_sum"), (k + 1) * NB)
                    sums = bank(0, 2).rearrange("p (n w) -> p n w", n=NH)[:, :, 0:NQ * HD]
                    ts(S_a.bitcast(I32), sums.bitcast(I32), 27, None, ALU.logical_shift_right)
                    chain(stt(S_b, sums, 0.0, upper[:].rearrange("p a b -> p (a b)").unsqueeze(1).to_broadcast(
                        [P, NH, NQ * HD]), ALU.is_gt, ALU.mult))
                    chain(tt(S_b, S_b, S_a.bitcast(I32), ALU.add))
                    chain(dve.tensor_reduce(dig[:, k], S_b.rearrange("p n (q h) -> p n h q", q=NQ), AX, ALU.max))
                    chain(ts(dig[:, k], dig[:, k], -1.0, 0.0, ALU.add, ALU.max))
                    if k + 1 < NDIG:
                        cp(dig16[:], dig[:, k]).then_inc(sem("l1b_dig"), 1)
                        columns()
                chain(cp(digI[:], dig[:]))
                for k in range(1, NDIG):
                    chain(stt(digI[:, 0], digI[:, 0], DIGIT, digI[:, k], ALU.logical_shift_left, ALU.bitwise_or))
                split3(lambda k: MX[:, :, k], f(digI[:, 0]),
                       part[:].rearrange("p (a b) -> p a b", a=NH)).then_inc(sem("l1_mx"), 1)

                dve.wait_ge(sem("l1_mg_ps"), 1)
                chain(dve.tensor_reduce(active, gathered(3), AX, ALU.add))
                tt(L[:], L[:], active, ALU.subtract).then_inc(sem("l1_shift"), 1)
                dve.wait_ge(sem("l1_p"), 1)
                split3(lambda k: P24[:, :, k], L[:], active).then_inc(sem("l1_p24"), 1)

                def message(t, b, j, wait):
                    q = j % 2
                    dve.wait_ge(sem("l1_hs_ps"), t + 1)
                    if wait:
                        dve.wait_ge(sem("l1_lo"), t - 1)
                    p = L[:, bass.ds(t, 1)].rearrange("p a b -> p (a b)").unsqueeze(2).to_broadcast([P, HD, C // HD])
                    tt(l1_m[:, q].rearrange("p (a b) -> p a b", a=HD), bank(4 + q).rearrange("p (a b) -> p a b", a=HD),
                       p, ALU.mult).then_inc(sem("l1_msg"), 1)

                def low(t, q):
                    dve.wait_ge(sem("l1_hi"), t + 1)
                    tt(MSG[:, q, 1, 0:C], l1_m[:, q], f(MSG[:, q, 0, 0:C]), ALU.subtract).then_inc(sem("l1_lo"), 1)

                def group(i, b, first, last):
                    g = i * 2 + b
                    begin = first and b == 0
                    for j in range(G):
                        t = g * G + j
                        message(t, b, j, not (begin and j < 2))
                        if not (begin and j == 0):
                            low(t - 1, (j - 1) % 2)
                group(0, 0, True, False)
                group(0, 1, False, False)
                with dve.Fori(1, NG // 2 - 1) as i:
                    group(i, 0, False, False)
                    group(i, 1, False, False)
                group(NG // 2 - 1, 0, False, False)
                group(NG // 2 - 1, 1, False, True)
                low(T - 1, 1)
                if layers > 2:
                    dve.wait_ge(sem("in_l2_filter"), 48)
                    split(WF2[:, 0], WF2[:, 1], LW[:, 0])
                    chain(cp(BF2[0:1], LW[0:1, 1]))
                    chain(cp(BF2[32:33], LW[32:33, 1]))
                    tt(BF2[32:33], LW[32:33, 1], f(BF2[32:33]), ALU.subtract).then_inc(sem("l2_wsplit"), 1)
                    filt(0, 0)
                dve.wait_ge(sem("l1_scat"), T)
                dve.wait_ge(sem("l1_den"), 1)
                for h in range(NH):
                    chain(dve.tensor_reduce(nt[:, 0, h], bank(2 + h)[:, 0:3 * HD].rearrange("p (w h) -> p h w", w=3),
                                            AX, ALU.add))
                    chain(ts(nt[:, 0, h], nt[:, 0, h], 1e-10, None, ALU.add))
                    chain(dve.reciprocal(nt[:, 0, h], nt[:, 0, h]))
                    chain(tt(l1_t[:, h].rearrange("p (a b) -> p a b", a=HD), bank(h).rearrange("p (a b) -> p a b", a=HD),
                             nt[:, 0, h].unsqueeze(2).to_broadcast([P, HD, C // HD]), ALU.mult))
                chain(tt(l1_t, l1_t, Hn[:], ALU.add))
                dve.wait_ge(sem("in_l1_affine"), 32)
                affine_norm("n1o", l1_t, V[:, 1], V[:, 2]).then_inc(sem("x_done"), 1)
                dve.wait_ge(sem("x_done"), 2)
                ts(rs[:, 3], rs[:, 0], 0.0, None, ALU.mult).then_inc(sem("l1_out"), 1)

            if layers > 2:
                relu_norm("n2")
                for h in range(NH):
                    dve.wait_ge(sem("l2_tab"), h + 1)
                    last = split(TAB[:, 0, 0, h], TAB[:, 0, 1, h], l2_tab[h])
                last.then_inc(sem("l2_ready"), 1)

                def message(t, q, wait):
                    m, w = l2_m[:, q], l2_w[:, q]
                    x = bank(4 + q).rearrange("p (a b) -> p a b", a=4)
                    y = Yv[:, bass.ds(t, 1), :].rearrange("p a b -> p (a b)")
                    dve.wait_ge(sem("l2_g_ps"), t + 1)
                    if wait:
                        dve.wait_ge(sem("l2_lo"), t - 1)
                    ts(m[:, 1], x[:, 1], y[:, 0:1], None, ALU.mult).then_inc(sem("l2_dot"), 1)
                    dve.wait_ge(sem("l2_w"), t + 1)
                    tt(m[:, 0:9:8], x[:, 0:1].to_broadcast([P, 2, F]), w[:, 0:3:2], ALU.mult).then_inc(sem("l2_sW"), 1)
                    dve.wait_ge(sem("l2_dot"), t * 3 + 1)
                    stt(m[:, 1], x[:, 2], y[:, 1:2], m[:, 1], ALU.mult, ALU.add).then_inc(sem("l2_dot"), 1)
                    tt(m[:, 5:8], x[:, 1:4], w[:, 3:4].to_broadcast([P, 3, F]), ALU.mult)
                    dve.wait_ge(sem("l2_dot"), t * 3 + 2)
                    stt(m[:, 1], x[:, 3], y[:, 2:3], m[:, 1], ALU.mult, ALU.add).then_inc(sem("l2_dot"), 1)
                    dve.wait_ge(sem("l2_dot"), t * 3 + 3)
                    tt(m[:, 1], m[:, 1], w[:, 1], ALU.mult).then_inc(sem("l2_msg"), 1)

                def low(t, q):
                    dve.wait_ge(sem("l2_hi"), t + 1)
                    tt(MSG[:, q, 1], l2_m[:, q, 0:8].rearrange("p a b -> p (a b)"), f(MSG[:, q, 0]),
                       ALU.subtract).then_inc(sem("l2_lo"), 1)

                def group(i, b, first, last):
                    g = i * 2 + b
                    begin = first and b == 0
                    for j in range(G):
                        t = g * G + j
                        message(t, j % 2, not (begin and j < 2))
                        if not (begin and j == 0):
                            low(t - 1, (j - 1) % 2)
                        if j == 2 and not (last and b == 1):
                            filt(g + 1, 1 - b)
                group(0, 0, True, False)
                group(0, 1, False, False)
                with dve.Fori(1, NG // 2 - 1) as i:
                    group(i, 0, False, False)
                    group(i, 1, False, False)
                group(NG // 2 - 1, 0, False, False)
                group(NG // 2 - 1, 1, False, True)
                low(T - 1, 1)
                dve.wait_ge(sem("l2_scat"), T)
                c = 1.0 / float(np.sqrt(2 * F))
                for h in range(NH):
                    a = bank(2 * h, 2).rearrange("p (a b) -> p a b", a=8)
                    for k0, k1, scale in ((0, 1, c * Y0), (1, 2, c / float(np.sqrt(3.0))), (2, 5, c), (5, 8, c * Y0)):
                        last = ts(l2_agg[:, h, k0:k1], a[:, k0:k1], scale, None, ALU.mult)
                    last.then_inc(sem("l2_agg"), 1)
                dve.wait_ge(sem("l2_aggT_ps"), 1)
                cp(aggT.rearrange("p a b -> p (a b)"), bank(4, 4)).then_inc(sem("l2_aggT"), 1)
                dve.wait_ge(sem("l2_V_ps"), 1)
                for k in range(3):
                    cp(SV[:, 1 + k], bank(5 + k)[:, 0:N])
                dve.wait_ge(sem("l2_S_ln"), 1)
                stt(SV[:, 0], s2[:, 1], -LOG2, s2[:, 0], ALU.add, ALU.add).then_inc(sem("l2_SV"), 1)
                dve.wait_ge(sem("l2_ps"), 1)
                c = 1.0 / float(np.sqrt(F))
                for h in range(NH):
                    a = bank(h).rearrange("p (a b) -> p a b", a=4)
                    stt(X[:, h, 0:F], a[:, 0], c, X[:, h, 0:F], ALU.mult, ALU.add)
                    xv = X[:, h, F:C].rearrange("p (f i) -> p i f", i=3)
                    last = stt(xv, a[:, 1:4], c, xv, ALU.mult, ALU.add)
                last.then_inc(sem("x_done"), 1)
                dve.wait_ge(sem("x_done"), 3)
                ts(rs[:, 3], rs[:, 0], 0.0, None, ALU.mult).then_inc(sem("l2_out"), 1)

            if layers > 3:
                relu_norm("n3")
                dve.wait_ge(sem("in_L3_W2"), 16)
                split(W2S[:, 0], W2S[:, 1], WN[:]).then_inc(sem("l3_w2split"), 1)
                dve.wait_ge(sem("in_l3_edge_weights"), 96)
                raw = u(0, 3, C)
                chain(cp(WEA[:, 0], raw[:, 0]))
                chain(tt(WEA[0:64, 1], raw[0:64, 0], f(WEA[0:64, 0]), ALU.subtract))
                chain(cp(WEA[64:65, 1], raw[64:65, 1]))
                chain(cp(WEA[96:97, 1], raw[96:97, 1]))
                chain(tt(WEA[96:97, 1], raw[96:97, 1], f(WEA[96:97, 1]), ALU.subtract))
                chain(cp(B2S[0:1], raw[0:1, 2]))
                chain(cp(B2S[32:33], raw[32:33, 2]))
                chain(tt(B2S[32:33], raw[32:33, 2], f(B2S[32:33]), ALU.subtract))

                def features(g, b):
                    dve.wait_ge(sem("in_ea"), g * 32 + 32)
                    cp(EA[:, b], ea_raw).then_inc(sem("l3_ea_hi"), 1)
                    dve.wait_ge(sem("l3_ea_hi"), g + 1)
                    tt(EA[64:P, b], ea_raw[64:P], f(EA[64:P, b]), ALU.subtract)
                    cp(EB[0:64, b], ea_raw[0:64]).then_inc(sem("l3_ea"), 1)

                def onehots(g, b, wait):
                    if wait:
                        dve.wait_ge(sem("l3a_ps"), g * G - G)
                    features(g, b)
                    onehot_T(ST, src_row, b, g)

                def onehots_D(g, b):
                    onehot_T(DT, dst_row, b, g).then_inc(sem("l3_onehots"), 1)

                def onehots_E(g, b, wait):
                    if wait:
                        dve.wait_ge(sem("l3_scat"), g * G - G)
                    onehot_E(dst_col, b, g).then_inc(sem("l3_en"), 1)
                onehots(0, 0, False)
                onehots_D(0, 0)
                for w in range(2):
                    dve.wait_ge(sem("l3_tab_ps"), w + 1)
                    for h in range(NH):
                        last = split(TAB[:, w, 0, h], TAB[:, w, 1, h], bank((5, 1)[w] + h))
                last.then_inc(sem("l3_ready"), 1)

                def clamp(kind, n, j):
                    buf = l3_scratch(kind, n, j)
                    dve.wait_ge(sem(f"l3{kind}_exp"), n + 1)
                    ts(buf, buf, CLAMP, None, ALU.min).then_inc(sem(f"l3{kind}_min"), 1)

                def mish(kind, n, j):
                    buf, x = l3_scratch(kind, n, j), l3_bank(kind, n, j)
                    dve.wait_ge(sem(f"l3{kind}_q"), n + 1)
                    stt(buf, buf, 1.0, x, ALU.subtract, ALU.mult, reverse0=True).then_inc(sem(f"l3{kind}_y"), 1)

                def parts(kind, n, j, p):
                    early = isinstance(n, int)
                    if kind == "a":
                        buf, used = l3_scratch(kind, n, j), "l3b_ps"
                        hi, lo = HT[:, p, 0, j], HT[:, p, 1, j]
                        count = None if early and n < 2 * G else n - j - G
                    else:
                        buf, used = l3_scratch(kind, n, j), "l3_scat"
                        s = slice(j % 2 * C, (j % 2 + 1) * C)
                        hi, lo = MSG[:, j // 2, 0, s], MSG[:, j // 2, 1, s]
                        count = None if early and n < G else n + 1 - G
                    if count is not None:
                        dve.wait_ge(sem(used), count)
                    dve.wait_ge(sem(f"l3{kind}_y"), n + 1)
                    cp(hi, buf).then_inc(sem(f"l3{kind}_hi"), 1)
                    dve.wait_ge(sem(f"l3{kind}_hi"), n + 1)
                    tt(lo, buf, f(hi), ALU.subtract).then_inc(sem(f"l3{kind}_lo"), 1)

                fl = lambda a: a.rearrange("p a b -> p (a b)")

                def body(g, p, behind, nxt=True):
                    early = isinstance(g, int) and g < 2
                    for unit in l3_units(g, G, True):
                        old = behind[0] if len(behind) == 2 else None
                        if old:
                            mish(*old[0])
                        clamp(*unit)
                        if old:
                            parts(*old[0], old[1])
                        behind = (behind + ((unit, p),))[-2:]
                        if nxt and unit[0] == "a" and unit[2] == 0:
                            onehots(g + 1, 1 - p, not (isinstance(g, int) and g == 0))
                        if nxt and unit[0] == "a" and unit[2] == 1:
                            onehots_D(g + 1, 1 - p)
                        if unit[0] == "a" and unit[2] == G - 1:
                            onehots_E(g, p, not early)
                    return behind
                before = lambda g, p: ((("a", g * G - 1, G - 1), p), (("b", g * G - 1 - LAG, (-1 - LAG) % G), p))
                behind = body(0, 0, ())
                behind = body(1, 1, behind)
                behind = body(2, 0, behind)
                body(3, 1, behind)
                with dve.Fori(2, NG // 2 - 1) as i:
                    body(i * 2, 0, before(i * 2, 1))
                    body(i * 2 + 1, 1, before(i * 2 + 1, 0))
                body(NG - 2, 0, before(NG - 2, 1))
                body(NG - 1, 1, before(NG - 1, 0), nxt=False)
                (old, p), (prev, _) = before(NG, 1)
                mish(*old)
                parts(*old, p)
                for unit in l3_units(NG, LAG, False):
                    clamp(*unit)
                    mish(*prev)
                    parts(*prev, 0)
                    prev = unit
                mish(*prev)
                parts(*prev, 0)
                dve.wait_ge(sem("l3_scat"), T)
                for h in range(NH):
                    last = cp(agg3[:, h], bank(6 + h))
                last.then_inc(sem("l3_agg"), 1)
                dve.wait_ge(sem("in_l3_vectors"), 64)
                for h in range(NH):
                    tt(Hn[:, h], Hn[:, h], V[:, 1], ALU.add)
                def bias(h):
                    dve.wait_ge(sem("l3_u_ps"), h + 1)
                    tt(UA[0][:, h], bank(4 + h), V[:, 0], ALU.add).then_inc(sem("l3_u_in"), 1)

                def clamp_u(h):
                    dve.wait_ge(sem("l3_u_exp"), h + 1)
                    ts(UA[1][:, h], UA[1][:, h], CLAMP, None, ALU.min).then_inc(sem("l3_u_min"), 1)

                def mish_u(h):
                    dve.wait_ge(sem("l3_u_q"), h + 1)
                    stt(UA[0][:, h], UA[1][:, h], 1.0, UA[0][:, h], ALU.subtract, ALU.mult,
                        reverse0=True).then_inc(sem("l3_u"), 1)

                def turned_u(h):
                    dve.wait_ge(sem("turned_ps"), 2 * TURNS.index("n3u") + h + 1)
                    cp(hT[:, :, h * P:(h + 1) * P], bank(h).rearrange("p (a b) -> p a b", a=KC)).then_inc(sem("turned"), 1)
                bias(0)
                clamp_u(0)
                mish_u(0)
                bias(1)
                clamp_u(1)
                turned_u(0)
                mish_u(1)
                turned_u(1)
                for h in range(NH):
                    dve.wait_ge(sem("l3_out_ps"), h + 1)
                    chain(tt(UA[1][:, h], bank(2 + h), Hn[:, h], ALU.add))
                    last = dve.bn_stats(stats[:, h], UA[1][:, h])
                chain(last)
                affine_norm("n3o", UA[1], V[:, 2], V[:, 3], counted=True).then_inc(sem("x_done"), 1)


_INS = {
    "x": lambda a: a["x"].reshape(NH, P, C).transpose(1, 0, 2),
    "idx_cols": lambda a: np.stack([a["src"].reshape(T, P).T, a["dst"].reshape(T, P).T], 1),
    "idx_rows": lambda a: np.stack([a["src"], a["dst"]]),
    "type_rows": lambda a: np.broadcast_to(a["edge_type_8"], (HD, E)),
    "ew": lambda a: a["edge_weight"].reshape(T, P).T,
    "ea3": lambda a: a["edge_attr_3"].reshape(T, P, 3).transpose(1, 0, 2),
    "ea20T": lambda a: a["edge_attr_20"].T,
    "ea64T": lambda a: a["edge_attr_64"].T,
    "L0_WT": lambda a: a["L0_gnn_W"].T.reshape(KC, P, C).transpose(1, 0, 2),
    "L0_b": lambda a: a["L0_gnn_b"],
    "L1_WT": lambda a: a["L1_gnn_W"].T.reshape(KC, P, C).transpose(1, 0, 2),
    "a_src": lambda a: a["L1_gnn_a_src"].reshape(C),
    "a_dst": lambda a: a["L1_gnn_a_dst"].reshape(C),
    "emb": lambda a: a["L1_gnn_et_emb"],
    "L1_gamma": lambda a: a["L1_gnn_ln_gamma"],
    "L1_beta": lambda a: a["L1_gnn_ln_beta"],
    "Win": lambda a: np.stack([a["L2_gnn_W_in2f_s"], a["L2_gnn_W_in2f_v"]], 1),
    "Wf1": lambda a: a["L2_gnn_Wf1"],
    "bf1": lambda a: a["L2_gnn_bf1"].reshape(F, 1),
    "Wf2": lambda a: a["L2_gnn_Wf2"].reshape(F, 3, F, 2).transpose(0, 1, 3, 2).reshape(F, 6 * F),
    "bf2": lambda a: a["L2_gnn_bf2"].reshape(3, F, 2).transpose(0, 2, 1).reshape(1, 6 * F),
    "W1sv": lambda a: np.stack([a["L2_gnn_W1_s"], a["L2_gnn_W1_v"]]).reshape(2, F, 2, F).transpose(1, 0, 2, 3),
    "W2sv": lambda a: np.stack([a["L2_gnn_W2_s"], a["L2_gnn_W2_v"]], 1),
    "L3_W1ab": lambda a: a["L3_gnn_W1"][0:2 * C].reshape(2 * KC, P, C).transpose(1, 0, 2),
    "W1c": lambda a: a["L3_gnn_W1"][2 * C:],
    "L3_b1": lambda a: a["L3_gnn_b1"].reshape(1, C),
    "L3_W2": lambda a: a["L3_gnn_W2"].reshape(KC, P, C).transpose(1, 0, 2),
    "L3_b2": lambda a: a["L3_gnn_b2"].reshape(1, C),
    "L3_W3": lambda a: a["L3_gnn_W3"].reshape(2 * KC, P, C).transpose(1, 0, 2),
    "L3_b3": lambda a: a["L3_gnn_b3"],
    "L3_W4": lambda a: a["L3_gnn_W4"].reshape(KC, P, C).transpose(1, 0, 2),
    "L3_b4": lambda a: a["L3_gnn_b4"],
    "L3_gamma": lambda a: a["L3_gnn_gamma"],
    "L3_beta": lambda a: a["L3_gnn_beta"],
}


def kernel(**inputs):
    import concourse.bacc as _bacc
    from concourse.bass_utils import run_bass_kernel_spmd as _run

    nc = _bacc.Bacc("TRN2", target_bir_lowering=False, num_devices=1)
    given = {k: np.asarray(v) for k, v in inputs.items()}
    arrays, aps = {}, {}
    for name, layout in _INS.items():
        a = np.ascontiguousarray(layout(given))
        arrays["in_" + name] = a
        aps[name] = nc.dram_tensor("in_" + name, a.shape, mybir.dt.from_np(a.dtype), kind="ExternalInput").ap()
    out = nc.dram_tensor("out_x", (P, NH, C), F32, kind="ExternalOutput").ap()
    gnn_stack(nc, aps, out)
    r = _run(nc, [arrays], core_ids=[0])
    return np.ascontiguousarray(r.results[0]["out_x"].transpose(1, 0, 2).reshape(N, C))
```
